# Optimizing a Trainium2 kernel written in Bass

```python
import numpy as np
import jax
import jax.numpy as jnp

def _softmax(x, axis=-1):
    return jax.nn.softmax(x, axis=axis)

def _gelu(x):
    return jax.nn.gelu(x, approximate=True)

def _silu(x):
    return jax.nn.silu(x)

def _sigmoid(x):
    return jax.nn.sigmoid(x)

def _layernorm(x, axis=-1, eps=1e-05):
    m = jnp.mean(x, axis=axis, keepdims=True)
    v = jnp.var(x, axis=axis, keepdims=True)
    return (x - m) / jnp.sqrt(v + eps)

def _scatter_add(tgt, idx, src, axis=0):
    return tgt.at[idx].add(src)

def _segment_sum(src, seg, n):
    return jax.ops.segment_sum(src, seg, n)
kernel_name = 'mk_flamingo_gated_d2_seqx_r8_e03677'

def setup_inputs(seed: int=0):
    np.random.seed(seed)
    _w = jnp.asarray

    def _rec_inputs():
        import jax
        import jax.numpy as jnp
        _rk = jax.random.key(seed)
        x = 0.002226 + 0.9996 * jax.random.normal(jax.random.fold_in(_rk, 1), (64, 64, 128), jnp.float32)
        _lenS = 64 - jax.random.randint(jax.random.fold_in(_rk, 7), (64,), 0, max(1, 64 // 4) + 1, jnp.int32)
        _lenS2 = 64 - jax.random.randint(jax.random.fold_in(_rk, 8), (64,), 0, max(1, 64 // 4) + 1, jnp.int32)
        _ctx_1024P = jax.random.normal(jax.random.fold_in(_rk, 11), (64, 16, 128), jnp.float32)
        _ctx_1024c = jax.random.dirichlet(jax.random.fold_in(_rk, 511), 0.3 * jnp.ones((16,), jnp.float32), (64, 64))
        _ctx_1024t = jnp.einsum('bsk,bkd->bsd', _ctx_1024c, _ctx_1024P)
        _ctx_1024t = _ctx_1024t * jax.lax.rsqrt(jnp.mean(jnp.square(_ctx_1024t)) + 1e-12) * 0.953939
        ctx_1024 = -0.000125008 + 0.999885 * (_ctx_1024t + 0.3 * jax.random.normal(jax.random.fold_in(_rk, 611), (64, 64, 128), jnp.float32))
        _validS = jnp.arange(64)[None, :] < _lenS[:, None]
        _validS2 = jnp.arange(64)[None, :] < _lenS2[:, None]
        _causal = jnp.tril(jnp.ones((64, 64), dtype=bool))
        mask_BxS2_bk0 = jnp.logical_not(jnp.broadcast_to(_validS2[:, :], (64, 64)))
        mask_SxS2_ff1 = jnp.where(jnp.ones((64, 64), dtype=bool), 1.0, 0.0).astype(jnp.float32)
        _g = jax.random.normal(jax.random.fold_in(_rk, 9001), (2, 2), jnp.float32)
        _g = jnp.sign(_g) * jnp.maximum(jnp.abs(_g), 1.0) + (_g == 0) * 1.0
        g_xattn = _g[0]
        g_ffn = _g[1]
        return (x, ctx_1024, mask_BxS2_bk0, mask_SxS2_ff1, g_xattn, g_ffn)
    x, ctx_1024, mask_BxS2_bk0, mask_SxS2_ff1, g_xattn, g_ffn = _rec_inputs()

    def _L0_xattn_setup():
        import jax, jax.numpy as jnp
        import numpy as np
        DIM = 128
        HEADS = 16
        DIM_HEAD = 64
        INNER = HEADS * DIM_HEAD
        EPS = 1e-05

        def layernorm(t, g, b):
            mu = jnp.mean(t, axis=-1, keepdims=True)
            var = jnp.var(t, axis=-1, keepdims=True)
            return (t - mu) * jax.lax.rsqrt(var + EPS) * g + b
        key = jax.random.key(seed)
        ks = jax.random.split(key, 8)
        b, n, m = (8, 512, 64)
        x = jax.random.normal(ks[0], (b, n, DIM), dtype=jnp.float32)
        latents = jax.random.normal(ks[1], (b, m, DIM), dtype=jnp.float32)
        mask = jax.random.randint(ks[2], (b, n), 0, 2).astype(bool)
        s = 0.02
        Wq = jax.random.normal(ks[3], (DIM, INNER), dtype=jnp.float32) * s
        Wkv = jax.random.normal(ks[4], (DIM, 2 * INNER), dtype=jnp.float32) * s
        Wout = jax.random.normal(ks[5], (INNER, DIM), dtype=jnp.float32) * s
        ln_x_g = jnp.ones((DIM,), jnp.float32)
        ln_x_b = jnp.zeros((DIM,), jnp.float32)
        ln_l_g = jnp.ones((DIM,), jnp.float32)
        ln_l_b = jnp.zeros((DIM,), jnp.float32)
        ln_o_g = jnp.ones((DIM,), jnp.float32)
        ln_o_b = jnp.zeros((DIM,), jnp.float32)
        return {'x': x, 'latents': latents, 'mask': mask, 'ln_x_g': ln_x_g, 'ln_x_b': ln_x_b, 'ln_l_g': ln_l_g, 'ln_l_b': ln_l_b, 'Wq': Wq, 'Wkv': Wkv, 'Wout': Wout, 'ln_o_g': ln_o_g, 'ln_o_b': ln_o_b}
    _L0_xattn_all = _L0_xattn_setup()
    _L0_xattn_in = {k: v for k, v in _L0_xattn_all.items() if k in ('ln_x_g', 'ln_x_b', 'ln_l_g', 'ln_l_b', 'Wq', 'Wkv', 'Wout', 'ln_o_g', 'ln_o_b')}
    del _L0_xattn_all

    def _L0_ffn_setup():
        import jax, jax.numpy as jnp
        import numpy as np
        N_HEADS = 4
        key = jax.random.key(seed)
        k1, k2, k3, k4 = jax.random.split(key, 4)
        dmodel, n_experts, expert_size = (128, 64, 128)
        B, S = (4, 256)
        x = jax.random.normal(k1, (B, S, dmodel), dtype=jnp.float32)
        expert_sel = jax.random.normal(k2, (n_experts, dmodel), dtype=jnp.float32) * dmodel ** (-0.5)
        keys = jax.random.normal(k3, (n_experts, dmodel, expert_size), dtype=jnp.float32) * dmodel ** (-0.5)
        values = jax.random.normal(k4, (n_experts, expert_size, dmodel), dtype=jnp.float32) * (n_experts * expert_size) ** (-0.5)
        return {'x': x, 'expert_sel': expert_sel, 'keys': keys, 'values': values}
    _L0_ffn_all = _L0_ffn_setup()
    _L0_ffn_in = {k: v for k, v in _L0_ffn_all.items() if k in ('expert_sel', 'keys', 'values')}
    del _L0_ffn_all

    def _L1_xattn_setup():
        import jax, jax.numpy as jnp
        import numpy as np
        B, N, M, D_MODEL, H, DH, D_OUT = (2, 256, 256, 128, 16, 64, 128)
        key0 = jax.random.key(seed)
        ks = jax.random.split(key0, 12)
        s_in = 1.0 / np.sqrt(D_MODEL)
        s_pr = 1.0 / np.sqrt(DH * H)
        return {'query': jax.random.normal(ks[0], (B, N, D_MODEL), jnp.float32), 'key': jax.random.normal(ks[1], (B, M, D_MODEL), jnp.float32), 'value': jax.random.normal(ks[2], (B, M, D_MODEL), jnp.float32), 'mask': jnp.ones((N, M), jnp.float32), 'Wq': jax.random.normal(ks[3], (H, D_MODEL, DH), jnp.float32) * s_in, 'bq': jnp.zeros((H, DH), jnp.float32), 'Wk': jax.random.normal(ks[4], (H, D_MODEL, DH), jnp.float32) * s_in, 'bk': jnp.zeros((H, DH), jnp.float32), 'Wv': jax.random.normal(ks[5], (H, D_MODEL, DH), jnp.float32) * s_in, 'bv': jnp.zeros((H, DH), jnp.float32), 'Wo': jax.random.normal(ks[6], (DH * H, D_OUT), jnp.float32) * s_pr, 'bo': jnp.zeros((D_OUT,), jnp.float32)}
    _L1_xattn_all = _L1_xattn_setup()
    _L1_xattn_in = {k: v for k, v in _L1_xattn_all.items() if k in ('Wq', 'bq', 'Wk', 'bk', 'Wv', 'bv', 'Wo', 'bo')}
    del _L1_xattn_all

    def _L1_ffn_setup():
        import jax, jax.numpy as jnp
        import numpy as np
        N_EXPERTS = 32
        TOP_K = 8
        N_GROUP = 4
        TOPK_GROUP = 2
        ROUTED_SCALING = 2.5

        def _gate(x, gate_w, gate_bias):
            T, E = (x.shape[0], gate_w.shape[0])
            logits = jnp.einsum('th,eh->te', x, gate_w)
            scores = jax.nn.sigmoid(logits)
            scores_choice = scores + gate_bias[None, :]
            grp = scores_choice.reshape(T, N_GROUP, E // N_GROUP)
            top2, _ = jax.lax.top_k(grp, 2)
            group_scores = top2.sum(-1)
            _, grp_idx = jax.lax.top_k(group_scores, TOPK_GROUP)
            group_mask = jax.nn.one_hot(grp_idx, N_GROUP, dtype=scores.dtype).sum(1)
            expert_mask = jnp.repeat(group_mask, E // N_GROUP, axis=1)
            masked = jnp.where(expert_mask > 0, scores_choice, 0.0)
            _, topk_idx = jax.lax.top_k(masked, TOP_K)
            topk_w = jnp.take_along_axis(scores, topk_idx, axis=1)
            topk_w = topk_w / (topk_w.sum(-1, keepdims=True) + 1e-20)
            topk_w = topk_w * ROUTED_SCALING
            return (topk_idx, topk_w)

        def _mlp(x, wg, wu, wd):
            return jnp.einsum('...i,hi->...h', jax.nn.silu(jnp.einsum('...h,ih->...i', x, wg)) * jnp.einsum('...h,ih->...i', x, wu), wd)
        key = jax.random.key(seed)
        ks = jax.random.split(key, 9)
        B, S, H, I = (2, 64, 128, 64)
        w = 0.02
        return {'hidden_states': jax.random.normal(ks[0], (B, S, H), jnp.float32), 'gate_w': jax.random.normal(ks[1], (N_EXPERTS, H), jnp.float32) * w, 'gate_bias': jax.random.normal(ks[2], (N_EXPERTS,), jnp.float32) * w, 'expert_gate': jax.random.normal(ks[3], (N_EXPERTS, I, H), jnp.float32) * w, 'expert_up': jax.random.normal(ks[4], (N_EXPERTS, I, H), jnp.float32) * w, 'expert_down': jax.random.normal(ks[5], (N_EXPERTS, H, I), jnp.float32) * w, 'shared_gate': jax.random.normal(ks[6], (2 * I, H), jnp.float32) * w, 'shared_up': jax.random.normal(ks[7], (2 * I, H), jnp.float32) * w, 'shared_down': jax.random.normal(ks[8], (H, 2 * I), jnp.float32) * w}
    _L1_ffn_all = _L1_ffn_setup()
    _L1_ffn_in = {k: v for k, v in _L1_ffn_all.items() if k in ('gate_w', 'gate_bias', 'expert_gate', 'expert_up', 'expert_down', 'shared_gate', 'shared_up', 'shared_down')}
    del _L1_ffn_all
    return {'x': x, 'ctx_1024': ctx_1024, 'mask_BxS2_bk0': mask_BxS2_bk0, 'mask_SxS2_ff1': mask_SxS2_ff1, 'g_xattn': g_xattn, 'g_ffn': g_ffn, 'L0_xattn_ln_x_g': _L0_xattn_in['ln_x_g'], 'L0_xattn_ln_x_b': _L0_xattn_in['ln_x_b'], 'L0_xattn_ln_l_g': _L0_xattn_in['ln_l_g'], 'L0_xattn_ln_l_b': _L0_xattn_in['ln_l_b'], 'L0_xattn_Wq': _L0_xattn_in['Wq'], 'L0_xattn_Wkv': _L0_xattn_in['Wkv'], 'L0_xattn_Wout': _L0_xattn_in['Wout'], 'L0_xattn_ln_o_g': _L0_xattn_in['ln_o_g'], 'L0_xattn_ln_o_b': _L0_xattn_in['ln_o_b'], 'L0_ffn_expert_sel': _L0_ffn_in['expert_sel'], 'L0_ffn_keys': _L0_ffn_in['keys'], 'L0_ffn_values': _L0_ffn_in['values'], 'L1_xattn_Wq': _L1_xattn_in['Wq'], 'L1_xattn_bq': _L1_xattn_in['bq'], 'L1_xattn_Wk': _L1_xattn_in['Wk'], 'L1_xattn_bk': _L1_xattn_in['bk'], 'L1_xattn_Wv': _L1_xattn_in['Wv'], 'L1_xattn_bv': _L1_xattn_in['bv'], 'L1_xattn_Wo': _L1_xattn_in['Wo'], 'L1_xattn_bo': _L1_xattn_in['bo'], 'L1_ffn_gate_w': _L1_ffn_in['gate_w'], 'L1_ffn_gate_bias': _L1_ffn_in['gate_bias'], 'L1_ffn_expert_gate': _L1_ffn_in['expert_gate'], 'L1_ffn_expert_up': _L1_ffn_in['expert_up'], 'L1_ffn_expert_down': _L1_ffn_in['expert_down'], 'L1_ffn_shared_gate': _L1_ffn_in['shared_gate'], 'L1_ffn_shared_up': _L1_ffn_in['shared_up'], 'L1_ffn_shared_down': _L1_ffn_in['shared_down']}

def reference(x, ctx_1024, mask_BxS2_bk0, mask_SxS2_ff1, g_xattn, g_ffn, L0_xattn_ln_x_g, L0_xattn_ln_x_b, L0_xattn_ln_l_g, L0_xattn_ln_l_b, L0_xattn_Wq, L0_xattn_Wkv, L0_xattn_Wout, L0_xattn_ln_o_g, L0_xattn_ln_o_b, L0_ffn_expert_sel, L0_ffn_keys, L0_ffn_values, L1_xattn_Wq, L1_xattn_bq, L1_xattn_Wk, L1_xattn_bk, L1_xattn_Wv, L1_xattn_bv, L1_xattn_Wo, L1_xattn_bo, L1_ffn_gate_w, L1_ffn_gate_bias, L1_ffn_expert_gate, L1_ffn_expert_up, L1_ffn_expert_down, L1_ffn_shared_gate, L1_ffn_shared_up, L1_ffn_shared_down):
    import jax
    import jax.numpy as jnp

    def _L0_xattn_ref(x, latents, mask, ln_x_g, ln_x_b, ln_l_g, ln_l_b, Wq, Wkv, Wout, ln_o_g, ln_o_b):
        import jax, jax.numpy as jnp
        import numpy as np
        DIM = 128
        HEADS = 16
        DIM_HEAD = 64
        INNER = HEADS * DIM_HEAD
        EPS = 1e-05

        def layernorm(t, g, b):
            mu = jnp.mean(t, axis=-1, keepdims=True)
            var = jnp.var(t, axis=-1, keepdims=True)
            return (t - mu) * jax.lax.rsqrt(var + EPS) * g + b
        b, n, _ = x.shape
        m = latents.shape[1]
        scale = DIM_HEAD ** (-0.5)
        xn = layernorm(x, ln_x_g, ln_x_b)
        ln = layernorm(latents, ln_l_g, ln_l_b)
        q = ln @ Wq
        kv_input = jnp.concatenate((xn, ln), axis=1)
        kv = kv_input @ Wkv
        k, v = jnp.split(kv, 2, axis=-1)

        def heads(t):
            return t.reshape(t.shape[0], t.shape[1], HEADS, DIM_HEAD).transpose(0, 2, 1, 3)
        q, k, v = (heads(q) * scale, heads(k), heads(v))
        sim = jnp.einsum('bhid,bhjd->bhij', q, k)
        mask_full = jnp.concatenate((mask, jnp.ones((b, m), dtype=bool)), axis=1)
        max_neg = -jnp.finfo(sim.dtype).max
        sim = jnp.where(mask_full[:, None, None, :], sim, max_neg)
        attn = jax.nn.softmax(sim.astype(jnp.float32), axis=-1).astype(sim.dtype)
        out = jnp.einsum('bhij,bhjd->bhid', attn, v)
        out = out.transpose(0, 2, 1, 3).reshape(b, m, INNER)
        out = out @ Wout
        return layernorm(out, ln_o_g, ln_o_b)

    def _L0_ffn_ref(x, expert_sel, keys, values):
        import jax, jax.numpy as jnp
        import numpy as np
        N_HEADS = 4
        B, S, d = x.shape
        n_experts = keys.shape[0]
        xf = x.reshape(-1, d)
        N = xf.shape[0]
        logits = xf @ expert_sel.T
        sel = jax.nn.sigmoid(logits)
        sel_val, sel_idx = jax.lax.top_k(sel, N_HEADS)
        gates = jnp.zeros((N, n_experts), dtype=x.dtype)
        gates = gates.at[jnp.arange(N)[:, None], sel_idx].set(sel_val)
        h = jnp.einsum('nd,kde->nke', xf, keys)
        scores = jax.nn.relu(h) * gates[:, :, None]
        out = jnp.einsum('nke,kev->nv', scores, values)
        return out.reshape(B, S, -1)

    def _L1_xattn_ref(query, key, value, mask, Wq, bq, Wk, bk, Wv, bv, Wo, bo):
        import jax, jax.numpy as jnp
        import numpy as np
        B, N, M, D_MODEL, H, DH, D_OUT = (2, 256, 256, 128, 16, 64, 128)
        q = jnp.einsum('bnd,hde->bhne', query, Wq) + bq[None, :, None, :]
        k = jnp.einsum('bmd,hde->bhme', key, Wk) + bk[None, :, None, :]
        v = jnp.einsum('bmd,hde->bhme', value, Wv) + bv[None, :, None, :]
        q = q / jnp.sqrt(jnp.asarray(q.shape[-1], q.dtype))
        logits = jnp.einsum('bhne,bhme->bhnm', q, k)
        logits = logits + -10000000000.0 * (1.0 - mask)
        attn = jax.nn.softmax(logits, axis=-1)
        ctx = jnp.einsum('bhnm,bhme->bhne', attn, v)
        ctx = jnp.transpose(ctx, (0, 2, 3, 1)).reshape(ctx.shape[0], ctx.shape[2], -1)
        return jnp.dot(ctx, Wo) + bo

    def _L1_ffn_ref(hidden_states, gate_w, gate_bias, expert_gate, expert_up, expert_down, shared_gate, shared_up, shared_down):
        import jax, jax.numpy as jnp
        import numpy as np
        N_EXPERTS = 32
        TOP_K = 8
        N_GROUP = 4
        TOPK_GROUP = 2
        ROUTED_SCALING = 2.5

        def _gate(x, gate_w, gate_bias):
            T, E = (x.shape[0], gate_w.shape[0])
            logits = jnp.einsum('th,eh->te', x, gate_w)
            scores = jax.nn.sigmoid(logits)
            scores_choice = scores + gate_bias[None, :]
            grp = scores_choice.reshape(T, N_GROUP, E // N_GROUP)
            top2, _ = jax.lax.top_k(grp, 2)
            group_scores = top2.sum(-1)
            _, grp_idx = jax.lax.top_k(group_scores, TOPK_GROUP)
            group_mask = jax.nn.one_hot(grp_idx, N_GROUP, dtype=scores.dtype).sum(1)
            expert_mask = jnp.repeat(group_mask, E // N_GROUP, axis=1)
            masked = jnp.where(expert_mask > 0, scores_choice, 0.0)
            _, topk_idx = jax.lax.top_k(masked, TOP_K)
            topk_w = jnp.take_along_axis(scores, topk_idx, axis=1)
            topk_w = topk_w / (topk_w.sum(-1, keepdims=True) + 1e-20)
            topk_w = topk_w * ROUTED_SCALING
            return (topk_idx, topk_w)

        def _mlp(x, wg, wu, wd):
            return jnp.einsum('...i,hi->...h', jax.nn.silu(jnp.einsum('...h,ih->...i', x, wg)) * jnp.einsum('...h,ih->...i', x, wu), wd)
        orig_shape = hidden_states.shape
        H = orig_shape[-1]
        residuals = hidden_states
        x = hidden_states.reshape(-1, H)
        topk_idx, topk_w = _gate(x, gate_w, gate_bias)
        g = jnp.einsum('th,eih->eti', x, expert_gate)
        u = jnp.einsum('th,eih->eti', x, expert_up)
        outs = jnp.einsum('eti,ehi->eth', jax.nn.silu(g) * u, expert_down)
        outs_t = jnp.transpose(outs, (1, 0, 2))
        gathered = jnp.take_along_axis(outs_t, topk_idx[:, :, None], axis=1)
        final = (gathered * topk_w[:, :, None]).sum(1)
        shared = _mlp(residuals, shared_gate, shared_up, shared_down)
        return final.reshape(orig_shape) + shared
    x = x + jnp.tanh(g_xattn[0]) * _L0_xattn_ref(ctx_1024, _layernorm(x, axis=-1), mask_BxS2_bk0, L0_xattn_ln_x_g, L0_xattn_ln_x_b, L0_xattn_ln_l_g, L0_xattn_ln_l_b, L0_xattn_Wq, L0_xattn_Wkv, L0_xattn_Wout, L0_xattn_ln_o_g, L0_xattn_ln_o_b)
    x = x + jnp.tanh(g_ffn[0]) * _L0_ffn_ref(_layernorm(x, axis=-1), L0_ffn_expert_sel, L0_ffn_keys, L0_ffn_values)
    x = x + jnp.tanh(g_xattn[1]) * _L1_xattn_ref(_layernorm(x, axis=-1), ctx_1024, ctx_1024, mask_SxS2_ff1, L1_xattn_Wq, L1_xattn_bq, L1_xattn_Wk, L1_xattn_bk, L1_xattn_Wv, L1_xattn_bv, L1_xattn_Wo, L1_xattn_bo)
    x = x + jnp.tanh(g_ffn[1]) * _L1_ffn_ref(_layernorm(x, axis=-1), L1_ffn_gate_w, L1_ffn_gate_bias, L1_ffn_expert_gate, L1_ffn_expert_up, L1_ffn_expert_down, L1_ffn_shared_gate, L1_ffn_shared_up, L1_ffn_shared_down)
    return x

_drawn_inputs = setup_inputs


def setup_inputs(seed=0):
    import zlib

    import numpy as np

    out = dict(_drawn_inputs(seed))
    spreads = {'mask_SxS2_ff1': (1.0, 0.2),
     'g_ffn': (-1.0, 0.6),
     'L0_xattn_ln_x_g': (1.0, 0.2),
     'L0_xattn_ln_x_b': (0.0, 0.1),
     'L0_xattn_ln_l_g': (1.0, 0.2),
     'L0_xattn_ln_l_b': (0.0, 0.1),
     'L0_xattn_ln_o_g': (1.0, 0.2),
     'L0_xattn_ln_o_b': (0.0, 0.1),
     'L1_xattn_bq': (0.0, 0.1),
     'L1_xattn_bk': (0.0, 0.1),
     'L1_xattn_bv': (0.0, 0.1),
     'L1_xattn_bo': (0.0, 0.1)}
    factors = {'L1_ffn_gate_w': 8.0,
     'L1_ffn_gate_bias': 8.0,
     'L1_ffn_expert_gate': 8.0,
     'L1_ffn_expert_up': 8.0,
     'L1_ffn_expert_down': 8.0,
     'L1_ffn_shared_gate': 8.0,
     'L1_ffn_shared_up': 8.0,
     'L1_ffn_shared_down': 8.0}
    for name, (base, spread) in spreads.items():
        noise = np.random.default_rng([zlib.crc32(name.encode()), seed]).standard_normal(out[name].shape)
        drawn = base * np.exp(spread * noise) if base else spread * noise
        out[name] = jnp.asarray(drawn.astype(out[name].dtype))
    for name, factor in factors.items():
        out[name] = (out[name] * factor).astype(out[name].dtype)
    return out
```

```python
from contextlib import ExitStack

import concourse.bass as bass
from concourse import mybir

ALU = mybir.AluOpType
ACT = mybir.ActivationFunctionType
F32 = mybir.dt.float32
BF16 = mybir.dt.bfloat16
AX_X = mybir.AxisListType.X

P = 128
B, S, D = 64, 64, 128
TILES = B * S // P
H, DH = 16, 64
INNER = H * DH
HALF_HEADS = H // 2
CH = INNER // P
E0, TOP0 = 64, 4
E1, I1 = 32, 64
GROUPS1, GSIZE1 = 4, 8
ROUTED_SCALING = 2.5
LN_EPS = 1e-5
MASK1 = -1e10
GATE, UP, DOWN, SHARED, SHARED_DOWN, ROUTER1, ROUTER0 = 0, 16, 32, 48, 50, 51, 52
BQ, BK, BV = 53, 54, 55
BLOCKS = 56
MASKED = -1e30
REGION = B * S + P
SLOTS0 = 192
BATCH = 4
BATCHES = SLOTS0 // BATCH
BANK = 512
SLOTS = 4


def head(hh):
    return 2 * (hh % HALF_HEADS) + hh // HALF_HEADS


class Steps:

    def __init__(self, sem, names, first=-1):
        self.sem, self.names, self.first = sem, names, first

    def at(self, name, it):
        if isinstance(it, int) and it < self.first:
            return 0
        return (it - self.first) * len(self.names) + self.names.index(name) + 1

    def skip(self, eng, name, it):
        if self.at(name, it) > 1:
            eng.wait_ge(self.sem, self.at(name, it) - 1)
        eng.sem_inc(self.sem, 1)


class Mem:

    def __init__(self, nc, ctx):
        self.nc, self.ctx = nc, ctx

    def sb(self, name, shape, dt=F32):
        return self.ctx.enter_context(self.nc.sbuf_tensor(name, shape, dt))

    def psum(self, name, shape, dt=F32):
        return self.ctx.enter_context(self.nc.psum_tensor(name, shape, dt))

    def sem(self, name):
        return self.ctx.enter_context(self.nc.semaphore(name))


def run_tiles(eng_loop, body, n=TILES, apart=1):
    body(-1, False, True)
    with eng_loop.Fori(0, n - apart) as it:
        body(it, True, True)
    for it in range(n - apart, n):
        body(it, True, it + 1 < n)


def setup(nc, m, w):
    g = {}
    g["x"] = m.sb("x_sb", [P, TILES, D])
    g["ctx"] = m.sb("ctx_sb", [P, TILES, D])
    g["ident"] = m.sb("ident", [P, P])
    g["neg_half"] = m.sb("neg_half", [P, 2])
    g["batch_sel"] = m.sb("batch_sel", [P, P], BF16)
    g["mask0"] = m.sb("mask0", [P, TILES, P], BF16)
    g["eps"] = m.sb("eps", [P, 2])
    g["tri"] = m.sb("tri", [P, GROUPS1, GROUPS1])
    g["before"] = m.sb("before", [P, P], BF16)
    g["ones"] = m.sb("ones", [P, P], BF16)
    g["zeros"] = m.sb("zeros", [P, D])
    g["expert_id"] = m.sb("expert_id", [P, E0])
    g["slot_id"] = m.sb("slot_id", [P, 2])
    g["starts"] = m.sb("starts", [P, TILES])
    g["base"] = m.sb("base", [P, E0])
    g["chosen"] = m.sb("chosen", [P, TILES, TOP0])
    g["position"] = m.sb("position", [P, TILES, TOP0])
    g["gates"] = m.sb("gates", [P, TILES, TOP0])
    g["first_row"] = m.sb("first_row", [P, E0])
    ids = m.sb("ids", [P, E0 + 2 + TILES], mybir.dt.int32)
    g["xs"] = nc.dram_tensor("expert_tokens", (E0 * REGION, D), F32).ap()
    g["ys"] = nc.dram_tensor("expert_outputs", (SLOTS0 * P, D), F32).ap()
    s_ids = m.sem("ids_made")
    g["tanh_g"] = m.sb("tanh_g", [P, 4])
    g["cols"] = m.sb("cols", [P, 4])
    g["wq0"] = m.sb("wq0", [P, INNER])
    g["wkv0"] = m.sb("wkv0", [P, 2 * INNER])
    g["wout0"] = m.sb("wout0", [P, CH, D])
    g["gain_o"] = m.sb("gain_o", [P, D])
    g["bias_o"] = m.sb("bias_o", [P, D])
    ident_one = m.sb("ident_one", [P, P])
    sel_low = m.sb("sel_low", [P, P])
    mask_raw = m.sb("mask_raw", [2, TILES, S], mybir.dt.uint8)
    g["wq1"] = m.sb("wq1", [P, H, DH])
    g["wk1"] = m.sb("wk1", [P, H, DH])
    g["wv1"] = m.sb("wv1", [P, H, DH])
    g["wo1"] = m.sb("wo1", [P, CH, D])
    g["out_bias1"] = m.sb("out_bias1", [P, D])
    g["mask1"] = m.sb("mask1", [P, S])
    g["gate_bias"] = m.sb("gate_bias", [P, E1])
    g["wT"] = m.sb("wT", [P, BLOCKS, P])
    g["loads"] = m.sem("loads")
    g["loads1"] = m.sem("loads1")
    ready = m.sem("ready")
    s_pool = m.sem("setup_pool")
    s_dve = m.sem("setup_dve")
    x_v = w["x"].rearrange("(t b) s d -> (b s) t d", b=2)
    ctx_v = w["ctx_1024"].rearrange("(t b) s d -> (b s) t d", b=2)
    out_v = w["L0_xattn_Wout"].rearrange("(k c p e) o -> p c e k o", c=2, p=2, e=DH)
    n_small = [0]
    with nc.Block() as block:
        @block.sync
        def _(sp):
            def load(dst, src):
                sp.dma_start(dst, src).then_inc(g["loads"], 16)
                n_small[0] += 16
            load(mask_raw[:, :, :], w["mask_BxS2_bk0"].rearrange("(t b) j -> b t j", b=2))
            load(g["tanh_g"][:, 0:2], w["g_xattn"].partition_broadcast(P))
            load(g["tanh_g"][:, 2:4], w["g_ffn"].partition_broadcast(P))
            for n, name in enumerate(("ln_x_g", "ln_x_b", "ln_l_g", "ln_l_b")):
                load(g["cols"][:, n:n + 1], w["L0_xattn_" + name].unsqueeze(1))
            load(g["gain_o"][:, :], w["L0_xattn_ln_o_g"].partition_broadcast(P))
            load(g["bias_o"][:, :], w["L0_xattn_ln_o_b"].partition_broadcast(P))
            load(g["ctx"][:, :, :], ctx_v)
            load(g["x"][:, :, :], x_v)
            load(g["wq0"][:, :], w["L0_xattn_Wq"])
            load(g["wkv0"][:, :], w["L0_xattn_Wkv"])
            for c in range(2):
                for p in range(2):
                    load(g["wout0"][DH * c:DH * c + DH, 4 * p:4 * p + 4, :], out_v[p, c])
            n = 0
            wo_v = w["L1_xattn_Wo"].rearrange("(e k c p) o -> p c e k o", c=2, p=2, k=4)
            late = [(g["wq1"][:, :, :], w["L1_xattn_Wq"].rearrange("h d e -> d h e")),
                    (g["wk1"][:, :, :], w["L1_xattn_Wk"].rearrange("h d e -> d h e")),
                    (g["out_bias1"][:, :], w["L1_xattn_bo"].partition_broadcast(P)),
                    (g["gate_bias"][:, :], w["L1_ffn_gate_bias"].partition_broadcast(P))]
            for p in range(2):
                late.append((g["mask1"][S * p:S * p + S, :], w["mask_SxS2_ff1"]))
                late.append((g["wv1"][:, 8 * p:8 * p + 8, :],
                             w["L1_xattn_Wv"].rearrange("(c p) d e -> p d c e", p=2)[p]))
                for c in range(2):
                    late.append((g["wo1"][DH * c:DH * c + DH, 4 * p:4 * p + 4, :], wo_v[p, c]))
            for dst, src in late:
                sp.dma_start(dst, src).then_inc(g["loads1"], 16)
            g["n_late"] = 16 * len(late)

        @block.gpsimd
        def _(pool):
            pool.memset(g["neg_half"][:, :], -0.5)
            pool.memset(g["eps"][:, :], LN_EPS)
            pool.memset(ident_one[:, :], 1.0).then_inc(s_pool, 1)
            pool.wait_ge(s_pool, 1)
            pool.affine_select(out=g["ident"][:, :], in_=ident_one[:, :], compare_op=ALU.is_equal, fill=0.0,
                               base=0, pattern=[[-1, P]], channel_multiplier=1).then_inc(s_pool, 1)
            pool.affine_select(out=g["before"][:, :], in_=ident_one[:, :], compare_op=ALU.is_gt, fill=0.0,
                               base=0, pattern=[[1, P]], channel_multiplier=-1)
            pool.iota(ids[:, 0:E0], [[1, E0]], 0, 0)
            pool.iota(ids[:, E0:E0 + 2], [[P, 2]], 0, 1)
            pool.iota(ids[:, E0 + 2:], [[P, TILES]], 0, 0).then_inc(s_ids, 1)
            pool.affine_select(out=g["tri"][:, :, :], in_=ident_one[:, 0:16].rearrange("p (a b) -> p a b", a=4),
                               compare_op=ALU.is_gt, fill=0.0, base=0, pattern=[[1, 4], [-1, 4]],
                               channel_multiplier=0)
            pool.affine_select(out=sel_low[:, :], in_=ident_one[:, :], compare_op=ALU.is_ge, fill=0.0, base=0,
                               pattern=[[1, P]], channel_multiplier=-S).then_inc(s_pool, 1)
            pool.wait_ge(s_pool, 3)
            pool.affine_select(out=g["batch_sel"][:, :], in_=sel_low[:, :], compare_op=ALU.is_ge, fill=0.0,
                               base=S - 1, pattern=[[-1, P]], channel_multiplier=S).then_inc(s_pool, 1)

        @block.scalar
        def _(act):
            act.wait_ge(g["loads"], n_small[0])
            act.activation(g["tanh_g"][:, :], g["tanh_g"][:, :], ACT.Tanh).then_inc(ready, 1)

        @block.vector
        def _(dve):
            dve.memset(g["mask0"][:, :, :], 0.0).then_inc(s_dve, 1)
            dve.memset(g["ones"][:, :], 1.0)
            dve.memset(g["zeros"][:, :], 0.0)
            dve.memset(g["base"][:, :], 0.0)
            dve.wait_ge(s_ids, 1)
            dve.tensor_copy(g["expert_id"][:, :], ids[:, 0:E0])
            dve.tensor_copy(g["slot_id"][:, :], ids[:, E0:E0 + 2])
            dve.tensor_copy(g["starts"][:, :], ids[:, E0 + 2:])
            dve.wait_ge(g["loads"], n_small[0])
            dve.wait_ge(s_dve, 1)
            dve.tensor_scalar(g["mask0"][0:2, :, 0:S], mask_raw[:, :, :], -MASKED, MASKED, ALU.mult, ALU.add)
            dve.wait_ge(ready, 1)
            dve.tensor_scalar(g["gain_o"][:, :], g["gain_o"][:, :], g["tanh_g"][:, 0:1], None, ALU.mult)
            dve.tensor_scalar(g["bias_o"][:, :], g["bias_o"][:, :], g["tanh_g"][:, 0:1], None,
                              ALU.mult).then_inc(s_dve, 1)
    return g


def attention0(nc, m0, g):
    with ExitStack() as ctx:
        m = Mem(nc, ctx)
        kvT = m.sb("a_kvT", [P, 2, 2 * S])
        kT = m.sb("a_kT", [P, CH, 2, 2 * S])
        qT = m.sb("a_qT", [P, CH, P])
        v = m.sb("a_v", [P, 2, INNER])
        probs = m.sb("a_probs", [P, H, P])
        probsT = m.sb("a_probsT", [P, H, P])
        o = m.sb("a_o", [P, INNER])
        oT = m.sb("a_oT", [P, CH, P])
        normed = m.sb("a_normed", [P, 2, D])
        y = m.sb("a_y", [P, D])
        stats = m.sb("a_stats", [P, 3, 6])
        mv = m.sb("a_mv", [P, 3, 2])
        tmp = m.sb("a_tmp", [P, 8])
        rstd = m.sb("a_rstd", [P, 3])
        mx = m.sb("a_mx", [P, H])
        sums = m.sb("a_sums", [P, H])
        rsum = m.sb("a_rsum", [P, H])
        scores = m.psum("a_scores", [P, 4, BANK])
        ring = m.psum("a_ring", [P, SLOTS, BANK])

        PE = Steps(m.sem("a_pe"), ["s0", "s1", "s2", "s3", "x", "k0", "k1", "k2", "k3", "q0", "q1",
                                   "pt0", "pt1", "pt2", "pt3", "pv0", "pv1", "v0", "v1", "v2", "v3",
                                   "ot0", "ot1", "y"])
        SC = Steps(m.sem("a_act"), ["exp0", "exp1", "x", "exp2", "k0", "exp3", "k1", "k2", "k3", "q0", "q1",
                                    "pt0", "pt1", "pt2", "pt3", "ot0", "ot1"])
        VE = Steps(m.sem("a_dve"), ["stats", "go1", "aggr", "norm", "max0", "sub0", "max1", "sub1", "max2", "sub2",
                                    "max3", "sub3", "sum0", "sum1", "sum2", "sum3", "recip", "pv0", "pv1",
                                    "v0", "v1", "v2", "v3", "ystats", "go2", "yaggr", "ynorm"])
        PO = Steps(m.sem("a_pool"), ["r1", "r2", "r3", "r4", "r5", "r6", "r7", "y1", "y2", "g1", "g2", "x1"])
        RING = PE.names[4:]
        assert len(RING) % SLOTS == 0
        evac = {n: (VE if n[0] == "v" or n[:2] == "pv" else SC) for n in RING}
        evac_step = {n: n for n in RING}
        evac["y"], evac_step["y"] = VE, "ynorm"

        def slot(n):
            return ring[:, RING.index(n) % SLOTS, :]

        with nc.Block() as block:
            @block.tensor
            def _(pe):
                def free(n, it):
                    i = RING.index(n) - SLOTS
                    old = RING[i]
                    pe.wait_ge(evac[old].sem, evac[old].at(evac_step[old], it if i >= 0 else it - 1))

                def body(it, cur, nxt):
                    for q in range(4):
                        if not cur:
                            PE.skip(pe, f"s{q}", it)
                            continue
                        if q == 0:
                            pe.wait_ge(SC.sem, SC.at("q1", it - 1))
                        pe.wait_ge(VE.sem, VE.at(f"sub{q}", it - 1))
                        pe.matmul(scores[:, q, :], g["batch_sel"][:, :],
                                  g["mask0"][:, it, :].unsqueeze(1).broadcast_to([P, 4, P]),
                                  start=True, stop=False, skip_group_check=True)
                        for n in range(4):
                            hh = 4 * q + n
                            r, c = DH * (hh // HALF_HEADS), hh % HALF_HEADS
                            for b in range(2):
                                last = pe.matmul(scores[S * b:S * b + S, q, n * P:n * P + P],
                                                 qT[r:r + DH, c, S * b:S * b + S], kT[r:r + DH, c, b, :],
                                                 start=False, stop=(n == 3), skip_group_check=True)
                        last.then_inc(PE.sem, 1)

                    def do(names, run, emit):
                        for n in names:
                            free(n, it)
                            if not run:
                                PE.skip(pe, n, it)
                                continue
                            emit(n).then_inc(PE.sem, 1)

                    def t_in(n):
                        pe.wait_ge(VE.sem, VE.at("norm", it))
                        for j in range(2):
                            last = pe.transpose(slot(n)[:, j * P:j * P + P], normed[:, j, :], g["ident"][:, :])
                        return last

                    def proj_k(n):
                        if n == "k0":
                            pe.wait_ge(SC.sem, SC.at("x", it))
                        for j in range(2):
                            c = 2 * int(n[1]) + j
                            last = pe.matmul(slot(n)[:, j * 256:j * 256 + 256], g["wkv0"][:, c * P:c * P + P],
                                             kvT[:, :, :], start=True, stop=True)
                        return last

                    def proj_q(n):
                        for j in range(4):
                            c = 4 * int(n[1]) + j
                            last = pe.matmul(slot(n)[:, j * P:j * P + P], g["wq0"][:, c * P:c * P + P],
                                             kvT[:, :, S:2 * S], start=True, stop=True)
                        return last

                    def proj_v(n):
                        b, half = int(n[1]) // 2, int(n[1]) % 2
                        at = INNER + half * BANK
                        return pe.matmul(slot(n), kvT[:, b, :], g["wkv0"][:, at:at + BANK],
                                         start=True, stop=True)

                    def t_probs(n):
                        q = int(n[2])
                        pe.wait_ge(SC.sem, SC.at(f"exp{q}", it))
                        for j in range(4):
                            last = pe.transpose(slot(n)[:, j * P:j * P + P], probs[:, 4 * q + j, :],
                                                g["ident"][:, :])
                        return last

                    def pv(n):
                        pe.wait_ge(SC.sem, SC.at(f"pt{2 * int(n[2]) + 1}", it))
                        pe.wait_ge(VE.sem, VE.at("v3", it - 1))
                        for j in range(HALF_HEADS):
                            hh = HALF_HEADS * int(n[2]) + j
                            for b in range(2):
                                last = pe.matmul(slot(n)[S * b:S * b + S, j * DH:j * DH + DH],
                                                 probsT[:, hh, S * b:S * b + S],
                                                 v[:, b, head(hh) * DH:head(hh) * DH + DH],
                                                 start=True, stop=True)
                        return last

                    def t_o(n):
                        pe.wait_ge(VE.sem, VE.at(f"pv{n[2]}", it))
                        for j in range(4):
                            k = 4 * int(n[2]) + j
                            last = pe.transpose(slot(n)[:, j * P:j * P + P], o[:, k * P:k * P + P],
                                                g["ident"][:, :])
                        return last

                    def out(n):
                        pe.wait_ge(SC.sem, SC.at("ot1", it))
                        for k in range(CH):
                            last = pe.matmul(slot(n)[:, 0:D], oT[:, k, :], g["wout0"][:, k, :],
                                             start=(k == 0), stop=(k == CH - 1))
                        return last

                    do(["x"], nxt, t_in)
                    do(["k0", "k1", "k2", "k3"], nxt, proj_k)
                    do(["q0", "q1"], nxt, proj_q)
                    do(["pt0", "pt1", "pt2", "pt3"], cur, t_probs)
                    do(["pv0", "pv1"], cur, pv)
                    do(["v0", "v1", "v2", "v3"], nxt, proj_v)
                    do(["ot0", "ot1"], cur, t_o)
                    do(["y"], cur, out)

                run_tiles(nc.tensor, body)

            @block.scalar
            def _(act):
                def body(it, cur, nxt):
                    for n in SC.names:
                        runs = nxt if n[0] in "xkq" else cur
                        if not runs:
                            SC.skip(act, n, it)
                            continue
                        if n[:3] == "exp":
                            q = int(n[3])
                            act.wait_ge(VE.sem, VE.at(f"sub{q}", it))
                            p = probs[:, 4 * q:4 * q + 4, :]
                            act.activation(p, p, ACT.Exp).then_inc(SC.sem, 1)
                            continue
                        act.wait_ge(PE.sem, PE.at(n, it))
                        if n == "x":
                            for j in range(2):
                                ins = act.activation(
                                    kvT[:, :, S * j:S * j + S],
                                    slot(n)[:, j * P:j * P + P].rearrange("p (b s) -> p b s", b=2),
                                    ACT.Identity, bias=g["cols"][:, 2 * j + 1:2 * j + 2],
                                    scale=g["cols"][:, 2 * j:2 * j + 1])
                        elif n[0] == "k":
                            c = 2 * int(n[1])
                            ins = act.activation(kT[:, c:c + 2, :, :].rearrange("p c b j -> p (c b j)"), slot(n),
                                                 ACT.Copy)
                        elif n[0] == "q":
                            c = 4 * int(n[1])
                            ins = act.activation(qT[:, c:c + 4, :].rearrange("p c j -> p (c j)"), slot(n),
                                                 ACT.Copy, scale=DH ** -0.5)
                        elif n[:2] == "pt":
                            c = 4 * int(n[2])
                            ins = act.activation(probsT[:, c:c + 4, :].rearrange("p c j -> p (c j)"), slot(n),
                                                 ACT.Copy)
                        else:
                            c = 4 * int(n[2])
                            ins = act.activation(oT[:, c:c + 4, :].rearrange("p c j -> p (c j)"), slot(n),
                                                 ACT.Copy)
                        ins.then_inc(SC.sem, 1)

                run_tiles(nc.scalar, body)

            @block.vector
            def _(dve):
                def body(it, cur, nxt):
                    if nxt:
                        dve.bn_stats(stats[:, 0, :], g["ctx"][:, it + 1, :])
                        dve.bn_stats(stats[:, 1, :], g["x"][:, it + 1, :]).then_inc(VE.sem, 1)
                        dve.wait_ge(VE.sem, VE.at("stats", it))
                        dve.wait_ge(PO.sem, PO.at("r7", it - 1))
                        dve.sem_inc(VE.sem, 1)
                        dve.bn_aggr(mv[:, 0, :], stats[:, 0, :])
                        dve.bn_aggr(mv[:, 1, :], stats[:, 1, :]).then_inc(VE.sem, 1)
                        dve.wait_ge(VE.sem, VE.at("aggr", it))
                        dve.wait_ge(PO.sem, PO.at("r7", it))
                        dve.wait_ge(PE.sem, PE.at("x", it - 1))
                        dve.tensor_scalar(normed[:, 0, :], g["ctx"][:, it + 1, :], mv[:, 0, 0:1], rstd[:, 0:1],
                                          ALU.subtract, ALU.mult)
                        dve.tensor_scalar(normed[:, 1, :], g["x"][:, it + 1, :], mv[:, 1, 0:1], rstd[:, 1:2],
                                          ALU.subtract, ALU.mult).then_inc(VE.sem, 1)
                    else:
                        for n in ("stats", "go1", "aggr", "norm"):
                            VE.skip(dve, n, it)
                    if cur:
                        for q in range(4):
                            s4 = scores[:, q, :].rearrange("p (h j) -> p h j", h=4)
                            dve.wait_ge(PE.sem, PE.at(f"s{q}", it))
                            if q == 0:
                                dve.wait_ge(VE.sem, VE.at("pv1", it - 1))
                            dve.tensor_reduce(mx[:, 4 * q:4 * q + 4], s4, AX_X, ALU.max).then_inc(VE.sem, 1)
                            dve.wait_ge(VE.sem, VE.at(f"max{q}", it))
                            dve.wait_ge(PE.sem, PE.at(f"pt{q}", it - 1))
                            dve.tensor_tensor(probs[:, 4 * q:4 * q + 4, :], s4,
                                              mx[:, 4 * q:4 * q + 4].unsqueeze(2).broadcast_to([P, 4, P]),
                                              ALU.subtract).then_inc(VE.sem, 1)
                        for q in range(4):
                            dve.wait_ge(SC.sem, SC.at(f"exp{q}", it))
                            dve.tensor_reduce(sums[:, 4 * q:4 * q + 4], probs[:, 4 * q:4 * q + 4, :], AX_X,
                                              ALU.add).then_inc(VE.sem, 1)
                        dve.wait_ge(VE.sem, VE.at("sum3", it))
                        dve.reciprocal(rsum[:, :], sums[:, :]).then_inc(VE.sem, 1)
                        dve.wait_ge(VE.sem, VE.at("recip", it))
                        for j in range(2):
                            dve.wait_ge(PE.sem, PE.at(f"pv{j}", it))
                            dve.wait_ge(PE.sem, PE.at(f"ot{j}", it - 1))
                            dve.tensor_tensor(
                                o[:, j * BANK:j * BANK + BANK].rearrange("p (h e) -> p h e", e=DH),
                                slot(f"pv{j}").rearrange("p (h e) -> p h e", e=DH),
                                rsum[:, 8 * j:8 * j + 8].unsqueeze(2).broadcast_to([P, 8, DH]),
                                ALU.mult).then_inc(VE.sem, 1)
                    else:
                        for n in VE.names[4:19]:
                            VE.skip(dve, n, it)
                    for n in ("v0", "v1", "v2", "v3"):
                        if not nxt:
                            VE.skip(dve, n, it)
                            continue
                        dve.wait_ge(PE.sem, PE.at(n, it))
                        b, half = int(n[1]) // 2, int(n[1]) % 2
                        dve.tensor_copy(v[:, b, half * BANK:half * BANK + BANK], slot(n)).then_inc(VE.sem, 1)
                    if cur:
                        ys = slot("y")[:, 0:D]
                        dve.wait_ge(PE.sem, PE.at("y", it))
                        dve.bn_stats(stats[:, 2, :], ys).then_inc(VE.sem, 1)
                        dve.wait_ge(VE.sem, VE.at("ystats", it))
                        dve.sem_inc(VE.sem, 1)
                        dve.bn_aggr(mv[:, 2, :], stats[:, 2, :]).then_inc(VE.sem, 1)
                        dve.wait_ge(VE.sem, VE.at("yaggr", it))
                        dve.wait_ge(PO.sem, PO.at("y2", it))
                        dve.wait_ge(PO.sem, PO.at("g1", it - 1))
                        dve.tensor_scalar(y[:, :], ys, mv[:, 2, 0:1], rstd[:, 2:3], ALU.subtract,
                                          ALU.mult).then_inc(VE.sem, 1)
                    else:
                        for n in ("ystats", "go2", "yaggr", "ynorm"):
                            VE.skip(dve, n, it)

                run_tiles(nc.vector, body)

            @block.gpsimd
            def _(pool):
                def body(it, cur, nxt):
                    def chain(name, ins):
                        ins.then_inc(PO.sem, 1)
                        pool.wait_ge(PO.sem, PO.at(name, it))
                    nh = g["neg_half"]
                    if nxt:
                        pool.wait_ge(VE.sem, VE.at("aggr", it))
                        pool.wait_ge(VE.sem, VE.at("norm", it - 1))
                        chain("r1", pool.tensor_tensor(tmp[:, 0:2], mv[:, 0:2, 1], g["eps"][:, :], ALU.add))
                        chain("r2", pool.tensor_tensor(rstd[:, 0:2], tmp[:, 0:2], nh[:, :], ALU.pow))
                        chain("r3", pool.tensor_tensor(tmp[:, 2:3], mv[:, 1, 1:2], rstd[:, 1:2], ALU.mult))
                        chain("r4", pool.tensor_tensor(tmp[:, 3:4], tmp[:, 2:3], rstd[:, 1:2], ALU.mult))
                        chain("r5", pool.tensor_tensor(tmp[:, 4:5], tmp[:, 3:4], g["eps"][:, 0:1], ALU.add))
                        chain("r6", pool.tensor_tensor(tmp[:, 5:6], tmp[:, 4:5], nh[:, 0:1], ALU.pow))
                        pool.tensor_tensor(rstd[:, 1:2], tmp[:, 5:6], rstd[:, 1:2], ALU.mult).then_inc(PO.sem, 1)
                    else:
                        for n in PO.names[:7]:
                            PO.skip(pool, n, it)
                    if cur:
                        pool.wait_ge(VE.sem, VE.at("yaggr", it))
                        chain("y1", pool.tensor_tensor(tmp[:, 6:7], mv[:, 2, 1:2], g["eps"][:, 0:1], ALU.add))
                        pool.tensor_tensor(rstd[:, 2:3], tmp[:, 6:7], nh[:, 0:1], ALU.pow).then_inc(PO.sem, 1)
                        pool.wait_ge(VE.sem, VE.at("ynorm", it))
                        chain("g1", pool.tensor_tensor(gy[:, :], y[:, :], g["gain_o"][:, :], ALU.mult))
                        chain("g2", pool.tensor_tensor(gy[:, :], gy[:, :], g["bias_o"][:, :], ALU.add))
                        pool.tensor_tensor(g["x"][:, it, :], g["x"][:, it, :], gy[:, :],
                                           ALU.add).then_inc(PO.sem, 1)
                    else:
                        for n in PO.names[7:]:
                            PO.skip(pool, n, it)

                gy = m.sb("a_gy", [P, D])
                run_tiles(nc.gpsimd, body)


def finish_weights(nc, m0, g, w):
    with ExitStack() as ctx:
        m = Mem(nc, ctx)
        raw = m.sb("raw_weights", [P, BLOCKS, P])
        banks = m.psum("w_banks", [P, 4, BANK])
        bias_bank = m.psum("w_bias_bank", [P, BANK])
        loaded = m.sem("raw_loaded")
        turned = m.sem("weights_turned")
        kept = m.sem("weights_kept")
        biased = m.sem("out_bias_summed")
        mask_step = m.sem("mask1_step")
        loads = [(raw[:, GATE:GATE + 16, :], w["L1_ffn_expert_gate"].rearrange("(k e) i d -> (e i) k d", e=2)),
                 (raw[:, UP:UP + 16, :], w["L1_ffn_expert_up"].rearrange("(k e) i d -> (e i) k d", e=2)),
                 (raw[:, DOWN:DOWN + 16, :].rearrange("p k (e i) -> p (k e) i", e=2),
                  w["L1_ffn_expert_down"].rearrange("e h i -> h e i")),
                 (raw[:, SHARED, :], w["L1_ffn_shared_gate"]),
                 (raw[:, SHARED + 1, :], w["L1_ffn_shared_up"]),
                 (raw[:, SHARED_DOWN, :], w["L1_ffn_shared_down"]),
                 (raw[0:E1, ROUTER1, :], w["L1_ffn_gate_w"]),
                 (raw[0:E0, ROUTER0, :], w["L0_ffn_expert_sel"]),
                 (raw[0:CH, BQ, :], w["L1_xattn_bq"].rearrange("(c p) e -> c (p e)", p=2)),
                 (raw[0:CH, BK, :], w["L1_xattn_bk"].rearrange("(c p) e -> c (p e)", p=2))]
        for p in range(2):
            loads.append((raw[4 * p:4 * p + 4, BV, :].rearrange("k (c e) -> k c e", c=2),
                          w["L1_xattn_bv"].rearrange("(k c p) e -> p k c e", c=2, p=2)[p]))
        rows = [P] * ROUTER1 + [E1, E0, CH, CH, CH]
        sets = [range(k, min(k + 4, BLOCKS)) for k in range(0, BLOCKS, 4)]
        with nc.Block() as block:
            @block.sync
            def _(sp):
                for dst, src in loads:
                    sp.dma_start(dst, src).then_inc(loaded, 16)

            @block.tensor
            def _(pe):
                pe.wait_ge(loaded, 16 * len(loads))
                for n, blocks in enumerate(sets):
                    if n >= 4:
                        pe.wait_ge(kept, n - 3)
                    for j, k in enumerate(blocks):
                        last = pe.transpose(banks[:, n % 4, j * P:j * P + rows[k]], raw[0:rows[k], k, :],
                                            g["ident"][0:rows[k], 0:rows[k]])
                    last.then_inc(turned, 1)
                pe.wait_ge(g["loads1"], g["n_late"])
                pe.wait_ge(kept, len(sets))
                for k in range(CH):
                    last = pe.matmul(bias_bank[:, 0:D], g["wT"][:, BV, k:k + 1].broadcast_to([P, P]),
                                     g["wo1"][:, k, :], start=(k == 0), stop=(k == CH - 1))
                last.then_inc(biased, 1)

            @block.scalar
            def _(act):
                for n, blocks in enumerate(sets):
                    act.wait_ge(turned, n + 1)
                    if blocks[-1] < ROUTER1:
                        last = act.activation(g["wT"][:, blocks[0]:blocks[-1] + 1, :].rearrange("p k c -> p (k c)"),
                                              banks[:, n % 4, 0:len(blocks) * P], ACT.Copy)
                    else:
                        for j, k in enumerate(blocks):
                            last = act.activation(g["wT"][:, k, 0:rows[k]], banks[:, n % 4, j * P:j * P + rows[k]],
                                                  ACT.Copy, scale=DH ** -0.5 if k == BQ else 1.0)
                    last.then_inc(kept, 1)

            @block.vector
            def _(dve):
                dve.wait_ge(g["loads1"], g["n_late"])
                dve.tensor_scalar(g["mask1"][:, :], g["mask1"][:, :], -1.0, 1.0, ALU.mult,
                                  ALU.add).then_inc(mask_step, 1)
                dve.wait_ge(mask_step, 1)
                dve.tensor_scalar(g["mask1"][:, :], g["mask1"][:, :], MASK1, None, ALU.mult)
                dve.wait_ge(biased, 1)
                dve.tensor_tensor(g["out_bias1"][:, :], bias_bank[:, 0:D], g["out_bias1"][:, :],
                                  ALU.add).then_inc(mask_step, 1)
                dve.wait_ge(mask_step, 2)
                dve.tensor_scalar(g["out_bias1"][:, :], g["out_bias1"][:, :], g["tanh_g"][:, 1:2], None,
                                  ALU.mult).then_inc(mask_step, 1)


class Route:

    def __init__(self, nc, m, g, bank):
        self.nc, self.g, self.bank = nc, g, bank
        self.xf = m.sb("r_xf", [P, D])
        self.xfT = m.sb("r_xfT", [P, P])
        self.stats = m.sb("r_stats", [P, 6])
        self.mv = m.sb("r_mv", [P, 2])
        self.tmp = m.sb("r_tmp", [P, 1])
        self.rstd = m.sb("r_rstd", [P, 1])
        self.th = m.sb("r_th", [P, E0])
        self.sc = m.sb("r_scores", [P, E0])
        self.top8 = m.sb("r_top8", [P, 8])
        self.index8 = m.sb("r_index8", [P, 8], mybir.dt.uint32)
        self.onehot = m.sb("r_onehot", [P, TOP0, E0])
        self.sent = m.sb("r_sent", [P, E0], BF16)
        self.pos = m.sb("r_pos", [P, E0])
        self.at = m.sb("r_at", [P, TOP0, E0])
        self.rows = m.sb("r_rows", [P, TOP0], mybir.dt.uint32)
        self.scattered = m.sem("scattered")
        self.PE = Steps(m.sem("r_pe"), ["x", "logits", "rank"])
        self.SC = Steps(m.sem("r_act"), ["x", "logits"])
        self.VE = Steps(m.sem("r_dve"), ["stats", "go", "aggr", "norm", "sc", "go_top", "top", "go_index", "index",
                                         "chosen", "onehot", "sent", "pos", "base", "at", "position", "rows"])
        self.PO = Steps(m.sem("r_pool"), ["r1", "r2", "go"])

    def on_tensor(self, pe, it, part):
        g, PE = self.g, self.PE
        if part == 0:
            pe.wait_ge(self.VE.sem, self.VE.at("norm", it))
            pe.transpose(self.bank[:, 0:P], self.xf[:, :], g["ident"][:, :]).then_inc(PE.sem, 1)
        elif part == 1:
            pe.wait_ge(self.SC.sem, self.SC.at("x", it))
            pe.matmul(self.bank[:, P:P + E0], self.xfT[:, :], g["wT"][:, ROUTER0, 0:E0], start=True,
                      stop=True).then_inc(PE.sem, 1)
        else:
            pe.wait_ge(self.VE.sem, self.VE.at("sent", it))
            pe.wait_ge(self.SC.sem, self.SC.at("logits", it))
            pe.matmul(self.bank[:, P + E0:P + 2 * E0], g["before"][:, :], self.sent[:, :], start=True, stop=True)
            pe.matmul(self.bank[:, P + 2 * E0:P + 3 * E0], g["ones"][:, :], self.sent[:, :], start=True,
                      stop=True).then_inc(PE.sem, 1)

    def on_scalar(self, act, it):
        act.wait_ge(self.PE.sem, self.PE.at("x", it))
        act.activation(self.xfT[:, :], self.bank[:, 0:P], ACT.Copy).then_inc(self.SC.sem, 1)
        act.wait_ge(self.PE.sem, self.PE.at("logits", it))
        act.wait_ge(self.VE.sem, self.VE.at("sc", it - 1))
        act.activation(self.th[:, :], self.bank[:, P:P + E0], ACT.Tanh, scale=0.5).then_inc(self.SC.sem, 1)

    def on_vector(self, dve, it, part):
        g, VE = self.g, self.VE
        xt = g["x"][:, it, :]

        def chain(name, ins):
            ins.then_inc(VE.sem, 1)
            dve.wait_ge(VE.sem, VE.at(name, it))

        def seen():
            dve.sem_inc(VE.sem, 1)
        if part == 0:
            chain("stats", dve.bn_stats(self.stats[:, :], xt))
            dve.wait_ge(self.PO.sem, self.PO.at("r2", it - 1))
            seen()
            dve.bn_aggr(self.mv[:, :], self.stats[:, :]).then_inc(VE.sem, 1)
        elif part == 1:
            dve.wait_ge(VE.sem, VE.at("aggr", it))
            dve.wait_ge(self.PO.sem, self.PO.at("r2", it))
            dve.wait_ge(self.PE.sem, self.PE.at("x", it - 1))
            if not (isinstance(it, int) and it == 0):
                dve.wait_ge(self.scattered, 16 * TOP0 * it)
            dve.tensor_scalar(self.xf[:, :], xt, self.mv[:, 0:1], self.rstd[:, :], ALU.subtract,
                              ALU.mult).then_inc(VE.sem, 1)
        elif part == 2:
            dve.wait_ge(self.SC.sem, self.SC.at("logits", it))
            chain("sc", dve.tensor_scalar(self.sc[:, :], self.th[:, :], 0.5, 0.5, ALU.mult, ALU.add))
            seen()
            chain("top", dve.max(self.top8[:, :], self.sc[:, :]))
            seen()
            dve.max_index(self.index8[:, :], self.top8[:, :], self.sc[:, :]).then_inc(VE.sem, 1)
            dve.tensor_scalar(g["gates"][:, it, :], self.top8[:, 0:TOP0], g["tanh_g"][:, 2:3], None, ALU.mult)
            dve.wait_ge(VE.sem, VE.at("index", it))
            chain("chosen", dve.tensor_copy(g["chosen"][:, it, :], self.index8[:, 0:TOP0]))
            ids = g["expert_id"][:, :].unsqueeze(1).broadcast_to([P, TOP0, E0])
            chain("onehot", dve.tensor_tensor(
                self.onehot[:, :, :], ids, g["chosen"][:, it, :].unsqueeze(2).broadcast_to([P, TOP0, E0]),
                ALU.is_equal))
            with self.nc.allow_low_precision("zeros and ones"):
                dve.tensor_reduce(self.sent[:, :], self.onehot[:, :, :].rearrange("p j e -> p e j"), AX_X,
                                  ALU.add).then_inc(VE.sem, 1)
        else:
            dve.wait_ge(self.PE.sem, self.PE.at("rank", it))
            chain("pos", dve.tensor_tensor(self.pos[:, :], self.bank[:, P + E0:P + 2 * E0], g["base"][:, :],
                                           ALU.add))
            dve.tensor_tensor(g["base"][:, :], self.bank[:, P + 2 * E0:P + 3 * E0], g["base"][:, :],
                              ALU.add).then_inc(VE.sem, 1)
            chain("at", dve.tensor_tensor(self.at[:, :, :], self.onehot[:, :, :],
                                          self.pos[:, :].unsqueeze(1).broadcast_to([P, TOP0, E0]), ALU.mult))
            chain("position", dve.tensor_reduce(g["position"][:, it, :], self.at[:, :, :], AX_X, ALU.add))
            dve.scalar_tensor_tensor(self.rows[:, :], g["chosen"][:, it, :], float(REGION),
                                     g["position"][:, it, :], ALU.mult, ALU.add).then_inc(VE.sem, 1)

    def on_gpsimd(self, pool, it, part):
        g, PO = self.g, self.PO
        if part == 0:
            pool.wait_ge(self.VE.sem, self.VE.at("aggr", it))
            pool.tensor_tensor(self.tmp[:, :], self.mv[:, 1:2], g["eps"][:, 0:1], ALU.add).then_inc(PO.sem, 1)
            pool.wait_ge(PO.sem, PO.at("r1", it))
            pool.wait_ge(self.VE.sem, self.VE.at("norm", it - 1))
            pool.tensor_tensor(self.rstd[:, :], self.tmp[:, :], g["neg_half"][:, 0:1], ALU.pow).then_inc(PO.sem, 1)
        else:
            pool.wait_ge(self.VE.sem, self.VE.at("rows", it))
            pool.sem_inc(PO.sem, 1)
            for j in range(TOP0):
                pool.indirect_dma_start(g["xs"], bass.IndirectOffsetOnAxis(self.rows[:, j:j + 1], 0), self.xf[:, :],
                                        None, bounds_check=E0 * REGION - 1).then_inc(self.scattered, 16)


def route_alone(nc, m0, g):
    with ExitStack() as ctx:
        m = Mem(nc, ctx)
        bank = m.psum("r_bank", [P, BANK])
        route = Route(nc, m, g, bank)
        for s in (route.PE, route.SC, route.VE, route.PO):
            s.first = 0
        with nc.Block() as block:
            def loop(eng, body):
                body(0)
                with eng.Fori(1, TILES) as it:
                    body(it)

            @block.tensor
            def _(pe):
                def body(it):
                    if not isinstance(it, int) or it > 0:
                        pe.wait_ge(route.VE.sem, route.VE.at("base", it - 1))
                    for part in range(3):
                        route.on_tensor(pe, it, part)
                loop(nc.tensor, body)

            @block.scalar
            def _(act):
                loop(nc.scalar, lambda it: route.on_scalar(act, it))

            @block.vector
            def _(dve):
                def body(it):
                    for part in range(4):
                        route.on_vector(dve, it, part)
                loop(nc.vector, body)

            @block.gpsimd
            def _(pool):
                def body(it):
                    for part in range(2):
                        route.on_gpsimd(pool, it, part)
                loop(nc.gpsimd, body)
                pool.wait_ge(route.scattered, 16 * TOP0 * TILES)


def experts0(nc, m0, g, w):
    with ExitStack() as ctx:
        m = Mem(nc, ctx)
        keys = m.sb("b_keys", [P, E0, P])
        values = m.sb("b_values", [P, E0, D])
        table = m.sb("b_table", [1, 512], mybir.dt.int32)
        counts = m.sb("b_counts", [1, E0], mybir.dt.int32)
        weights_in = m.sem("b_weights_in")
        tails_sp, tails_act = m.sem("b_tails_sp"), m.sem("b_tails_act")
        with ExitStack() as ctx2:
            n = Mem(nc, ctx2)
            over = n.sb("b_over", [P, E0, TILES])
            tiles = n.sb("b_tiles", [P, E0])
            upto = n.sb("b_upto", [P, E0])
            none = n.sb("b_none", [P, E0])
            passed = n.sb("b_passed", [P, 2, E0])
            before = n.sb("b_before", [P, 2, E0])
            slot = n.sb("b_slot", [P, 4, 2])
            plan_bank = n.psum("b_plan_bank", [P, BANK])
            V = n.sem("b_plan")
            counted, planned, tabled = n.sem("b_counted"), n.sem("b_planned"), n.sem("b_tabled")
            with nc.Block() as block:
                @block.sync
                def _(sp):
                    sp.dma_start(keys[:, :, :], w["L0_ffn_keys"].rearrange("k d e -> d k e")).then_inc(weights_in, 16)
                    sp.dma_start(values[:, :, :],
                                 w["L0_ffn_values"].rearrange("k e v -> e k v")).then_inc(weights_in, 16)
                    sp.wait_ge(counted, 1)
                    with nc.sync.Fori(0, E0 // 2) as e:
                        row = sp.value_load(counts[0:1, bass.ds(e, 1)], min_val=0, max_val=E0 * REGION - P)
                        sp.dma_start(g["xs"][bass.ds(row, P), :], g["zeros"][:, :]).then_inc(tails_sp, 16)

                @block.scalar
                def _(act):
                    act.wait_ge(counted, 1)
                    with nc.scalar.Fori(E0 // 2, E0) as e:
                        row = act.value_load(counts[0:1, bass.ds(e, 1)], min_val=0, max_val=E0 * REGION - P)
                        act.dma_start(g["xs"][bass.ds(row, P), :], g["zeros"][:, :]).then_inc(tails_act, 16)

                @block.tensor
                def _(pe):
                    pe.wait_ge(planned, 1)
                    for v in range(2):
                        for h in range(2):
                            last = pe.matmul(plan_bank[0:1, 256 * v + P * h:256 * v + P * h + P],
                                             slot[:, 3 * v, h:h + 1], g["ident"][:, :], start=True, stop=True)
                    last.then_inc(tabled, 1)

                @block.vector
                def _(dve):
                    step = [0]

                    def chain(ins):
                        ins.then_inc(V, 1)
                        step[0] += 1
                        dve.wait_ge(V, step[0])
                    base = g["base"][:, :]
                    dve.scalar_tensor_tensor(counts[:, :], g["expert_id"][0:1, :], float(REGION), g["base"][0:1, :],
                                             ALU.mult, ALU.add).then_inc(counted, 1)
                    chain(dve.tensor_tensor(over[:, :, :], base.unsqueeze(2).broadcast_to([P, E0, TILES]),
                                            g["starts"][:, :].unsqueeze(1).broadcast_to([P, E0, TILES]), ALU.is_gt))
                    chain(dve.tensor_reduce(tiles[:, :], over[:, :, :], AX_X, ALU.add))
                    chain(dve.memset(none[:, :], 0.0))
                    chain(dve.tensor_tensor_scan(upto[:, :], tiles[:, :], none[:, :], 0.0, ALU.add, ALU.add))
                    chain(dve.tensor_tensor(none[:, :], upto[:, :], tiles[:, :], ALU.subtract))
                    chain(dve.tensor_scalar(g["first_row"][:, :], none[:, :], float(P), None, ALU.mult))
                    both = [P, 2, E0]
                    sid = g["slot_id"][:, :]
                    chain(dve.tensor_tensor(passed[:, :, :], upto[:, :].unsqueeze(1).broadcast_to(both),
                                            sid.unsqueeze(2).broadcast_to(both), ALU.is_le))
                    chain(dve.tensor_reduce(slot[:, 0, :], passed[:, :, :], AX_X, ALU.add))
                    chain(dve.tensor_tensor(before[:, :, :], passed[:, :, :],
                                            tiles[:, :].unsqueeze(1).broadcast_to(both), ALU.mult))
                    chain(dve.tensor_reduce(slot[:, 1, :], before[:, :, :], AX_X, ALU.add))
                    chain(dve.tensor_scalar(slot[:, 2, :], slot[:, 0, :], E0 - 0.5, None, ALU.is_lt))
                    chain(dve.tensor_tensor(slot[:, 1, :], sid, slot[:, 1, :], ALU.subtract))
                    chain(dve.tensor_tensor(slot[:, 0, :], slot[:, 0, :], slot[:, 2, :], ALU.mult))
                    chain(dve.tensor_tensor(slot[:, 1, :], slot[:, 1, :], slot[:, 2, :], ALU.mult))
                    chain(dve.tensor_scalar(slot[:, 1, :], slot[:, 1, :], float(P), None, ALU.mult))
                    dve.scalar_tensor_tensor(slot[:, 3, :], slot[:, 0, :], float(REGION), slot[:, 1, :], ALU.mult,
                                             ALU.add).then_inc(planned, 1)
                    dve.wait_ge(tabled, 1)
                    dve.tensor_copy(table[:, :], plan_bank[0:1, :]).then_inc(V, 1)

        xr = m.sb("b_rows", [P, 4, BATCH, D])
        xT = m.sb("b_xT", [P, BATCH, P])
        h = m.sb("b_h", [P, BATCH, P])
        hT = m.sb("b_hT", [P, BATCH, P])
        y = m.sb("b_y", [P, 4, BATCH, D])
        x_bank = m.psum("b_x_bank", [P, BANK])
        h_bank = m.psum("b_h_bank", [P, BANK])
        t_bank = m.psum("b_t_bank", [P, BANK])
        y_bank = m.psum("b_y_bank", [P, BANK])
        loaded = [m.sem(f"b_loaded{u}") for u in range(4)]
        stored = [m.sem(f"b_stored{u}") for u in range(4)]
        LAG = {"y": 3, "ht": 2, "h": 1, "x": 0}
        PE = Steps(m.sem("b_pe"), ["y", "ht", "h", "x"], 0)
        SC = Steps(m.sem("b_act"), ["ht", "x"], 0)
        VE = Steps(m.sem("b_dve"), ["y", "h"], 0)
        END = BATCHES + 3

        def active(name, n):
            return True if not isinstance(n, int) else LAG[name] <= n < BATCHES + LAG[name]

        def over_time(eng, body):
            for n in range(4):
                body(n, n, 0)
            with eng.Fori(4, BATCHES, 4) as n4:
                for u in range(4):
                    body(n4 + u, u, n4)
            for n in range(BATCHES, END):
                body(n, n % 4, n - n % 4)

        with nc.Block() as block:
            @block.sync
            def _(sp):
                sp.wait_ge(tails_sp, 16 * (E0 // 2))
                sp.wait_ge(tails_act, 16 * (E0 // 2))
                ys_v = g["ys"].rearrange("(b j p) d -> b p j d", j=BATCH, p=P)

                def load(n, u):
                    if not isinstance(n, int) or n >= 4:
                        sp.wait_ge(PE.sem, PE.at("x", n - 4))
                    for j in range(BATCH):
                        row = sp.value_load(table[0:1, bass.ds(n * BATCH + (256 + j), 1)], min_val=0,
                                            max_val=E0 * REGION - P)
                        sp.dma_start(xr[:, u, j, :], g["xs"][bass.ds(row, P), :]).then_inc(loaded[u], 16)

                def store(b, u):
                    sp.wait_ge(VE.sem, VE.at("y", b + 3))
                    sp.dma_start(ys_v[b], y[:, u, :, :]).then_inc(stored[u], 16)

                for n in range(8):
                    load(n, n % 4)
                    if n == 7:
                        store(0, 0)
                with nc.sync.Fori(8, BATCHES, 4) as n4:
                    for u in range(4):
                        load(n4 + u, u)
                        store(n4 + (u - 7), (u + 1) % 4)
                for b in range(BATCHES - 7, BATCHES):
                    store(b, b % 4)
                for u in range(4):
                    sp.wait_ge(stored[u], 16 * (BATCHES // 4))

            @block.tensor
            def _(pe):
                def experts(b):
                    return [pe.value_load(table[0:1, bass.ds(b * BATCH + j, 1)], min_val=0, max_val=E0 - 1)
                            for j in range(BATCH)]

                def body(n, u, n4):
                    for name in PE.names:
                        if not active(name, n):
                            PE.skip(pe, name, n)
                            continue
                        if name == "y":
                            es = experts(n - 3)
                            pe.wait_ge(SC.sem, SC.at("ht", n - 1))
                            pe.wait_ge(VE.sem, VE.at("y", n - 1))
                            for j in range(BATCH):
                                last = pe.matmul(y_bank[:, j * P:j * P + P], hT[:, j, :], values[:, es[j], :],
                                                 start=True, stop=True)
                        elif name == "ht":
                            pe.wait_ge(VE.sem, VE.at("h", n - 1))
                            for j in range(BATCH):
                                last = pe.transpose(t_bank[:, j * P:j * P + P], h[:, j, :], g["ident"][:, :])
                        elif name == "h":
                            es = experts(n - 1)
                            pe.wait_ge(SC.sem, SC.at("x", n - 1))
                            for j in range(BATCH):
                                last = pe.matmul(h_bank[:, j * P:j * P + P], xT[:, j, :], keys[:, es[j], :],
                                                 start=True, stop=True)
                        else:
                            pe.wait_ge(loaded[u], n4 * 16 + 64)
                            for j in range(BATCH):
                                last = pe.transpose(x_bank[:, j * P:j * P + P], xr[:, u, j, :], g["ident"][:, :])
                        last.then_inc(PE.sem, 1)

                pe.wait_ge(weights_in, 32)
                over_time(nc.tensor, body)

            @block.scalar
            def _(act):
                def body(n, u, n4):
                    for name, bank, dst in (("ht", t_bank, hT), ("x", x_bank, xT)):
                        if not active(name, n):
                            SC.skip(act, name, n)
                            continue
                        act.wait_ge(PE.sem, PE.at(name, n))
                        act.activation(dst[:, :, :].rearrange("p j c -> p (j c)"), bank[:, :],
                                       ACT.Copy).then_inc(SC.sem, 1)
                over_time(nc.scalar, body)

            @block.vector
            def _(dve):
                def body(n, u, n4):
                    if active("y", n):
                        dve.wait_ge(PE.sem, PE.at("y", n))
                        if not isinstance(n, int) or n >= 7:
                            dve.wait_ge(stored[(u + 1) % 4], n4 * 4 if u == 3 else (n4 - 4) * 4)
                        dve.tensor_copy(y[:, (u + 1) % 4, :, :].rearrange("p j c -> p (j c)"),
                                        y_bank[:, :]).then_inc(VE.sem, 1)
                    else:
                        VE.skip(dve, "y", n)
                    if active("h", n):
                        dve.wait_ge(PE.sem, PE.at("h", n))
                        dve.tensor_scalar(h[:, :, :].rearrange("p j c -> p (j c)"), h_bank[:, :], 0.0, None,
                                          ALU.max).then_inc(VE.sem, 1)
                    else:
                        VE.skip(dve, "h", n)
                over_time(nc.vector, body)


def attention1(nc, m0, g):
    with ExitStack() as ctx:
        m = Mem(nc, ctx)
        inT = m.sb("c_inT", [P, 2, P])
        kT = m.sb("c_kT", [P, CH, P])
        qT = m.sb("c_qT", [P, CH, P])
        v = m.sb("c_v", [P, 2, BANK])
        probs = m.sb("c_probs", [P, CH, 2, S])
        probsT = m.sb("c_probsT", [P, CH, P])
        o = m.sb("c_o", [P, INNER])
        oT = m.sb("c_oT", [P, CH, P])
        rows = m.sb("c_rows", [P, 2, D])
        stats = m.sb("c_stats", [P, 6])
        mv = m.sb("c_mv", [P, 2])
        tmp = m.sb("c_tmp", [P, 1])
        rstd = m.sb("c_rstd", [P, 1])
        mx = m.sb("c_mx", [P, H])
        sums = m.sb("c_sums", [P, H])
        rsum = m.sb("c_rsum", [P, H])
        scores = m.psum("c_scores", [P, 2, BANK])
        in_bank = m.psum("c_in_bank", [P, BANK])
        y_bank = m.psum("c_y_bank", [P, BANK])
        ring = m.psum("c_ring", [P, SLOTS, BANK])

        PE = Steps(m.sem("c_pe"), ["s0", "s1", "x", "k0", "k1", "q0", "q1", "pt0", "pt1", "pv0", "pv1",
                                  
                                   "v0", "v1", "ot0", "ot1", "y"])
        SC = Steps(m.sem("c_act"), ["exp0", "x", "exp1", "pt0", "pt1", "v0", "v1", "ot0", "ot1"])
        VE = Steps(m.sem("c_dve"), ["stats", "go", "aggr", "norm", "add0", "max0", "sub0", "add1", "max1", "sub1",
                                    "k0", "k1", "q0", "q1", "sum0", "sum1", "recip", "pv0", "pv1", "y1", "y2"])
        PO = Steps(m.sem("c_pool"), ["copy", "r1", "r2"])
        GV = Steps(m.sem("c_gather_dve"), ["sum0", "sum1", "sum2", "sum3", "onehot", "row", "first", "rows"], -2)
        gathered = m.sem("c_gathered")
        rows_seen = m.sem("c_rows_seen")
        pe_free = m.sem("c_pe_free")
        onehot = m.sb("c_onehot", [P, TOP0, E0])
        first = m.sb("c_first", [P, TOP0])
        rows_u = m.sb("c_out_rows", [P, TOP0], mybir.dt.uint32)
        fetched = m.sb("c_fetched", [P, TOP0, D])
        RING = ["k0", "k1", "q0", "q1", "pt0", "pt1", "pv0", "pv1", "v0", "v1", "ot0", "ot1"]
        assert len(RING) % SLOTS == 0
        evac = {n: (VE if n[0] in "kq" or n[:2] == "pv" else SC) for n in RING}

        def slot(n):
            return ring[:, RING.index(n) % SLOTS, :]

        with nc.Block() as block:
            @block.tensor
            def _(pe):
                def body(it, cur, nxt):
                    def free(n):
                        i = RING.index(n) - SLOTS
                        old = RING[i]
                        pe.wait_ge(evac[old].sem, evac[old].at(old, it if i >= 0 else it - 1))

                    def do(names, run, emit):
                        for n in names:
                            if n in RING:
                                free(n)
                            if not run:
                                PE.skip(pe, n, it)
                                continue
                            emit(n).then_inc(PE.sem, 1)

                    def score(n):
                        h2 = int(n[1])
                        r = DH * h2
                        pe.wait_ge(VE.sem, VE.at("q1", it - 1))
                        pe.sem_inc(pe_free, 1)
                        for c in range(CH):
                            for b in range(2):
                                last = pe.matmul(scores[S * b:S * b + S, h2, c * S:c * S + S],
                                                 qT[r:r + DH, c, S * b:S * b + S],
                                                 kT[r:r + DH, c, S * b:S * b + S], start=True, stop=True)
                        return last

                    def t_in(n):
                        pe.wait_ge(VE.sem, VE.at("norm", it))
                        pe.wait_ge(PO.sem, PO.at("copy", it))
                        pe.wait_ge(SC.sem, SC.at("x", it - 1))
                        for j in range(2):
                            last = pe.transpose(in_bank[:, j * P:j * P + P], rows[:, j, :], g["ident"][:, :])
                        return last

                    def proj(n):
                        if n == "k0":
                            pe.wait_ge(SC.sem, SC.at("x", it))
                        wt, src = (g["wk1"], 1) if n[0] == "k" else (g["wq1"], 0)
                        for j in range(4):
                            c = 4 * int(n[1]) + j
                            last = pe.matmul(slot(n)[:, j * P:j * P + P],
                                             wt[:, 2 * c:2 * c + 2, :].rearrange("p h e -> p (h e)"),
                                             inT[:, src, :], start=True, stop=True)
                        return last

                    def proj_v(n):
                        b = int(n[1])
                        for h2 in range(2):
                            last = pe.matmul(slot(n)[S * h2:S * h2 + S, :], inT[:, 1, S * b:S * b + S],
                                             g["wv1"][:, 8 * h2:8 * h2 + 8, :].rearrange("p h e -> p (h e)"),
                                             start=True, stop=True)
                        return last

                    def t_probs(n):
                        if n == "pt0":
                            pe.wait_ge(SC.sem, SC.at("exp1", it))
                        for j in range(4):
                            last = pe.transpose(slot(n)[:, j * P:j * P + P], probs[:, 4 * int(n[2]) + j, :, :].rearrange("p a j -> p (a j)"),
                                                g["ident"][:, :])
                        return last

                    def pv(n):
                        if n == "pv0":
                            pe.wait_ge(SC.sem, SC.at("pt1", it))
                        pe.sem_inc(pe_free, 1)
                        r = S * int(n[2])
                        for c in range(CH):
                            for b in range(2):
                                last = pe.matmul(slot(n)[S * b:S * b + S, c * DH:c * DH + DH],
                                                 probsT[r:r + S, c, S * b:S * b + S],
                                                 v[r:r + S, b, c * DH:c * DH + DH], start=True, stop=True)
                        return last

                    def t_o(n):
                        pe.wait_ge(VE.sem, VE.at(f"pv{n[2]}", it))
                        for j in range(4):
                            k = 4 * int(n[2]) + j
                            last = pe.transpose(slot(n)[:, j * P:j * P + P], o[:, k * P:k * P + P],
                                                g["ident"][:, :])
                        return last

                    def out(n):
                        pe.wait_ge(SC.sem, SC.at("ot1", it))
                        pe.wait_ge(VE.sem, VE.at("y1", it - 1))
                        for k in range(CH):
                            last = pe.matmul(y_bank[:, 0:D], oT[:, k, :], g["wo1"][:, k, :],
                                             start=(k == 0), stop=(k == CH - 1))
                        return last

                    do(["s0", "s1"], cur, score)
                    do(["x"], nxt, t_in)
                    do(["k0", "k1", "q0", "q1"], nxt, proj)
                    do(["pt0", "pt1"], cur, t_probs)
                    do(["pv0", "pv1"], cur, pv)
                    do(["v0", "v1"], nxt, proj_v)
                    do(["ot0", "ot1"], cur, t_o)
                    do(["y"], cur, out)

                run_tiles(nc.tensor, body)

            @block.scalar
            def _(act):
                def body(it, cur, nxt):
                    for n in SC.names:
                        if not (nxt if n[0] in "xv" else cur):
                            SC.skip(act, n, it)
                            continue
                        if n[:3] == "exp":
                            act.wait_ge(VE.sem, VE.at(f"sub{n[3]}", it))
                            p = probs[:, :, int(n[3]), :]
                            act.activation(p, p, ACT.Exp).then_inc(SC.sem, 1)
                            continue
                        act.wait_ge(PE.sem, PE.at(n, it))
                        if n == "x":
                            src, dst = in_bank[:, 0:2 * P], inT[:, :, :].rearrange("p a b -> p (a b)")
                        elif n[0] == "v":
                            src, dst = slot(n), v[:, int(n[1]), :]
                        else:
                            c = 4 * int(n[2])
                            to = probsT if n[:2] == "pt" else oT
                            src, dst = slot(n), to[:, c:c + 4, :].rearrange("p c j -> p (c j)")
                        act.activation(dst, src, ACT.Copy).then_inc(SC.sem, 1)

                run_tiles(nc.scalar, body)

            @block.vector
            def _(dve):
                def body(it, cur, nxt):
                    def skip(names):
                        for n in names:
                            VE.skip(dve, n, it)
                    combine(it, nxt)
                    locate(it, nxt and not (isinstance(it, int) and it + 2 >= TILES))
                    if nxt:
                        dve.bn_stats(stats[:, :], g["x"][:, it + 1, :]).then_inc(VE.sem, 1)
                        dve.wait_ge(VE.sem, VE.at("stats", it))
                        dve.wait_ge(PO.sem, PO.at("r2", it - 1))
                        dve.sem_inc(VE.sem, 1)
                        dve.bn_aggr(mv[:, :], stats[:, :]).then_inc(VE.sem, 1)
                        dve.wait_ge(VE.sem, VE.at("aggr", it))
                        dve.wait_ge(PO.sem, PO.at("r2", it))
                        dve.wait_ge(PE.sem, PE.at("x", it - 1))
                        dve.tensor_scalar(rows[:, 0, :], g["x"][:, it + 1, :], mv[:, 0:1], rstd[:, :],
                                          ALU.subtract, ALU.mult).then_inc(VE.sem, 1)
                    else:
                        skip(["stats", "go", "aggr", "norm"])
                    if cur:
                        for h2 in range(2):
                            s8 = scores[:, h2, :].rearrange("p (c j) -> p c j", j=S)
                            p8 = probs[:, :, h2, :]
                            m8 = mx[:, 8 * h2:8 * h2 + 8]
                            dve.wait_ge(PE.sem, PE.at(f"s{h2}", it))
                            dve.wait_ge(PE.sem, PE.at("pt1", it - 1))
                            dve.tensor_tensor(p8, s8, g["mask1"][:, :].unsqueeze(1).broadcast_to([P, CH, S]),
                                              ALU.add).then_inc(VE.sem, 1)
                            dve.wait_ge(VE.sem, VE.at(f"add{h2}", it))
                            dve.tensor_reduce(m8, p8, AX_X, ALU.max).then_inc(VE.sem, 1)
                            dve.wait_ge(VE.sem, VE.at(f"max{h2}", it))
                            dve.tensor_tensor(p8, p8, m8.unsqueeze(2).broadcast_to([P, CH, S]),
                                              ALU.subtract).then_inc(VE.sem, 1)
                    else:
                        skip(VE.names[4:10])
                    for n in ("k0", "k1", "q0", "q1"):
                        if not nxt:
                            skip([n])
                            continue
                        c = 4 * int(n[1])
                        dst, bias, scale = (kT, BK, 1.0) if n[0] == "k" else (qT, BQ, DH ** -0.5)
                        dve.wait_ge(PE.sem, PE.at(n, it))
                        dve.scalar_tensor_tensor(dst[:, c:c + 4, :], slot(n).rearrange("p (c j) -> p c j", c=4),
                                                 scale, g["wT"][:, bias, c:c + 4].unsqueeze(2).broadcast_to([P, 4, P]),
                                                 ALU.mult, ALU.add).then_inc(VE.sem, 1)
                    if cur:
                        for h2 in range(2):
                            dve.wait_ge(SC.sem, SC.at(f"exp{h2}", it))
                            dve.tensor_reduce(sums[:, 8 * h2:8 * h2 + 8], probs[:, :, h2, :], AX_X,
                                              ALU.add).then_inc(VE.sem, 1)
                        dve.wait_ge(VE.sem, VE.at("sum1", it))
                        dve.reciprocal(rsum[:, :], sums[:, :]).then_inc(VE.sem, 1)
                        dve.wait_ge(VE.sem, VE.at("recip", it))
                        for j in range(2):
                            dve.wait_ge(PE.sem, PE.at(f"pv{j}", it))
                            dve.wait_ge(PE.sem, PE.at(f"ot{j}", it - 1))
                            dve.tensor_tensor(
                                o[:, j * BANK:j * BANK + BANK].rearrange("p (h e) -> p h e", e=DH),
                                slot(f"pv{j}").rearrange("p (h e) -> p h e", e=DH),
                                rsum[:, 8 * j:8 * j + 8].unsqueeze(2).broadcast_to([P, 8, DH]),
                                ALU.mult).then_inc(VE.sem, 1)
                        dve.wait_ge(PE.sem, PE.at("y", it))
                        xt = g["x"][:, it, :]
                        dve.scalar_tensor_tensor(xt, y_bank[:, 0:D], g["tanh_g"][:, 1:2], xt, ALU.mult,
                                                 ALU.add).then_inc(VE.sem, 1)
                        dve.wait_ge(VE.sem, VE.at("y1", it))
                        dve.tensor_tensor(xt, xt, g["out_bias1"][:, :], ALU.add).then_inc(VE.sem, 1)
                    else:
                        skip(VE.names[14:])

                def combine(it, run):
                    if not run:
                        for n in GV.names[:4]:
                            GV.skip(dve, n, it)
                        return
                    xt = g["x"][:, it + 1, :]
                    dve.wait_ge(gathered, (it + 2) * 16 * TOP0)
                    for j in range(TOP0):
                        dve.scalar_tensor_tensor(xt, fetched[:, j, :], g["gates"][:, it + 1, j:j + 1], xt, ALU.mult,
                                                 ALU.add).then_inc(GV.sem, 1)
                        dve.wait_ge(GV.sem, GV.at(f"sum{j}", it))

                def locate(it, run):
                    if not run:
                        for n in GV.names[4:]:
                            GV.skip(dve, n, it)
                        return
                    shape = [P, TOP0, E0]
                    dve.tensor_tensor(onehot[:, :, :], g["expert_id"][:, :].unsqueeze(1).broadcast_to(shape),
                                      g["chosen"][:, it + 2, :].unsqueeze(2).broadcast_to(shape),
                                      ALU.is_equal).then_inc(GV.sem, 1)
                    dve.wait_ge(GV.sem, GV.at("onehot", it))
                    dve.tensor_tensor(onehot[:, :, :], onehot[:, :, :],
                                      g["first_row"][:, :].unsqueeze(1).broadcast_to(shape),
                                      ALU.mult).then_inc(GV.sem, 1)
                    dve.wait_ge(GV.sem, GV.at("row", it))
                    dve.tensor_reduce(first[:, :], onehot[:, :, :], AX_X, ALU.add).then_inc(GV.sem, 1)
                    dve.wait_ge(GV.sem, GV.at("first", it))
                    dve.tensor_tensor(rows_u[:, :], first[:, :], g["position"][:, it + 2, :],
                                      ALU.add).then_inc(GV.sem, 1)

                combine(-2, False)
                locate(-2, True)
                run_tiles(nc.vector, body, apart=2)

            @block.gpsimd
            def _(pool):
                def gather(it):
                    pool.wait_ge(GV.sem, GV.at("rows", it))
                    pool.sem_inc(rows_seen, 1)
                    for j in range(TOP0):
                        pool.indirect_dma_start(fetched[:, j, :], None, g["ys"],
                                                bass.IndirectOffsetOnAxis(rows_u[:, j:j + 1], 0),
                                                bounds_check=SLOTS0 * P - 1).then_inc(gathered, 16)
                gather(-2)

                def body(it, cur, nxt):
                    if nxt and not (isinstance(it, int) and it + 2 >= TILES):
                        gather(it)
                    if not nxt:
                        for n in PO.names:
                            PO.skip(pool, n, it)
                        return
                    pool.wait_ge(PE.sem, PE.at("x", it - 1))
                    pool.tensor_copy(rows[:, 1, :], g["ctx"][:, it + 1, :]).then_inc(PO.sem, 1)
                    pool.wait_ge(VE.sem, VE.at("aggr", it))
                    pool.wait_ge(VE.sem, VE.at("norm", it - 1))
                    pool.tensor_tensor(tmp[:, :], mv[:, 1:2], g["eps"][:, 0:1], ALU.add).then_inc(PO.sem, 1)
                    pool.wait_ge(PO.sem, PO.at("r1", it))
                    pool.tensor_tensor(rstd[:, :], tmp[:, :], g["neg_half"][:, 0:1], ALU.pow).then_inc(PO.sem, 1)

                run_tiles(nc.gpsimd, body, apart=2)


def experts1(nc, m0, g, out):
    with ExitStack() as ctx:
        m = Mem(nc, ctx)
        xfT = m.sb("d_xfT", [P, P])
        xf = m.sb("d_xf", [P, D])
        stats = m.sb("d_stats", [P, 6])
        mv = m.sb("d_mv", [P, 2])
        tmp = m.sb("d_tmp", [P, 1])
        rstd = m.sb("d_rstd", [P, 1])
        th_l = m.sb("d_th_l", [P, E1])
        sc = m.sb("d_scores", [P, E1])
        choice = m.sb("d_choice", [P, E1])
        top = m.sb("d_top", [P, GROUPS1, 8])
        gs = m.sb("d_group_scores", [P, GROUPS1])
        gt = m.sb("d_gt", [P, GROUPS1, GROUPS1])
        eq = m.sb("d_eq", [P, GROUPS1, GROUPS1])
        rank = m.sb("d_rank", [P, GROUPS1])
        gm = m.sb("d_group_mask", [P, GROUPS1])
        masked = m.sb("d_masked", [P, E1])
        top8 = m.sb("d_top8", [P, 8])
        left = m.sb("d_left", [P, E1])
        picked = m.sb("d_picked", [P, E1])
        wsum = m.sb("d_wsum", [P, 4])
        wts = m.sb("d_wts", [P, E1])
        th = m.sb("d_th", [P, 2, BANK])
        a = m.sb("d_a", [P, 2, BANK])
        h = m.sb("d_h", [P, 2, BANK])
        hT = m.sb("d_hT", [P, 2, BANK])
        g_bank = m.psum("d_g_bank", [P, 2, BANK])
        u_bank = m.psum("d_u_bank", [P, 2, BANK])
        t_bank = m.psum("d_t_bank", [P, 2, BANK])
        in_bank = m.psum("d_in_bank", [P, BANK])
        y_bank = m.psum("d_y_bank", [P, BANK])
        stored = m.sem("stored")

        NQ = 5
        WIDTH = [BANK] * 4 + [P]
        PE = Steps(m.sem("d_pe"), ["gu0", "gu1", "t0", "gu2", "t1", "y0", "gu3", "t2", "y1", "gu4", "x", "t3", "y2",
                                   "t4", "y3", "logits", "y4"])
        SC = Steps(m.sem("d_act"), ["th0", "th1", "t0", "th2", "t1", "th3", "t2", "th4", "x", "t3", "t4", "logits"])
        ROUTE = ["sc", "choice", "go_top", "top", "gs", "gt", "eq", "eqtri", "beat", "rank", "gm", "masked",
                 "go_top8", "top8", "go_left", "left",
                 "picked", "w", "wsum", "wsum_eps", "wrec", "wts"]
        VE = Steps(m.sem("d_dve"), ["a0", "b0", "a1", "b1", "a2", "b2", "stats", "go", "aggr", "norm",
                                    "a3", "b3", "a4", "b4", "y"] + ROUTE)
        PO = Steps(m.sem("d_pool"), ["c0", "c1", "c2", "r1", "r2", "c3"])

        with nc.Block() as block:
            @block.tensor
            def _(pe):
                def body(it, cur, nxt):
                    def gate_up(q):
                        if q == 0:
                            pe.wait_ge(SC.sem, SC.at("x", it - 1))
                        pe.wait_ge(VE.sem, VE.at(f"b{q - 2}" if q >= 2 else f"b{q + (2 if q == 1 else 4)}",
                                it if q >= 2 else it - 1))
                        if q < 4:
                            pe.matmul(g_bank[:, q % 2, :], xfT[:, :],
                                      g["wT"][:, GATE + 4 * q:GATE + 4 * q + 4, :].rearrange("p k c -> p (k c)"),
                                      start=True, stop=True)
                            return pe.matmul(u_bank[:, q % 2, :], xfT[:, :],
                                             g["wT"][:, UP + 4 * q:UP + 4 * q + 4, :].rearrange("p k c -> p (k c)"),
                                             start=True, stop=True)
                        pe.matmul(g_bank[:, 0, 0:P], xfT[:, :], g["wT"][:, SHARED, :], start=True, stop=True)
                        return pe.matmul(u_bank[:, 0, 0:P], xfT[:, :], g["wT"][:, SHARED + 1, :],
                                         start=True, stop=True)

                    def turn(q):
                        pe.wait_ge(PO.sem, PO.at(f"c{q}", it)) if q < 4 else pe.wait_ge(VE.sem, VE.at("b4", it))
                        if q >= 2:
                            pe.wait_ge(SC.sem, SC.at(f"t{q - 2}", it))
                        else:
                            pe.wait_ge(SC.sem, SC.at("t4" if q == 0 else "t3", it - 1))
                        for j in range(WIDTH[q] // P):
                            last = pe.transpose(t_bank[:, q % 2, j * P:j * P + P], h[:, q % 2, j * P:j * P + P],
                                                g["ident"][:, :])
                        return last

                    def down(q):
                        pe.wait_ge(SC.sem, SC.at(f"t{q}", it))
                        if q == 0:
                            pe.wait_ge(VE.sem, VE.at("y", it - 1))
                        for j in range(WIDTH[q] // P):
                            k = DOWN + 4 * q + j if q < 4 else SHARED_DOWN
                            last = pe.matmul(y_bank[:, 0:D], hT[:, q % 2, j * P:j * P + P], g["wT"][:, k, :],
                                             start=(q == 0 and j == 0), stop=(q == 4))
                        return last

                    for n in PE.names:
                        if not (nxt if n in ("x", "logits") else cur):
                            PE.skip(pe, n, it)
                            continue
                        if n == "x":
                            pe.wait_ge(VE.sem, VE.at("norm", it))
                            last = pe.transpose(in_bank[:, 0:P], xf[:, :], g["ident"][:, :])
                        elif n == "logits":
                            pe.wait_ge(SC.sem, SC.at("x", it))
                            last = pe.matmul(in_bank[:, P:P + E1], xfT[:, :], g["wT"][:, ROUTER1, 0:E1],
                                             start=True, stop=True)
                        else:
                            last = {"g": gate_up, "t": turn, "y": down}[n[0]](int(n[-1]))
                        last.then_inc(PE.sem, 1)

                run_tiles(nc.tensor, body)

            @block.scalar
            def _(act):
                def body(it, cur, nxt):
                    for n in SC.names:
                        if not (nxt if n in ("x", "logits") else cur):
                            SC.skip(act, n, it)
                            continue
                        q = int(n[-1]) if n[-1].isdigit() else 0
                        if n[:2] == "th":
                            act.wait_ge(PE.sem, PE.at(f"gu{q}", it))
                            if q >= 2:
                                act.wait_ge(VE.sem, VE.at(f"a{q - 2}", it))
                            else:
                                act.wait_ge(VE.sem, VE.at("a4" if q == 0 else "a3", it - 1))
                            ins = act.activation(th[:, q % 2, 0:WIDTH[q]], g_bank[:, q % 2, 0:WIDTH[q]], ACT.Tanh,
                                                 scale=0.5)
                        elif n == "x":
                            act.wait_ge(PE.sem, PE.at("x", it))
                            ins = act.activation(xfT[:, :], in_bank[:, 0:P], ACT.Copy)
                        elif n == "logits":
                            act.wait_ge(PE.sem, PE.at("logits", it))
                            act.wait_ge(VE.sem, VE.at("sc", it - 1))
                            ins = act.activation(th_l[:, :], in_bank[:, P:P + E1], ACT.Tanh, scale=0.5)
                        else:
                            act.wait_ge(PE.sem, PE.at(n, it))
                            ins = act.activation(hT[:, q % 2, 0:WIDTH[q]], t_bank[:, q % 2, 0:WIDTH[q]], ACT.Copy)
                            
                        ins.then_inc(SC.sem, 1)

                run_tiles(nc.scalar, body)

            @block.vector
            def _(dve):
                def body(it, cur, nxt):
                    def act_out(q):
                        if not cur:
                            VE.skip(dve, f"a{q}", it)
                            VE.skip(dve, f"b{q}", it)
                            return
                        wd = WIDTH[q]
                        ah = a[:, q % 2, 0:wd]
                        dve.wait_ge(SC.sem, SC.at(f"th{q}", it))
                        if q < 2:
                            dve.wait_ge(PO.sem, PO.at("c2" if q == 0 else "c3", it - 1))
                        elif q < 4:
                            dve.wait_ge(PO.sem, PO.at(f"c{q - 2}", it))
                        dve.scalar_tensor_tensor(ah, th[:, q % 2, 0:wd], 1.0, g_bank[:, q % 2, 0:wd], ALU.add,
                                                 ALU.mult).then_inc(VE.sem, 1)
                        dve.wait_ge(VE.sem, VE.at(f"a{q}", it))
                        if q == 4:
                            dve.wait_ge(PE.sem, PE.at("t2", it))
                            dve.wait_ge(PO.sem, PO.at("c2", it))
                        dst = ah if q < 4 else h[:, 0, 0:wd]
                        dve.scalar_tensor_tensor(dst, ah, 0.5, u_bank[:, q % 2, 0:wd], ALU.mult,
                                                 ALU.mult).then_inc(VE.sem, 1)

                    act_out(0)
                    act_out(1)
                    act_out(2)
                    if nxt:
                        dve.bn_stats(stats[:, :], g["x"][:, it + 1, :]).then_inc(VE.sem, 1)
                        dve.wait_ge(VE.sem, VE.at("stats", it))
                        dve.wait_ge(PO.sem, PO.at("r2", it - 1))
                        dve.sem_inc(VE.sem, 1)
                        dve.bn_aggr(mv[:, :], stats[:, :]).then_inc(VE.sem, 1)
                        dve.wait_ge(VE.sem, VE.at("aggr", it))
                        dve.wait_ge(PO.sem, PO.at("r2", it))
                        dve.wait_ge(PE.sem, PE.at("x", it - 1))
                        dve.tensor_scalar(xf[:, :], g["x"][:, it + 1, :], mv[:, 0:1], rstd[:, :], ALU.subtract,
                                          ALU.mult).then_inc(VE.sem, 1)
                    else:
                        for n in ("stats", "go", "aggr", "norm"):
                            VE.skip(dve, n, it)
                    act_out(3)
                    act_out(4)
                    if cur:
                        dve.wait_ge(PE.sem, PE.at("y4", it))
                        xt = g["x"][:, it, :]
                        dve.scalar_tensor_tensor(xt, y_bank[:, 0:D], g["tanh_g"][:, 3:4], xt, ALU.mult,
                                                 ALU.add).then_inc(VE.sem, 1)
                    else:
                        VE.skip(dve, "y", it)
                    if not nxt:
                        for n in ROUTE:
                            VE.skip(dve, n, it)
                        return

                    def chain(name, ins):
                        ins.then_inc(VE.sem, 1)
                        dve.wait_ge(VE.sem, VE.at(name, it))
                    dve.wait_ge(SC.sem, SC.at("logits", it))
                    chain("sc", dve.tensor_scalar(sc[:, :], th_l[:, :], 0.5, 0.5, ALU.mult, ALU.add))
                    def seen(name):
                        dve.sem_inc(VE.sem, 1)
                    chain("choice", dve.tensor_tensor(choice[:, :], sc[:, :], g["gate_bias"][:, :], ALU.add))
                    seen("go_top")
                    for n in range(GROUPS1):
                        last = dve.max(top[:, n, :], choice[:, n * GSIZE1:n * GSIZE1 + GSIZE1])
                    chain("top", last)
                    chain("gs", dve.tensor_tensor(gs[:, :], top[:, :, 0], top[:, :, 1], ALU.add))
                    mine = gs[:, :].unsqueeze(2).broadcast_to([P, GROUPS1, GROUPS1])
                    other = gs[:, :].unsqueeze(1).broadcast_to([P, GROUPS1, GROUPS1])
                    chain("gt", dve.tensor_tensor(gt[:, :, :], other, mine, ALU.is_gt))
                    chain("eq", dve.tensor_tensor(eq[:, :, :], other, mine, ALU.is_equal))
                    chain("eqtri", dve.tensor_tensor(eq[:, :, :], eq[:, :, :], g["tri"][:, :, :], ALU.mult))
                    chain("beat", dve.tensor_tensor(gt[:, :, :], gt[:, :, :], eq[:, :, :], ALU.add))
                    chain("rank", dve.tensor_reduce(rank[:, :], gt[:, :, :], AX_X, ALU.add))
                    chain("gm", dve.tensor_scalar(gm[:, :], rank[:, :], 1.5, None, ALU.is_lt))
                    chain("masked", dve.tensor_tensor(
                        masked[:, :].rearrange("p (g e) -> p g e", g=GROUPS1),
                        choice[:, :].rearrange("p (g e) -> p g e", g=GROUPS1),
                        gm[:, :].unsqueeze(2).broadcast_to([P, GROUPS1, GSIZE1]), ALU.mult))
                    seen("go_top8")
                    chain("top8", dve.max(top8[:, :], masked[:, :]))
                    seen("go_left")
                    chain("left", dve.match_replace(left[:, :], top8[:, :], masked[:, :], MASKED))
                    chain("picked", dve.tensor_tensor(picked[:, :], masked[:, :], left[:, :], ALU.not_equal))
                    chain("w", dve.tensor_tensor(picked[:, :], sc[:, :], picked[:, :], ALU.mult))
                    chain("wsum", dve.tensor_reduce(wsum[:, 0:1], picked[:, :], AX_X, ALU.add))
                    chain("wsum_eps", dve.tensor_scalar(wsum[:, 1:2], wsum[:, 0:1], 1e-20, None, ALU.add))
                    chain("wrec", dve.reciprocal(wsum[:, 2:3], wsum[:, 1:2]))
                    dve.wait_ge(PO.sem, PO.at("c3", it))
                    dve.tensor_scalar(wts[:, :], picked[:, :], wsum[:, 2:3], ROUTED_SCALING, ALU.mult,
                                      ALU.mult).then_inc(VE.sem, 1)

                run_tiles(nc.vector, body)

            @block.gpsimd
            def _(pool):
                def body(it, cur, nxt):
                    def weigh(q):
                        if not cur:
                            PO.skip(pool, f"c{q}", it)
                            return
                        if q == 0:
                            pool.wait_ge(VE.sem, VE.at("wts", it - 1))
                            pool.wait_ge(PE.sem, PE.at("t4", it - 1))
                        else:
                            pool.wait_ge(PE.sem, PE.at("t3", it - 1)) if q == 1 else pool.wait_ge(PE.sem, PE.at(f"t{q - 2}", it))
                        pool.wait_ge(VE.sem, VE.at(f"b{q}", it))
                        pool.tensor_tensor(h[:, q % 2, :].rearrange("p (e i) -> p e i", e=8),
                                           a[:, q % 2, :].rearrange("p (e i) -> p e i", e=8),
                                           wts[:, 8 * q:8 * q + 8].unsqueeze(2).broadcast_to([P, 8, I1]),
                                           ALU.mult).then_inc(PO.sem, 1)
                    weigh(0)
                    weigh(1)
                    weigh(2)
                    if nxt:
                        pool.wait_ge(VE.sem, VE.at("aggr", it))
                        pool.tensor_tensor(tmp[:, :], mv[:, 1:2], g["eps"][:, 0:1], ALU.add).then_inc(PO.sem, 1)
                        pool.wait_ge(PO.sem, PO.at("r1", it))
                        pool.wait_ge(VE.sem, VE.at("norm", it - 1))
                        pool.tensor_tensor(rstd[:, :], tmp[:, :], g["neg_half"][:, 0:1], ALU.pow).then_inc(PO.sem, 1)
                    else:
                        PO.skip(pool, "r1", it)
                        PO.skip(pool, "r2", it)
                    weigh(3)

                run_tiles(nc.gpsimd, body)

            @block.sync
            def _(sp):
                out_v = out.rearrange("(t b) s d -> t (b s) d", b=2)
                with nc.sync.Fori(0, TILES) as it:
                    sp.wait_ge(VE.sem, VE.at("y", it))
                    sp.dma_start(out_v[it], g["x"][:, it, :]).then_inc(stored, 16)
                sp.wait_ge(stored, 16 * TILES)


STAGES = 15


def flamingo(nc, w, out):
    with ExitStack() as ctx:
        m = Mem(nc, ctx)
        g = setup(nc, m, w)
        finish_weights(nc, m, g, w)
        if STAGES & 1:
            attention0(nc, m, g)
        if STAGES & 2:
            route_alone(nc, m, g)
            experts0(nc, m, g, w)
        if STAGES & 4:
            attention1(nc, m, g)
        if STAGES & 8:
            experts1(nc, m, g, out)
        else:
            write_out(nc, m, g, out)


def write_out(nc, m, g, out):
    stored = m.sem("stored")
    with nc.Block() as block:
        @block.sync
        def _(sp):
            sp.dma_start(out.rearrange("(t b) s d -> (b s) t d", b=2), g["x"][:, :, :]).then_inc(stored, 16)
            sp.wait_ge(stored, 16)


_OUTS = [((B, S, D), 'float32')]


def kernel(**inputs):
    import numpy as _np
    import concourse.bacc as _bacc
    from concourse.bass_utils import run_bass_kernel_spmd as _run

    nc = _bacc.Bacc("TRN2", target_bir_lowering=False, num_devices=1)
    arrays, w = {}, {}
    for name, value in inputs.items():
        a = _np.ascontiguousarray(value)
        arrays[f"in_{name}_dram"] = a
        w[name] = nc.dram_tensor(f"in_{name}_dram", a.shape, mybir.dt.from_np(a.dtype), kind="ExternalInput").ap()
    shape, dtype = _OUTS[0]
    out = nc.dram_tensor("out_0_dram", shape, mybir.dt.from_np(_np.dtype(dtype)), kind="ExternalOutput").ap()
    flamingo(nc, w, out)
    r = _run(nc, [arrays], core_ids=[0])
    return r.results[0]["out_0_dram"]
```

```python
from contextlib import ExitStack

import concourse.bass as bass
from concourse import mybir

ALU = mybir.AluOpType
ACT = mybir.ActivationFunctionType
F32 = mybir.dt.float32
BF16 = mybir.dt.bfloat16
AX_X = mybir.AxisListType.X

P = 128
B, S, D = 64, 64, 128
TILES = B * S // P
H, DH = 16, 64
INNER = H * DH
CH = INNER // P
E0, TOP0 = 64, 4
E1, I1 = 32, 64
GROUPS1, GSIZE1 = 4, 8
ROUTED_SCALING = 2.5
LN_EPS = 1e-5
MASK1 = -1e10
GATE, UP, DOWN, SHARED, SHARED_DOWN, ROUTER1, ROUTER0 = 0, 16, 32, 48, 50, 51, 52
BQ, BK, BV = 53, 54, 55
BLOCKS = 56
MASKED = -1e30
REGION = B * S + P
SLOTS0 = 192
BATCH = 4
BATCHES = SLOTS0 // BATCH
BANK = 512
SLOTS = 4


class Steps:

    def __init__(self, sem, names, first=-1):
        self.sem, self.names, self.first = sem, names, first

    def at(self, name, it):
        if isinstance(it, int) and it < self.first:
            return 0
        return (it - self.first) * len(self.names) + self.names.index(name) + 1

    def skip(self, eng, name, it):
        if self.at(name, it) > 1:
            eng.wait_ge(self.sem, self.at(name, it) - 1)
        eng.sem_inc(self.sem, 1)


class Mem:

    def __init__(self, nc, ctx):
        self.nc, self.ctx = nc, ctx

    def sb(self, name, shape, dt=F32):
        return self.ctx.enter_context(self.nc.sbuf_tensor(name, shape, dt))

    def psum(self, name, shape, dt=F32):
        return self.ctx.enter_context(self.nc.psum_tensor(name, shape, dt))

    def sem(self, name):
        return self.ctx.enter_context(self.nc.semaphore(name))


def run_tiles(eng_loop, body, n=TILES, apart=1):
    body(-1, False, True)
    with eng_loop.Fori(0, n - apart) as it:
        body(it, True, True)
    for it in range(n - apart, n):
        body(it, True, it + 1 < n)


def setup(nc, m, w):
    g = {}
    g["x"] = m.sb("x_sb", [P, TILES, D])
    g["ctx"] = m.sb("ctx_sb", [P, TILES, D])
    g["ident"] = m.sb("ident", [P, P])
    g["neg_half"] = m.sb("neg_half", [P, 2])
    g["mask0"] = m.sb("mask0", [P, TILES, 2, S], BF16)
    g["eps"] = m.sb("eps", [P, 2])
    g["tri"] = m.sb("tri", [P, GROUPS1, GROUPS1])
    g["before"] = m.sb("before", [P, P], BF16)
    g["ones"] = m.sb("ones", [P, P], BF16)
    g["zeros"] = m.sb("zeros", [P, D])
    g["expert_id"] = m.sb("expert_id", [P, E0])
    g["slot_id"] = m.sb("slot_id", [P, 2])
    g["starts"] = m.sb("starts", [P, TILES])
    g["base"] = m.sb("base", [P, E0])
    g["chosen"] = m.sb("chosen", [P, TILES, TOP0])
    g["position"] = m.sb("position", [P, TILES, TOP0])
    g["gates"] = m.sb("gates", [P, TILES, TOP0])
    g["first_row"] = m.sb("first_row", [P, E0])
    g["out_rows"] = m.sb("out_rows", [P, TILES, TOP0], mybir.dt.uint32)
    ids = m.sb("ids", [P, E0 + 2 + TILES], mybir.dt.int32)
    g["xs"] = nc.dram_tensor("expert_tokens", (E0 * REGION, D), F32).ap()
    g["ys"] = nc.dram_tensor("expert_outputs", (SLOTS0 * P, D), F32).ap()
    s_ids = m.sem("ids_made")
    g["tanh_g"] = m.sb("tanh_g", [P, 4])
    g["cols"] = m.sb("cols", [P, 4])
    g["wq0"] = m.sb("wq0", [P, INNER])
    g["wkv0"] = m.sb("wkv0", [P, 2 * INNER])
    g["wout0"] = m.sb("wout0", [P, CH, D])
    g["gain_o"] = m.sb("gain_o", [P, D])
    g["bias_o"] = m.sb("bias_o", [P, D])
    ident_one = m.sb("ident_one", [P, P])
    mask_raw = m.sb("mask_raw", [1, TILES * 2 * S], mybir.dt.uint8)
    g["ln_mv"] = m.sb("ln_mv", [P, 2, TILES, 2])
    g["ln_rstd"] = m.sb("ln_rstd", [P, 2, TILES, 1])
    g["wq1"] = m.sb("wq1", [P, H, DH])
    g["wk1"] = m.sb("wk1", [P, H, DH])
    g["wv1"] = m.sb("wv1", [P, H, DH])
    g["wo1"] = m.sb("wo1", [P, CH, D])
    g["out_bias1"] = m.sb("out_bias1", [P, D])
    g["mask1"] = m.sb("mask1", [P, S])
    g["gate_bias"] = m.sb("gate_bias", [P, E1])
    g["wT"] = m.sb("wT", [P, BLOCKS, P])
    g["loads"] = m.sem("loads")
    g["loads1"] = m.sem("loads1")
    ready = m.sem("ready")
    s_pool = m.sem("setup_pool")
    s_dve = m.sem("setup_dve")
    x_v = w["x"].rearrange("(t b) s d -> (b s) t d", b=2)
    ctx_v = w["ctx_1024"].rearrange("(t b) s d -> (b s) t d", b=2)
    n_small = [0]
    with nc.Block() as block:
        @block.sync
        def _(sp):
            def load(dst, src):
                sp.dma_start(dst, src).then_inc(g["loads"], 16)
                n_small[0] += 16
            load(mask_raw[:, :], w["mask_BxS2_bk0"].rearrange("b j -> (b j)").unsqueeze(0))
            load(g["tanh_g"][:, 0:2], w["g_xattn"].partition_broadcast(P))
            load(g["tanh_g"][:, 2:4], w["g_ffn"].partition_broadcast(P))
            for n, name in enumerate(("ln_x_g", "ln_x_b", "ln_l_g", "ln_l_b")):
                load(g["cols"][:, n:n + 1], w["L0_xattn_" + name].unsqueeze(1))
            load(g["gain_o"][:, :], w["L0_xattn_ln_o_g"].partition_broadcast(P))
            load(g["bias_o"][:, :], w["L0_xattn_ln_o_b"].partition_broadcast(P))
            load(g["ctx"][:, :, :], ctx_v)
            load(g["x"][:, :, :], x_v)
            load(g["wq0"][:, :], w["L0_xattn_Wq"])
            load(g["wkv0"][:, :], w["L0_xattn_Wkv"])
            load(g["wout0"][:, :, :], w["L0_xattn_Wout"].rearrange("(c p) o -> p c o", p=P))
            n = 0
            wo_v = w["L1_xattn_Wo"].rearrange("(e c p) o -> p e c o", c=CH, p=2)
            late = [(g["wq1"][:, :, :], w["L1_xattn_Wq"].rearrange("h d e -> d h e")),
                    (g["wk1"][:, :, :], w["L1_xattn_Wk"].rearrange("h d e -> d h e")),
                    (g["wv1"][:, :, :], w["L1_xattn_Wv"].rearrange("h d e -> d h e")),
                    (g["out_bias1"][:, :], w["L1_xattn_bo"].partition_broadcast(P)),
                    (g["gate_bias"][:, :], w["L1_ffn_gate_bias"].partition_broadcast(P))]
            for p in range(2):
                late.append((g["mask1"][p:P:2, :], w["mask_SxS2_ff1"]))
                late.append((g["wo1"][DH * p:DH * p + DH, :, :], wo_v[p]))
            for dst, src in late:
                sp.dma_start(dst, src).then_inc(g["loads1"], 16)
            g["n_late"] = 16 * len(late)

        @block.gpsimd
        def _(pool):
            pool.memset(g["neg_half"][:, :], -0.5)
            pool.memset(g["eps"][:, :], LN_EPS)
            pool.memset(ident_one[:, :], 1.0).then_inc(s_pool, 1)
            pool.wait_ge(s_pool, 1)
            pool.affine_select(out=g["ident"][:, :], in_=ident_one[:, :], compare_op=ALU.is_equal, fill=0.0,
                               base=0, pattern=[[-1, P]], channel_multiplier=1).then_inc(s_pool, 1)
            pool.affine_select(out=g["before"][:, :], in_=ident_one[:, :], compare_op=ALU.is_gt, fill=0.0,
                               base=0, pattern=[[1, P]], channel_multiplier=-1)
            pool.iota(ids[:, 0:E0], [[1, E0]], 0, 0)
            pool.iota(ids[:, E0:E0 + 2], [[P, 2]], 0, 1)
            pool.iota(ids[:, E0 + 2:], [[P, TILES]], 0, 0).then_inc(s_ids, 1)
            pool.affine_select(out=g["tri"][:, :, :], in_=ident_one[:, 0:16].rearrange("p (a b) -> p a b", a=4),
                               compare_op=ALU.is_gt, fill=0.0, base=0, pattern=[[1, 4], [-1, 4]],
                               channel_multiplier=0)

        @block.scalar
        def _(act):
            act.wait_ge(g["loads"], n_small[0])
            act.activation(g["tanh_g"][:, :], g["tanh_g"][:, :], ACT.Tanh).then_inc(ready, 1)

        @block.vector
        def _(dve):
            dve.memset(g["mask0"][:, :, :], 0.0).then_inc(s_dve, 1)
            dve.memset(g["ones"][:, :], 1.0)
            dve.memset(g["zeros"][:, :], 0.0)
            dve.memset(g["base"][:, :], 0.0)
            dve.wait_ge(s_ids, 1)
            dve.tensor_copy(g["expert_id"][:, :], ids[:, 0:E0])
            dve.tensor_copy(g["slot_id"][:, :], ids[:, E0:E0 + 2])
            dve.tensor_copy(g["starts"][:, :], ids[:, E0 + 2:])
            dve.wait_ge(g["loads"], n_small[0])
            dve.wait_ge(s_dve, 1)
            dve.tensor_scalar(g["mask0"][0:1, :, :, :].rearrange("p t b j -> p (t b j)"), mask_raw[:, :], -MASKED, MASKED, ALU.mult, ALU.add)
            dve.wait_ge(ready, 1)
            dve.tensor_scalar(g["gain_o"][:, :], g["gain_o"][:, :], g["tanh_g"][:, 0:1], None, ALU.mult)
            dve.tensor_scalar(g["bias_o"][:, :], g["bias_o"][:, :], g["tanh_g"][:, 0:1], None,
                              ALU.mult).then_inc(s_dve, 1)
    return g


class Route:

    def __init__(self, nc, m, g, bank):
        self.nc, self.g, self.bank = nc, g, bank
        self.xf = m.sb("r_xf", [P, D])
        self.xfT = m.sb("r_xfT", [P, P])
        self.stats = m.sb("r_stats", [P, 6])
        self.mv = m.sb("r_mv", [P, 2])
        self.tmp = m.sb("r_tmp", [P, 1])
        self.rstd = m.sb("r_rstd", [P, 1])
        self.th = m.sb("r_th", [P, E0])
        self.sc = m.sb("r_scores", [P, E0])
        self.top8 = m.sb("r_top8", [P, 8])
        self.index8 = m.sb("r_index8", [P, 8], mybir.dt.uint32)
        self.onehot = m.sb("r_onehot", [P, TOP0, E0])
        self.sent = m.sb("r_sent", [P, E0], BF16)
        self.pos = m.sb("r_pos", [P, E0])
        self.at = m.sb("r_at", [P, TOP0, E0])
        self.rows = m.sb("r_rows", [P, TOP0], mybir.dt.uint32)
        self.scattered = m.sem("scattered")
        self.PE = Steps(m.sem("r_pe"), ["x", "logits", "rank"], 0)
        self.SC = Steps(m.sem("r_act"), ["x", "logits"], 0)
        self.VE = Steps(m.sem("r_dve"), ["stats", "go", "aggr", "norm", "sc", "go_top", "top", "go_index", "index",
                                         "chosen", "onehot", "sent", "pos", "base", "at", "position", "rows"], 0)
        self.PO = Steps(m.sem("r_pool"), ["r1", "r2"], 0)
        self.rows_seen = m.sem("r_rows_seen")

    def on_tensor(self, pe, it, part):
        g, PE = self.g, self.PE
        if part == 0:
            pe.wait_ge(self.VE.sem, self.VE.at("norm", it))
            pe.wait_ge(self.SC.sem, self.SC.at("logits", it - 1))
            pe.transpose(self.bank[:, 0:P], self.xf[:, :], g["ident"][:, :]).then_inc(PE.sem, 1)
        elif part == 1:
            pe.wait_ge(self.SC.sem, self.SC.at("x", it))
            pe.matmul(self.bank[:, P:P + E0], self.xfT[:, :], g["wT"][:, ROUTER0, 0:E0], start=True,
                      stop=True).then_inc(PE.sem, 1)
        else:
            pe.wait_ge(self.VE.sem, self.VE.at("sent", it))
            pe.wait_ge(self.SC.sem, self.SC.at("logits", it))
            pe.wait_ge(self.VE.sem, self.VE.at("base", it - 1))
            pe.matmul(self.bank[:, P + E0:P + 2 * E0], g["before"][:, :], self.sent[:, :], start=True, stop=True)
            pe.matmul(self.bank[:, P + 2 * E0:P + 3 * E0], g["ones"][:, :], self.sent[:, :], start=True,
                      stop=True).then_inc(PE.sem, 1)

    def on_scalar(self, act, it, part):
        if part == 0:
            act.wait_ge(self.PE.sem, self.PE.at("x", it))
            act.activation(self.xfT[:, :], self.bank[:, 0:P], ACT.Copy).then_inc(self.SC.sem, 1)
            return
        act.wait_ge(self.PE.sem, self.PE.at("logits", it))
        act.wait_ge(self.VE.sem, self.VE.at("sc", it - 1))
        act.activation(self.th[:, :], self.bank[:, P:P + E0], ACT.Tanh, scale=0.5).then_inc(self.SC.sem, 1)

    def on_vector(self, dve, it, part):
        g, VE = self.g, self.VE
        xt = g["x"][:, it, :]

        def chain(name, ins):
            ins.then_inc(VE.sem, 1)
            dve.wait_ge(VE.sem, VE.at(name, it))

        def seen():
            dve.sem_inc(VE.sem, 1)
        if part == 0:
            chain("stats", dve.bn_stats(self.stats[:, :], xt))
            dve.wait_ge(self.PO.sem, self.PO.at("r2", it - 1))
            seen()
            dve.bn_aggr(self.mv[:, :], self.stats[:, :]).then_inc(VE.sem, 1)
        elif part == 1:
            dve.wait_ge(VE.sem, VE.at("aggr", it))
            dve.wait_ge(self.PO.sem, self.PO.at("r2", it))
            dve.wait_ge(self.PE.sem, self.PE.at("x", it - 1))
            if not (isinstance(it, int) and it == 0):
                dve.wait_ge(self.scattered, 16 * TOP0 * it)
            dve.tensor_scalar(self.xf[:, :], xt, self.mv[:, 0:1], self.rstd[:, :], ALU.subtract,
                              ALU.mult).then_inc(VE.sem, 1)
        elif part == 2:
            dve.wait_ge(self.SC.sem, self.SC.at("logits", it))
            chain("sc", dve.tensor_scalar(self.sc[:, :], self.th[:, :], 0.5, 0.5, ALU.mult, ALU.add))
            seen()
            chain("top", dve.max(self.top8[:, :], self.sc[:, :]))
            seen()
            dve.max_index(self.index8[:, :], self.top8[:, :], self.sc[:, :]).then_inc(VE.sem, 1)
            dve.tensor_scalar(g["gates"][:, it, :], self.top8[:, 0:TOP0], g["tanh_g"][:, 2:3], None, ALU.mult)
            dve.wait_ge(VE.sem, VE.at("index", it))
            chain("chosen", dve.tensor_copy(g["chosen"][:, it, :], self.index8[:, 0:TOP0]))
            ids = g["expert_id"][:, :].unsqueeze(1).broadcast_to([P, TOP0, E0])
            chain("onehot", dve.tensor_tensor(
                self.onehot[:, :, :], ids, g["chosen"][:, it, :].unsqueeze(2).broadcast_to([P, TOP0, E0]),
                ALU.is_equal))
            with self.nc.allow_low_precision("zeros and ones"):
                dve.tensor_reduce(self.sent[:, :], self.onehot[:, :, :].rearrange("p j e -> p e j"), AX_X,
                                  ALU.add).then_inc(VE.sem, 1)
        else:
            dve.wait_ge(self.PE.sem, self.PE.at("rank", it))
            chain("pos", dve.tensor_tensor(self.pos[:, :], self.bank[:, P + E0:P + 2 * E0], g["base"][:, :],
                                           ALU.add))
            dve.tensor_tensor(g["base"][:, :], self.bank[:, P + 2 * E0:P + 3 * E0], g["base"][:, :],
                              ALU.add).then_inc(VE.sem, 1)
            chain("at", dve.tensor_tensor(self.at[:, :, :], self.onehot[:, :, :],
                                          self.pos[:, :].unsqueeze(1).broadcast_to([P, TOP0, E0]), ALU.mult))
            chain("position", dve.tensor_reduce(g["position"][:, it, :], self.at[:, :, :], AX_X, ALU.add))
            dve.scalar_tensor_tensor(self.rows[:, :], g["chosen"][:, it, :], float(REGION),
                                     g["position"][:, it, :], ALU.mult, ALU.add).then_inc(VE.sem, 1)

    def on_gpsimd(self, pool, it, part):
        g, PO = self.g, self.PO
        if part == 0:
            pool.wait_ge(self.VE.sem, self.VE.at("aggr", it))
            pool.tensor_tensor(self.tmp[:, :], self.mv[:, 1:2], g["eps"][:, 0:1], ALU.add).then_inc(PO.sem, 1)
            pool.wait_ge(PO.sem, PO.at("r1", it))
            pool.wait_ge(self.VE.sem, self.VE.at("norm", it - 1))
            pool.tensor_tensor(self.rstd[:, :], self.tmp[:, :], g["neg_half"][:, 0:1], ALU.pow).then_inc(PO.sem, 1)
        else:
            pool.wait_ge(self.VE.sem, self.VE.at("rows", it))
            pool.sem_inc(self.rows_seen, 1)
            for j in range(TOP0):
                pool.indirect_dma_start(g["xs"], bass.IndirectOffsetOnAxis(self.rows[:, j:j + 1], 0), self.xf[:, :],
                                        None, bounds_check=E0 * REGION - 1).then_inc(self.scattered, 16)


def attention0(nc, m0, g):
    with ExitStack() as ctx:
        m = Mem(nc, ctx)
        kvT = m.sb("a_kvT", [P, 2, 2 * S])
        kT = m.sb("a_kT", [P, CH, 2, 2 * S])
        qT = m.sb("a_qT", [P, CH, 2, 2, S])
        v = m.sb("a_v", [P, 2, INNER])
        probs = m.sb("a_probs", [P, CH, 2, P])
        probsT = m.sb("a_probsT", [P, CH, 2, P])
        oT = m.sb("a_oT", [P, CH, P])
        normed = m.sb("a_normed", [P, 2, D])
        y_raw = m.sb("a_y_raw", [P, D])
        y = m.sb("a_y", [P, D])
        gy = m.sb("a_gy", [P, D])
        stats = m.sb("a_stats", [P, 6])
        mv = m.sb("a_mv", [P, 2])
        tmp = m.sb("a_tmp", [P, 1])
        rstd = m.sb("a_rstd", [P, 1])
        mx = m.sb("a_mx", [P, H])
        sums = m.sb("a_sums", [P, H])
        rsum = m.sb("a_rsum", [P, H])
        cleared = m.sem("a_qT_cleared")
        scores = m.psum("a_scores", [P, 4, BANK])
        ring = m.psum("a_ring", [P, 3, BANK])
        route = Route(nc, m, g, m.psum("r_bank", [P, BANK]))

        PE = Steps(m.sem("a_pe"), ["s0", "s1", "s2", "s3", "pv0", "pv1", "v0", "y", "v1", "v2", "v3", "x",
                                   "pt0", "pt1", "k0", "k1", "k2", "k3", "q0", "q1", "pt2", "pt3"])
        SC = Steps(m.sem("a_act"), ["exp0", "exp1", "exp2", "pv0", "pv1", "exp3", "v0", "y", "v1", "v2", "v3", "x",
                                    "pt0", "pt1", "k0", "k1", "k2", "k3", "q0", "q1", "pt2", "pt3"])
        VE = Steps(m.sem("a_dve"), ["max0", "max1", "sub0", "max2", "sub1", "max3", "sub2", "sum0", "sub3",
                                    "norm", "sum1", "sum2", "sum3", "recip", "scale0", "scale1", "scale2", "scale3",
                                    "ystats", "go", "yaggr", "ynorm"])
        PO = Steps(m.sem("a_pool"), ["y1", "y2", "g1", "g2", "x1"])
        RING = PE.names[4:]
        RSLOTS = 3
        assert len(RING) % RSLOTS == 0

        def slot(n):
            return ring[:, RING.index(n) % RSLOTS, :]

        def runs(n, it):
            if not isinstance(it, int):
                return True
            tile = it + 1 if n[0] in "xkq" or n == "norm" else it - 1 if n[0] == "y" or n[:2] == "pv" else it
            return 0 <= tile < TILES

        def routes(tile):
            return not isinstance(tile, int) or 0 <= tile < TILES

        def over_tiles(eng, body):
            for it in range(-1, 4):
                body(it)
            with eng.Fori(4, TILES - 1) as it:
                body(it)
            for it in range(TILES - 1, TILES + 3):
                body(it)

        with nc.Block() as block:
            @block.tensor
            def _(pe):
                def body(it):
                    def score(n):
                        q = int(n[1])
                        if q == 0:
                            pe.wait_ge(SC.sem, SC.at("q1", it - 1))
                        pe.wait_ge(VE.sem, VE.at(f"sub{q}", it - 1))
                        for k in range(4):
                            c, b = 2 * q + k // 2, k % 2
                            pe.matmul(scores[:, q, k * P:k * P + P], qT[:, c, b, :, :].rearrange("p h s -> p (h s)"),
                                      kT[:, c, b, :], start=(k == 0), stop=False, skip_group_check=True)
                        return pe.matmul(scores[:, q, :].rearrange("p (c b j) -> p c b j", c=2, b=2)[:, :, :, 0:S],
                                         g["ones"][:, :],
                                         g["mask0"][:, it, :, :].unsqueeze(1).broadcast_to([P, 2, 2, S]),
                                         start=False, stop=True, skip_group_check=True)

                    def pv(n):
                        if n == "pv0":
                            pe.wait_ge(SC.sem, SC.at("pt3", it - 1))
                        for k in range(4):
                            c = 4 * int(n[2]) + k
                            for b in range(2):
                                for h2 in range(2):
                                    last = pe.matmul(slot(n)[S * h2:S * h2 + S, k * P + S * b:k * P + S * b + S],
                                                     v[:, b, c * P + S * h2:c * P + S * h2 + S],
                                                     probsT[:, c, b, S * h2:S * h2 + S], start=True, stop=True)
                        return last

                    def proj_v(n):
                        b, half = int(n[1]) // 2, int(n[1]) % 2
                        at = INNER + half * BANK
                        return pe.matmul(slot(n), kvT[:, b, :], g["wkv0"][:, at:at + BANK], start=True, stop=True)

                    def out(n):
                        pe.wait_ge(SC.sem, SC.at("pv1", it))
                        for c in range(CH):
                            last = pe.matmul(slot(n)[:, 0:D], oT[:, c, :], g["wout0"][:, c, :],
                                             start=(c == 0), stop=(c == CH - 1))
                        return last

                    def t_in(n):
                        pe.wait_ge(VE.sem, VE.at("norm", it))
                        for j in range(2):
                            last = pe.transpose(slot(n)[:, j * P:j * P + P], normed[:, j, :], g["ident"][:, :])
                        return last

                    def t_probs(n):
                        q = int(n[2])
                        pe.wait_ge(VE.sem, VE.at(f"scale{q}", it))
                        for k in range(4):
                            last = pe.transpose(slot(n)[:, k * P:k * P + P], probs[:, 2 * q + k // 2, k % 2, :],
                                                g["ident"][:, :])
                        return last

                    def proj_k(n):
                        if n == "k0":
                            pe.wait_ge(SC.sem, SC.at("x", it))
                        for j in range(2):
                            c = 2 * int(n[1]) + j
                            last = pe.matmul(slot(n)[:, j * 256:j * 256 + 256], g["wkv0"][:, c * P:c * P + P],
                                             kvT[:, :, :], start=True, stop=True)
                        return last

                    def proj_q(n):
                        for j in range(4):
                            c = 4 * int(n[1]) + j
                            last = pe.matmul(slot(n)[:, j * P:j * P + P], g["wq0"][:, c * P:c * P + P],
                                             kvT[:, :, S:2 * S], start=True, stop=True)
                        return last

                    emit = {"s": score, "v": proj_v, "y": out, "x": t_in, "k": proj_k, "q": proj_q}
                    for n in PE.names:
                        if n in ("s1", "s3", "v3") and routes(it - 3):
                            route.on_tensor(pe, it - 3, ("s1", "s3", "v3").index(n))
                        if n in RING:
                            i = RING.index(n) - RSLOTS
                            pe.wait_ge(SC.sem, SC.at(RING[i], it if i >= 0 else it - 1))
                        if not runs(n, it):
                            PE.skip(pe, n, it)
                            continue
                        step = {"pv": pv, "pt": t_probs}[n[:2]] if n[0] == "p" else emit[n[0]]
                        step(n).then_inc(PE.sem, 1)

                pe.wait_ge(cleared, 1)
                over_tiles(nc.tensor, body)

            @block.scalar
            def _(act):
                def body(it):
                    for n in SC.names:
                        if n in ("exp0", "exp1") and routes(it - 3):
                            route.on_scalar(act, it - 3, int(n[3]))
                        if not runs(n, it):
                            SC.skip(act, n, it)
                            continue
                        if n[:3] == "exp":
                            q = int(n[3])
                            act.wait_ge(VE.sem, VE.at(f"sub{q}", it))
                            p = probs[:, 2 * q:2 * q + 2, :, :].rearrange("p c b j -> p (c b j)")
                            act.activation(p, p, ACT.Exp).then_inc(SC.sem, 1)
                            continue
                        act.wait_ge(PE.sem, PE.at(n, it))
                        if n == "x":
                            for j in range(2):
                                ins = act.activation(
                                    kvT[:, :, S * j:S * j + S],
                                    slot(n)[:, j * P:j * P + P].rearrange("p (b s) -> p b s", b=2),
                                    ACT.Identity, bias=g["cols"][:, 2 * j + 1:2 * j + 2],
                                    scale=g["cols"][:, 2 * j:2 * j + 1])
                        elif n[0] == "k":
                            c = 2 * int(n[1])
                            ins = act.activation(kT[:, c:c + 2, :, :].rearrange("p c b j -> p (c b j)"), slot(n),
                                                 ACT.Copy)
                        elif n[0] == "q":
                            c = 4 * int(n[1])
                            for h2 in range(2):
                                r = slice(S * h2, S * h2 + S)
                                ins = act.activation(qT[r, c:c + 4, :, h2, :],
                                                     slot(n)[r, :].rearrange("p (c b s) -> p c b s", c=4, b=2),
                                                     ACT.Copy, scale=DH ** -0.5)
                        elif n[0] == "v":
                            b, half = int(n[1]) // 2, int(n[1]) % 2
                            ins = act.activation(v[:, b, half * BANK:half * BANK + BANK], slot(n), ACT.Copy)
                        elif n == "y":
                            act.wait_ge(VE.sem, VE.at("ynorm", it - 1))
                            ins = act.activation(y_raw[:, :], slot(n)[:, 0:D], ACT.Copy)
                        elif n[:2] == "pt":
                            c = 2 * int(n[2])
                            ins = act.activation(probsT[:, c:c + 2, :, :].rearrange("p c b j -> p (c b j)"),
                                                 slot(n), ACT.Copy)
                        else:
                            c = 4 * int(n[2])
                            ins = act.activation(oT[:, c:c + 4, :].rearrange("p c j -> p (c j)"), slot(n),
                                                 ACT.Copy)
                        ins.then_inc(SC.sem, 1)

                over_tiles(nc.scalar, body)

            @block.vector
            def _(dve):
                def body(it):
                    for n in VE.names:
                        if n in ("sum1", "scale2") and routes(it - 3):
                            route.on_vector(dve, it - 3, 2 + ("sum1", "scale2").index(n))
                        if n == "ynorm" and routes(it - 2):
                            dve.wait_ge(PO.sem, PO.at("x1", it - 1))
                            route.on_vector(dve, it - 2, 0)
                        if not runs(n, it) or (n == "go" and not runs("y", it)):
                            VE.skip(dve, n, it)
                        elif n == "norm":
                            dve.wait_ge(PE.sem, PE.at("x", it - 1))
                            for j, src in enumerate(("ctx", "x")):
                                ins = dve.tensor_scalar(normed[:, j, :], g[src][:, it + 1, :],
                                                        g["ln_mv"][:, j, it + 1, 0:1], g["ln_rstd"][:, j, it + 1, :],
                                                        ALU.subtract, ALU.mult)
                            ins.then_inc(VE.sem, 1)
                        elif n[:3] in ("max", "sub", "sum", "sca"):
                            q = int(n[-1])
                            s4 = scores[:, q, :].rearrange("p (h j) -> p h j", h=4)
                            p4 = probs[:, 2 * q:2 * q + 2, :, :].rearrange("p c b j -> p (c b) j")
                            per = [P, 4, P]
                            if n[:3] == "max":
                                dve.wait_ge(PE.sem, PE.at(f"s{q}", it))
                                dve.tensor_reduce(mx[:, 4 * q:4 * q + 4], s4, AX_X, ALU.max).then_inc(VE.sem, 1)
                            elif n[:3] == "sub":
                                dve.wait_ge(VE.sem, VE.at(f"max{q}", it))
                                dve.wait_ge(PE.sem, PE.at(f"pt{q}", it - 1))
                                dve.tensor_tensor(p4, s4, mx[:, 4 * q:4 * q + 4].unsqueeze(2).broadcast_to(per),
                                                  ALU.subtract).then_inc(VE.sem, 1)
                            elif n[:3] == "sum":
                                dve.wait_ge(SC.sem, SC.at(f"exp{q}", it))
                                dve.tensor_reduce(sums[:, 4 * q:4 * q + 4], p4, AX_X, ALU.add).then_inc(VE.sem, 1)
                            else:
                                dve.wait_ge(VE.sem, VE.at("recip", it))
                                dve.tensor_tensor(p4, p4, rsum[:, 4 * q:4 * q + 4].unsqueeze(2).broadcast_to(per),
                                                  ALU.mult).then_inc(VE.sem, 1)
                        elif n == "recip":
                            dve.wait_ge(VE.sem, VE.at("sum3", it))
                            dve.reciprocal(rsum[:, :], sums[:, :]).then_inc(VE.sem, 1)
                        elif n == "ystats":
                            dve.wait_ge(SC.sem, SC.at("y", it))
                            dve.bn_stats(stats[:, :], y_raw[:, :]).then_inc(VE.sem, 1)
                        elif n == "go":
                            dve.wait_ge(VE.sem, VE.at("ystats", it))
                            dve.sem_inc(VE.sem, 1)
                        elif n == "yaggr":
                            dve.bn_aggr(mv[:, :], stats[:, :]).then_inc(VE.sem, 1)
                        else:
                            dve.wait_ge(VE.sem, VE.at("yaggr", it))
                            dve.wait_ge(PO.sem, PO.at("y2", it))
                            dve.wait_ge(PO.sem, PO.at("g1", it - 1))
                            dve.tensor_scalar(y[:, :], y_raw[:, :], mv[:, 0:1], rstd[:, :], ALU.subtract,
                                              ALU.mult).then_inc(VE.sem, 1)
                    if routes(it - 2):
                        route.on_vector(dve, it - 2, 1)

                dve.memset(qT[:, :, :, :, :], 0.0).then_inc(cleared, 1)
                over_tiles(nc.vector, body)

            @block.gpsimd
            def _(pool):
                def body(it):
                    if routes(it - 3):
                        route.on_gpsimd(pool, it - 3, 1)
                    if runs("y", it):
                        pool.wait_ge(VE.sem, VE.at("yaggr", it))
                        pool.wait_ge(VE.sem, VE.at("ynorm", it - 1))
                        pool.tensor_tensor(tmp[:, :], mv[:, 1:2], g["eps"][:, 0:1], ALU.add).then_inc(PO.sem, 1)
                        pool.wait_ge(PO.sem, PO.at("y1", it))
                        pool.tensor_tensor(rstd[:, :], tmp[:, :], g["neg_half"][:, 0:1], ALU.pow).then_inc(PO.sem, 1)
                    else:
                        PO.skip(pool, "y1", it)
                        PO.skip(pool, "y2", it)
                    if routes(it - 2):
                        route.on_gpsimd(pool, it - 2, 0)
                    if runs("y", it):
                        t = it - 1
                        pool.wait_ge(VE.sem, VE.at("ynorm", it))
                        pool.tensor_tensor(gy[:, :], y[:, :], g["gain_o"][:, :], ALU.mult).then_inc(PO.sem, 1)
                        pool.wait_ge(PO.sem, PO.at("g1", it))
                        pool.tensor_tensor(gy[:, :], gy[:, :], g["bias_o"][:, :], ALU.add).then_inc(PO.sem, 1)
                        pool.wait_ge(PO.sem, PO.at("g2", it))
                        pool.tensor_tensor(g["x"][:, t, :], g["x"][:, t, :], gy[:, :],
                                           ALU.add).then_inc(PO.sem, 1)
                    else:
                        for n in PO.names[2:]:
                            PO.skip(pool, n, it)

                over_tiles(nc.gpsimd, body)
                pool.wait_ge(route.scattered, 16 * TOP0 * TILES)


def finish_weights(nc, m0, g, w):
    with ExitStack() as ctx:
        m = Mem(nc, ctx)
        raw = m.sb("raw_weights", [P, BLOCKS, P])
        banks = m.psum("w_banks", [P, 4, BANK])
        bias_bank = m.psum("w_bias_bank", [P, BANK])
        loaded = m.sem("raw_loaded")
        turned = m.sem("weights_turned")
        kept = m.sem("weights_kept")
        biased = m.sem("out_bias_summed")
        mask_step = m.sem("mask1_step")
        stats = m.sb("w_stats", [P, 2, TILES, 6])
        tmp = m.sb("w_tmp", [P, 2, TILES])
        rstd_step = m.sem("rstd_step")
        counted, aggregated, gathered = m.sem("w_stats_counted"), m.sem("w_stats_aggregated"), m.sem("w_stats_gathered")
        loads = [(raw[:, GATE:GATE + 16, :], w["L1_ffn_expert_gate"].rearrange("(k e) i d -> (e i) k d", e=2)),
                 (raw[:, UP:UP + 16, :], w["L1_ffn_expert_up"].rearrange("(k e) i d -> (e i) k d", e=2)),
                 (raw[:, DOWN:DOWN + 16, :].rearrange("p k (e i) -> p (k e) i", e=2),
                  w["L1_ffn_expert_down"].rearrange("e h i -> h e i")),
                 (raw[:, SHARED, :], w["L1_ffn_shared_gate"]),
                 (raw[:, SHARED + 1, :], w["L1_ffn_shared_up"]),
                 (raw[:, SHARED_DOWN, :], w["L1_ffn_shared_down"]),
                 (raw[0:E1, ROUTER1, :], w["L1_ffn_gate_w"]),
                 (raw[0:E0, ROUTER0, :], w["L0_ffn_expert_sel"]),
                 (raw[0:CH, BQ, :], w["L1_xattn_bq"].rearrange("(c p) e -> c (p e)", p=2)),
                 (raw[0:CH, BK, :], w["L1_xattn_bk"].rearrange("(c p) e -> c (p e)", p=2)),
                 (raw[0:CH, BV, :], w["L1_xattn_bv"].rearrange("(c p) e -> c (p e)", p=2))]
        rows = [P] * ROUTER1 + [E1, E0, CH, CH, CH]
        sets = [range(k, min(k + 4, BLOCKS)) for k in range(0, BLOCKS, 4)]
        with nc.Block() as block:
            @block.sync
            def _(sp):
                for dst, src in loads:
                    sp.dma_start(dst, src).then_inc(loaded, 16)

            @block.tensor
            def _(pe):
                pe.wait_ge(loaded, 16 * len(loads))
                for n, blocks in enumerate(sets):
                    if n >= 4:
                        pe.wait_ge(kept, n - 3)
                    for j, k in enumerate(blocks):
                        last = pe.transpose(banks[:, n % 4, j * P:j * P + rows[k]], raw[0:rows[k], k, :],
                                            g["ident"][0:rows[k], 0:rows[k]])
                    last.then_inc(turned, 1)
                pe.wait_ge(g["loads1"], g["n_late"])
                pe.wait_ge(kept, len(sets))
                for k in range(CH):
                    last = pe.matmul(bias_bank[:, 0:D], g["wT"][:, BV, k:k + 1].broadcast_to([P, P]),
                                     g["wo1"][:, k, :], start=(k == 0), stop=(k == CH - 1))
                last.then_inc(biased, 1)

            @block.scalar
            def _(act):
                for n, blocks in enumerate(sets):
                    act.wait_ge(turned, n + 1)
                    if blocks[-1] < ROUTER1:
                        last = act.activation(g["wT"][:, blocks[0]:blocks[-1] + 1, :].rearrange("p k c -> p (k c)"),
                                              banks[:, n % 4, 0:len(blocks) * P], ACT.Copy)
                    else:
                        for j, k in enumerate(blocks):
                            last = act.activation(g["wT"][:, k, 0:rows[k]], banks[:, n % 4, j * P:j * P + rows[k]],
                                                  ACT.Copy, scale=DH ** -0.5 if k == BQ else 1.0)
                    last.then_inc(kept, 1)

            @block.gpsimd
            def _(pool):
                rstd = g["ln_rstd"][:, :, :, 0]
                rstd_x = g["ln_rstd"][:, 1, :, 0]
                eps = g["eps"][:, 0:1]
                nh = g["neg_half"][:, 0:1]

                def chain(n, ins):
                    ins.then_inc(rstd_step, 1)
                    pool.wait_ge(rstd_step, n)
                pool.wait_ge(gathered, 2)
                chain(1, pool.tensor_tensor(tmp[:, :, :], g["ln_mv"][:, :, :, 1],
                                            eps.unsqueeze(2).broadcast_to([P, 2, TILES]), ALU.add))
                chain(2, pool.tensor_tensor(rstd, tmp[:, :, :], nh.unsqueeze(2).broadcast_to([P, 2, TILES]), ALU.pow))
                chain(3, pool.tensor_tensor(tmp[:, 0, :], g["ln_mv"][:, 1, :, 1], rstd_x, ALU.mult))
                chain(4, pool.tensor_tensor(tmp[:, 0, :], tmp[:, 0, :], rstd_x, ALU.mult))
                chain(5, pool.tensor_tensor(tmp[:, 0, :], tmp[:, 0, :], eps.broadcast_to([P, TILES]), ALU.add))
                chain(6, pool.tensor_tensor(tmp[:, 0, :], tmp[:, 0, :], nh.broadcast_to([P, TILES]), ALU.pow))
                pool.tensor_tensor(rstd_x, tmp[:, 0, :], rstd_x, ALU.mult).then_inc(rstd_step, 1)

            @block.vector
            def _(dve):
                with nc.vector.Fori(0, TILES) as t:
                    dve.bn_stats(stats[:, 0, t, :], g["ctx"][:, t, :])
                    dve.bn_stats(stats[:, 1, t, :], g["x"][:, t, :]).then_inc(counted, 1)
                dve.wait_ge(counted, TILES)
                dve.sem_inc(gathered, 1)
                for t in range(TILES):
                    dve.bn_aggr(g["ln_mv"][:, 0, t, :], stats[:, 0, t, :])
                    dve.bn_aggr(g["ln_mv"][:, 1, t, :], stats[:, 1, t, :]).then_inc(aggregated, 1)
                dve.wait_ge(aggregated, TILES)
                dve.sem_inc(gathered, 1)
                dve.wait_ge(g["loads1"], g["n_late"])
                dve.tensor_scalar(g["mask1"][:, :], g["mask1"][:, :], -1.0, 1.0, ALU.mult,
                                  ALU.add).then_inc(mask_step, 1)
                dve.wait_ge(mask_step, 1)
                dve.tensor_scalar(g["mask1"][:, :], g["mask1"][:, :], MASK1, None, ALU.mult)
                dve.wait_ge(biased, 1)
                dve.tensor_tensor(g["out_bias1"][:, :], bias_bank[:, 0:D], g["out_bias1"][:, :],
                                  ALU.add).then_inc(mask_step, 1)
                dve.wait_ge(mask_step, 2)
                dve.tensor_scalar(g["out_bias1"][:, :], g["out_bias1"][:, :], g["tanh_g"][:, 1:2], None,
                                  ALU.mult).then_inc(mask_step, 1)


def experts0(nc, m0, g, w):
    with ExitStack() as ctx:
        m = Mem(nc, ctx)
        keys = m.sb("b_keys", [P, E0, P])
        values = m.sb("b_values", [P, E0, D])
        table = m.sb("b_table", [1, 512], mybir.dt.int32)
        counts = m.sb("b_counts", [1, E0], mybir.dt.int32)
        weights_in = m.sem("b_weights_in")
        tails_sp, tails_act = m.sem("b_tails_sp"), m.sem("b_tails_act")
        with ExitStack() as ctx2:
            n = Mem(nc, ctx2)
            over = n.sb("b_over", [P, E0, TILES])
            tiles = n.sb("b_tiles", [P, E0])
            upto = n.sb("b_upto", [P, E0])
            none = n.sb("b_none", [P, E0])
            passed = n.sb("b_passed", [P, 2, E0])
            before = n.sb("b_before", [P, 2, E0])
            slot = n.sb("b_slot", [P, 4, 2])
            plan_bank = n.psum("b_plan_bank", [P, BANK])
            V = n.sem("b_plan")
            counted, planned, tabled = n.sem("b_counted"), n.sem("b_planned"), n.sem("b_tabled")
            with nc.Block() as block:
                @block.sync
                def _(sp):
                    sp.dma_start(keys[:, :, :], w["L0_ffn_keys"].rearrange("k d e -> d k e")).then_inc(weights_in, 16)
                    sp.dma_start(values[:, :, :],
                                 w["L0_ffn_values"].rearrange("k e v -> e k v")).then_inc(weights_in, 16)
                    sp.wait_ge(counted, 1)
                    with nc.sync.Fori(0, E0 // 2) as e:
                        row = sp.value_load(counts[0:1, bass.ds(e, 1)], min_val=0, max_val=E0 * REGION - P)
                        sp.dma_start(g["xs"][bass.ds(row, P), :], g["zeros"][:, :]).then_inc(tails_sp, 16)

                @block.scalar
                def _(act):
                    act.wait_ge(counted, 1)
                    with nc.scalar.Fori(E0 // 2, E0) as e:
                        row = act.value_load(counts[0:1, bass.ds(e, 1)], min_val=0, max_val=E0 * REGION - P)
                        act.dma_start(g["xs"][bass.ds(row, P), :], g["zeros"][:, :]).then_inc(tails_act, 16)

                @block.tensor
                def _(pe):
                    pe.wait_ge(planned, 1)
                    for v in range(2):
                        for h in range(2):
                            last = pe.matmul(plan_bank[0:1, 256 * v + P * h:256 * v + P * h + P],
                                             slot[:, 3 * v, h:h + 1], g["ident"][:, :], start=True, stop=True)
                    last.then_inc(tabled, 1)

                @block.vector
                def _(dve):
                    step = [0]

                    def chain(ins):
                        ins.then_inc(V, 1)
                        step[0] += 1
                        dve.wait_ge(V, step[0])
                    base = g["base"][:, :]
                    dve.scalar_tensor_tensor(counts[:, :], g["expert_id"][0:1, :], float(REGION), g["base"][0:1, :],
                                             ALU.mult, ALU.add).then_inc(counted, 1)
                    chain(dve.tensor_tensor(over[:, :, :], base.unsqueeze(2).broadcast_to([P, E0, TILES]),
                                            g["starts"][:, :].unsqueeze(1).broadcast_to([P, E0, TILES]), ALU.is_gt))
                    chain(dve.tensor_reduce(tiles[:, :], over[:, :, :], AX_X, ALU.add))
                    chain(dve.memset(none[:, :], 0.0))
                    chain(dve.tensor_tensor_scan(upto[:, :], tiles[:, :], none[:, :], 0.0, ALU.add, ALU.add))
                    chain(dve.tensor_tensor(none[:, :], upto[:, :], tiles[:, :], ALU.subtract))
                    chain(dve.tensor_scalar(g["first_row"][:, :], none[:, :], float(P), None, ALU.mult))
                    both = [P, 2, E0]
                    sid = g["slot_id"][:, :]
                    chain(dve.tensor_tensor(passed[:, :, :], upto[:, :].unsqueeze(1).broadcast_to(both),
                                            sid.unsqueeze(2).broadcast_to(both), ALU.is_le))
                    chain(dve.tensor_reduce(slot[:, 0, :], passed[:, :, :], AX_X, ALU.add))
                    chain(dve.tensor_tensor(before[:, :, :], passed[:, :, :],
                                            tiles[:, :].unsqueeze(1).broadcast_to(both), ALU.mult))
                    chain(dve.tensor_reduce(slot[:, 1, :], before[:, :, :], AX_X, ALU.add))
                    chain(dve.tensor_scalar(slot[:, 2, :], slot[:, 0, :], E0 - 0.5, None, ALU.is_lt))
                    chain(dve.tensor_tensor(slot[:, 1, :], sid, slot[:, 1, :], ALU.subtract))
                    chain(dve.tensor_tensor(slot[:, 0, :], slot[:, 0, :], slot[:, 2, :], ALU.mult))
                    chain(dve.tensor_tensor(slot[:, 1, :], slot[:, 1, :], slot[:, 2, :], ALU.mult))
                    chain(dve.tensor_scalar(slot[:, 1, :], slot[:, 1, :], float(P), None, ALU.mult))
                    dve.scalar_tensor_tensor(slot[:, 3, :], slot[:, 0, :], float(REGION), slot[:, 1, :], ALU.mult,
                                             ALU.add).then_inc(planned, 1)
                    dve.wait_ge(tabled, 1)
                    dve.tensor_copy(table[:, :], plan_bank[0:1, :]).then_inc(V, 1)

        xr = m.sb("b_rows", [P, 4, BATCH, D])
        xT = m.sb("b_xT", [P, BATCH, P])
        h = m.sb("b_h", [P, BATCH, P])
        hT = m.sb("b_hT", [P, BATCH, P])
        y = m.sb("b_y", [P, 4, BATCH, D])
        x_bank = m.psum("b_x_bank", [P, BANK])
        h_bank = m.psum("b_h_bank", [P, BANK])
        t_bank = m.psum("b_t_bank", [P, BANK])
        y_bank = m.psum("b_y_bank", [P, BANK])
        loaded = [m.sem(f"b_loaded{u}") for u in range(4)]
        stored = [m.sem(f"b_stored{u}") for u in range(4)]
        LAG = {"y": 3, "ht": 2, "h": 1, "x": 0}
        PE = Steps(m.sem("b_pe"), ["y", "ht", "h", "x"], 0)
        SC = Steps(m.sem("b_act"), ["ht", "x"], 0)
        VE = Steps(m.sem("b_dve"), ["y", "h"], 0)
        L = Steps(m.sem("b_rows_located"), ["onehot", "times", "first", "row"], 0)
        onehot = m.sb("b_onehot", [P, TOP0, E0])
        first = m.sb("b_first", [P, TOP0])
        END = BATCHES + 3

        def active(name, n):
            return True if not isinstance(n, int) else LAG[name] <= n < BATCHES + LAG[name]

        def over_time(eng, body):
            for n in range(4):
                body(n, n, 0)
            with eng.Fori(4, BATCHES, 4) as n4:
                for u in range(4):
                    body(n4 + u, u, n4)
            for n in range(BATCHES, END):
                body(n, n % 4, n - n % 4)

        with nc.Block() as block:
            @block.sync
            def _(sp):
                sp.wait_ge(tails_sp, 16 * (E0 // 2))
                sp.wait_ge(tails_act, 16 * (E0 // 2))
                ys_v = g["ys"].rearrange("(b j p) d -> b p j d", j=BATCH, p=P)

                def load(n, u):
                    if not isinstance(n, int) or n >= 4:
                        sp.wait_ge(PE.sem, PE.at("x", n - 4))
                    for j in range(BATCH):
                        row = sp.value_load(table[0:1, bass.ds(n * BATCH + (256 + j), 1)], min_val=0,
                                            max_val=E0 * REGION - P)
                        sp.dma_start(xr[:, u, j, :], g["xs"][bass.ds(row, P), :]).then_inc(loaded[u], 16)

                def store(b, u):
                    sp.wait_ge(VE.sem, VE.at("y", b + 3))
                    sp.dma_start(ys_v[b], y[:, u, :, :]).then_inc(stored[u], 16)

                for n in range(8):
                    load(n, n % 4)
                    if n == 7:
                        store(0, 0)
                with nc.sync.Fori(8, BATCHES, 4) as n4:
                    for u in range(4):
                        load(n4 + u, u)
                        store(n4 + (u - 7), (u + 1) % 4)
                for b in range(BATCHES - 7, BATCHES):
                    store(b, b % 4)
                for u in range(4):
                    sp.wait_ge(stored[u], 16 * (BATCHES // 4))

            @block.tensor
            def _(pe):
                def experts(b):
                    return [pe.value_load(table[0:1, bass.ds(b * BATCH + j, 1)], min_val=0, max_val=E0 - 1)
                            for j in range(BATCH)]

                def body(n, u, n4):
                    for name in PE.names:
                        if not active(name, n):
                            PE.skip(pe, name, n)
                            continue
                        if name == "y":
                            es = experts(n - 3)
                            pe.wait_ge(SC.sem, SC.at("ht", n - 1))
                            pe.wait_ge(VE.sem, VE.at("y", n - 1))
                            for j in range(BATCH):
                                last = pe.matmul(y_bank[:, j * P:j * P + P], hT[:, j, :], values[:, es[j], :],
                                                 start=True, stop=True)
                        elif name == "ht":
                            pe.wait_ge(VE.sem, VE.at("h", n - 1))
                            for j in range(BATCH):
                                last = pe.transpose(t_bank[:, j * P:j * P + P], h[:, j, :], g["ident"][:, :])
                        elif name == "h":
                            es = experts(n - 1)
                            pe.wait_ge(SC.sem, SC.at("x", n - 1))
                            for j in range(BATCH):
                                last = pe.matmul(h_bank[:, j * P:j * P + P], xT[:, j, :], keys[:, es[j], :],
                                                 start=True, stop=True)
                        else:
                            pe.wait_ge(loaded[u], n4 * 16 + 64)
                            for j in range(BATCH):
                                last = pe.transpose(x_bank[:, j * P:j * P + P], xr[:, u, j, :], g["ident"][:, :])
                        last.then_inc(PE.sem, 1)

                pe.wait_ge(weights_in, 32)
                over_time(nc.tensor, body)

            @block.scalar
            def _(act):
                def body(n, u, n4):
                    for name, bank, dst in (("ht", t_bank, hT), ("x", x_bank, xT)):
                        if not active(name, n):
                            SC.skip(act, name, n)
                            continue
                        act.wait_ge(PE.sem, PE.at(name, n))
                        act.activation(dst[:, :, :].rearrange("p j c -> p (j c)"), bank[:, :],
                                       ACT.Copy).then_inc(SC.sem, 1)
                over_time(nc.scalar, body)

            @block.vector
            def _(dve):
                def locate(tile):
                    shape = [P, TOP0, E0]
                    dve.wait_ge(L.sem, L.at("row", tile - 1))
                    dve.tensor_tensor(onehot[:, :, :], g["expert_id"][:, :].unsqueeze(1).broadcast_to(shape),
                                      g["chosen"][:, tile, :].unsqueeze(2).broadcast_to(shape),
                                      ALU.is_equal).then_inc(L.sem, 1)
                    dve.wait_ge(L.sem, L.at("onehot", tile))
                    dve.tensor_tensor(onehot[:, :, :], onehot[:, :, :],
                                      g["first_row"][:, :].unsqueeze(1).broadcast_to(shape),
                                      ALU.mult).then_inc(L.sem, 1)
                    dve.wait_ge(L.sem, L.at("times", tile))
                    dve.tensor_reduce(first[:, :], onehot[:, :, :], AX_X, ALU.add).then_inc(L.sem, 1)
                    dve.wait_ge(L.sem, L.at("first", tile))
                    dve.tensor_tensor(g["out_rows"][:, tile, :], first[:, :], g["position"][:, tile, :],
                                      ALU.add).then_inc(L.sem, 1)

                def body(n, u, n4):
                    if active("y", n):
                        dve.wait_ge(PE.sem, PE.at("y", n))
                        if not isinstance(n, int) or n >= 7:
                            dve.wait_ge(stored[(u + 1) % 4], n4 * 4 if u == 3 else (n4 - 4) * 4)
                        dve.tensor_copy(y[:, (u + 1) % 4, :, :].rearrange("p j c -> p (j c)"),
                                        y_bank[:, :]).then_inc(VE.sem, 1)
                    else:
                        VE.skip(dve, "y", n)
                    if active("h", n):
                        dve.wait_ge(PE.sem, PE.at("h", n))
                        dve.tensor_scalar(h[:, :, :].rearrange("p j c -> p (j c)"), h_bank[:, :], 0.0, None,
                                          ALU.max).then_inc(VE.sem, 1)
                    else:
                        VE.skip(dve, "h", n)

                for n in range(4):
                    body(n, n, 0)
                    locate(n)
                with nc.vector.Fori(1, TILES // 4) as k:
                    for u in range(4):
                        body(k * 4 + u, u, k * 4)
                        locate(k * 4 + u)
                with nc.vector.Fori(TILES, BATCHES, 4) as n4:
                    for u in range(4):
                        body(n4 + u, u, n4)
                for n in range(BATCHES, END):
                    body(n, n % 4, n - n % 4)


def attention1(nc, m0, g):
    with ExitStack() as ctx:
        m = Mem(nc, ctx)
        inT = m.sb("c_inT", [P, 2, P])
        kT = m.sb("c_kT", [P, CH, P])
        qT = m.sb("c_qT", [P, CH, P, 2])
        v = m.sb("c_v", [P, INNER])
        probs = m.sb("c_probs", [P, CH, 2, S])
        probsT = m.sb("c_probsT", [P, CH, S, 2])
        oT = m.sb("c_oT", [P, CH, P])
        rows = m.sb("c_rows", [P, 2, D])
        y_raw = m.sb("c_y_raw", [P, D])
        stats = m.sb("c_stats", [P, 6])
        mv = m.sb("c_mv", [P, 2])
        tmp = m.sb("c_tmp", [P, 1])
        rstd = m.sb("c_rstd", [P, 1])
        mx = m.sb("c_mx", [P, H])
        sums = m.sb("c_sums", [P, H])
        rsum = m.sb("c_rsum", [P, H])
        fetched = m.sb("c_fetched", [P, TOP0, D])
        RSLOTS = 6
        scores = m.psum("c_scores", [P, 2, BANK])
        ring = m.psum("c_ring", [P, RSLOTS, BANK])
        cleared = m.sem("c_qT_cleared")

        PE = Steps(m.sem("c_pe"), ["s0", "s1", "pv0", "pv1", "v0", "v1", "x", "y", "q0", "k0", "q1", "k1",
                                   "pt0", "pt1"], -2)
        SC = Steps(m.sem("c_act"), ["pv0", "pv1", "v0", "exp0", "exp1", "v1", "x", "y", "k0", "k1",
                                    "pt0", "pt1"], -2)
        VE = Steps(m.sem("c_dve"), ["add0", "add1", "norm", "max0", "max1", "sub0", "sub1", "sum0", "sum1",
                                    "recip", "q0", "scale0", "scale1", "q1", "mix0", "y1", "mix1", "y2", "mix2",
                                    "mix3", "mixed", "stats", "go", "aggr"], -2)
        PO = Steps(m.sem("c_pool"), ["copy", "r1", "r2"], -2)
        gathered = m.sem("c_gathered")
        rows_u = m.sb("c_out_rows", [P, TOP0], mybir.dt.uint32)
        rows_copied, rows_seen = m.sem("c_rows_copied"), m.sem("c_rows_seen")
        pe_free = m.sem("c_pe_free")
        RING = PE.names[2:]
        assert len(RING) % RSLOTS == 0

        def slot(n):
            return ring[:, RING.index(n) % RSLOTS, :]

        def runs(n, it):
            if not isinstance(it, int):
                return True
            if n[:3] == "mix" or n in ("stats", "go", "aggr", "r1", "r2"):
                tile = it + 2
            elif n[0] in "xkq" or n in ("norm", "copy"):
                tile = it + 1
            else:
                tile = it - 1 if n[0] == "y" or n[:2] == "pv" else it
            return 0 <= tile < TILES

        def fetches(tile):
            return not isinstance(tile, int) or 0 <= tile < TILES

        def over_tiles(eng, body):
            for it in range(-2, 1):
                body(it)
            with eng.Fori(1, TILES - 3) as it:
                body(it)
            for it in range(TILES - 3, TILES + 1):
                body(it)

        with nc.Block() as block:
            @block.tensor
            def _(pe):
                def body(it):
                    def score(n):
                        h2 = int(n[1])
                        if h2 == 0:
                            pe.wait_ge(SC.sem, SC.at("k1", it - 1))
                            pe.wait_ge(VE.sem, VE.at("q1", it - 1))
                            pe.sem_inc(pe_free, 1)
                        for k in range(4):
                            for b in range(2):
                                c = 4 * h2 + k
                                last = pe.matmul(scores[:, h2, k * P + S * b:k * P + S * b + S],
                                                 qT[:, c, S * b:S * b + S, :].rearrange("p s h -> p (s h)"),
                                                 kT[:, c, S * b:S * b + S], start=True, stop=True)
                        return last

                    def pv(n):
                        b = int(n[2])
                        if b == 0:
                            pe.wait_ge(SC.sem, SC.at("pt1", it - 1))
                        pe.sem_inc(pe_free, 1)
                        r = slice(S * b, S * b + S)
                        for c in range(CH):
                            for h2 in range(2):
                                last = pe.matmul(slot(n)[S * h2:S * h2 + S, c * S:c * S + S],
                                                 v[r, c * P + S * h2:c * P + S * h2 + S],
                                                 probsT[r, c, :, h2], start=True, stop=True)
                        return last

                    def proj_v(n):
                        at = BANK * int(n[1])
                        return pe.matmul(slot(n), inT[:, 1, :],
                                         g["wv1"][:, :, :].rearrange("p h e -> p (h e)")[:, at:at + BANK],
                                         start=True, stop=True)

                    def out(n):
                        pe.wait_ge(SC.sem, SC.at("pv1", it))
                        for k in range(CH):
                            last = pe.matmul(slot(n)[:, 0:D], oT[:, k, :], g["wo1"][:, k, :],
                                             start=(k == 0), stop=(k == CH - 1))
                        return last

                    def t_in(n):
                        pe.wait_ge(VE.sem, VE.at("norm", it))
                        pe.wait_ge(PO.sem, PO.at("copy", it))
                        for j in range(2):
                            last = pe.transpose(slot(n)[:, j * P:j * P + P], rows[:, j, :], g["ident"][:, :])
                        return last

                    def proj(n):
                        if n == "q0":
                            pe.wait_ge(SC.sem, SC.at("x", it))
                        wt, src = (g["wk1"], 1) if n[0] == "k" else (g["wq1"], 0)
                        for j in range(4):
                            c = 4 * int(n[1]) + j
                            last = pe.matmul(slot(n)[:, j * P:j * P + P],
                                             wt[:, 2 * c:2 * c + 2, :].rearrange("p h e -> p (h e)"),
                                             inT[:, src, :], start=True, stop=True)
                        return last

                    def t_probs(n):
                        h2 = int(n[2])
                        pe.wait_ge(VE.sem, VE.at(f"scale{h2}", it))
                        for j in range(4):
                            last = pe.transpose(slot(n)[:, j * P:j * P + P],
                                                probs[:, 4 * h2 + j, :, :].rearrange("p b j -> p (b j)"),
                                                g["ident"][:, :])
                        return last

                    emit = {"s": score, "v": proj_v, "y": out, "x": t_in, "k": proj, "q": proj}
                    for n in PE.names:
                        if n in RING:
                            i = RING.index(n) - RSLOTS
                            src = VE if RING[i][0] == "q" else SC
                            pe.wait_ge(src.sem, src.at(RING[i], it if i >= 0 else it - 1))
                        if not runs(n, it):
                            PE.skip(pe, n, it)
                            continue
                        step = {"pv": pv, "pt": t_probs}[n[:2]] if n[0] == "p" else emit[n[0]]
                        step(n).then_inc(PE.sem, 1)

                pe.wait_ge(cleared, 1)
                over_tiles(nc.tensor, body)

            @block.scalar
            def _(act):
                def body(it):
                    for n in SC.names:
                        if not runs(n, it):
                            SC.skip(act, n, it)
                            continue
                        if n[:3] == "exp":
                            h2 = int(n[3])
                            act.wait_ge(VE.sem, VE.at(f"sub{h2}", it))
                            p = probs[:, 4 * h2:4 * h2 + 4, :, :].rearrange("p c b j -> p (c b j)")
                            act.activation(p, p, ACT.Exp).then_inc(SC.sem, 1)
                            continue
                        act.wait_ge(PE.sem, PE.at(n, it))
                        if n == "x":
                            ins = act.activation(inT[:, :, :].rearrange("p a b -> p (a b)"), slot(n)[:, 0:2 * P],
                                                 ACT.Copy)
                        elif n == "y":
                            act.wait_ge(VE.sem, VE.at("y1", it - 1))
                            ins = act.activation(y_raw[:, :], slot(n)[:, 0:D], ACT.Copy)
                        elif n[0] == "v":
                            at = BANK * int(n[1])
                            ins = act.activation(v[:, at:at + BANK], slot(n), ACT.Copy)
                        elif n[0] == "k":
                            for j in range(4):
                                c = 4 * int(n[1]) + j
                                ins = act.activation(kT[:, c, :], slot(n)[:, j * P:j * P + P], ACT.Identity,
                                                     bias=g["wT"][:, BK, c:c + 1])
                        elif n[:2] == "pv":
                            b = int(n[2])
                            ins = act.activation(oT[:, :, S * b:S * b + S],
                                                 slot(n).rearrange("p (c s) -> p c s", c=CH), ACT.Copy)
                        else:
                            c = 4 * int(n[2])
                            ins = act.activation(probsT[:, c:c + 4, :, :].rearrange("p c s h -> p (c s h)"), slot(n),
                                                 ACT.Copy)
                        ins.then_inc(SC.sem, 1)

                over_tiles(nc.scalar, body)

            @block.vector
            def _(dve):
                def body(it):
                    per = [P, 8, S]
                    for n in VE.names:
                        if not runs(n, it):
                            VE.skip(dve, n, it)
                        elif n == "mixed":
                            dve.wait_ge(VE.sem, VE.at("mix3", it))
                            dve.sem_inc(VE.sem, 1)
                        elif n[:3] == "mix":
                            j = int(n[3])
                            xt = g["x"][:, it + 2, :]
                            if j == 0:
                                dve.wait_ge(gathered, (it + 3) * 16 * TOP0)
                            else:
                                dve.wait_ge(VE.sem, VE.at(f"mix{j - 1}", it))
                            dve.scalar_tensor_tensor(xt, fetched[:, j, :], g["gates"][:, it + 2, j:j + 1], xt,
                                                     ALU.mult, ALU.add).then_inc(VE.sem, 1)
                        elif n == "stats":
                            dve.bn_stats(stats[:, :], g["x"][:, it + 2, :]).then_inc(VE.sem, 1)
                        elif n == "go":
                            dve.wait_ge(VE.sem, VE.at("stats", it))
                            dve.wait_ge(PO.sem, PO.at("r2", it - 1))
                            dve.sem_inc(VE.sem, 1)
                        elif n == "aggr":
                            dve.bn_aggr(mv[:, :], stats[:, :]).then_inc(VE.sem, 1)
                        elif n == "norm":
                            dve.wait_ge(PO.sem, PO.at("r2", it - 1))
                            dve.wait_ge(PE.sem, PE.at("x", it - 1))
                            dve.tensor_scalar(rows[:, 0, :], g["x"][:, it + 1, :], mv[:, 0:1], rstd[:, :],
                                              ALU.subtract, ALU.mult).then_inc(VE.sem, 1)
                        elif n == "recip":
                            dve.wait_ge(VE.sem, VE.at("sum1", it))
                            dve.reciprocal(rsum[:, :], sums[:, :]).then_inc(VE.sem, 1)
                        elif n[0] == "q":
                            c = 4 * int(n[1])
                            dve.wait_ge(PE.sem, PE.at(n, it))
                            for h2 in range(2):
                                r = slice(S * h2, S * h2 + S)
                                ins = dve.scalar_tensor_tensor(
                                    qT[r, c:c + 4, :, h2], slot(n)[r, :].rearrange("p (c s) -> p c s", c=4), DH ** -0.5,
                                    g["wT"][r, BQ, c:c + 4].unsqueeze(2).broadcast_to([S, 4, P]),
                                    ALU.mult, ALU.add)
                            ins.then_inc(VE.sem, 1)
                        elif n == "y1":
                            dve.wait_ge(SC.sem, SC.at("y", it))
                            xt = g["x"][:, it - 1, :]
                            dve.scalar_tensor_tensor(xt, y_raw[:, :], g["tanh_g"][:, 1:2], xt, ALU.mult,
                                                     ALU.add).then_inc(VE.sem, 1)
                        elif n == "y2":
                            dve.wait_ge(VE.sem, VE.at("y1", it))
                            xt = g["x"][:, it - 1, :]
                            dve.tensor_tensor(xt, xt, g["out_bias1"][:, :], ALU.add).then_inc(VE.sem, 1)
                        else:
                            h2 = int(n[-1])
                            p8 = probs[:, 4 * h2:4 * h2 + 4, :, :].rearrange("p c b j -> p (c b) j")
                            m8 = slice(8 * h2, 8 * h2 + 8)
                            if n[:3] == "add":
                                dve.wait_ge(PE.sem, PE.at(f"s{h2}", it))
                                dve.wait_ge(PE.sem, PE.at(f"pt{h2}", it - 1))
                                dve.tensor_tensor(p8, scores[:, h2, :].rearrange("p (c j) -> p c j", j=S),
                                                  g["mask1"][:, :].unsqueeze(1).broadcast_to(per),
                                                  ALU.add).then_inc(VE.sem, 1)
                            elif n[:3] == "max":
                                dve.wait_ge(VE.sem, VE.at(f"add{h2}", it))
                                dve.tensor_reduce(mx[:, m8], p8, AX_X, ALU.max).then_inc(VE.sem, 1)
                            elif n[:3] == "sub":
                                dve.wait_ge(VE.sem, VE.at(f"max{h2}", it))
                                dve.tensor_tensor(p8, p8, mx[:, m8].unsqueeze(2).broadcast_to(per),
                                                  ALU.subtract).then_inc(VE.sem, 1)
                            elif n[:3] == "sum":
                                dve.wait_ge(SC.sem, SC.at(f"exp{h2}", it))
                                dve.tensor_reduce(sums[:, m8], p8, AX_X, ALU.add).then_inc(VE.sem, 1)
                            else:
                                dve.wait_ge(VE.sem, VE.at("recip", it))
                                dve.tensor_tensor(p8, p8, rsum[:, m8].unsqueeze(2).broadcast_to(per),
                                                  ALU.mult).then_inc(VE.sem, 1)

                dve.memset(qT[:, :, :, :], 0.0).then_inc(cleared, 1)
                over_tiles(nc.vector, body)

            @block.gpsimd
            def _(pool):
                def gather(it):
                    if not (isinstance(it, int) and it < -2):
                        pool.wait_ge(VE.sem, VE.at("mix3", it))
                    pool.tensor_copy(rows_u[:, :], g["out_rows"][:, it + 3, :]).then_inc(rows_copied, 1)
                    pool.wait_ge(rows_copied, it + 4)
                    pool.sem_inc(rows_seen, 1)
                    for j in range(TOP0):
                        pool.indirect_dma_start(fetched[:, j, :], None, g["ys"],
                                                bass.IndirectOffsetOnAxis(rows_u[:, j:j + 1], 0),
                                                bounds_check=SLOTS0 * P - 1).then_inc(gathered, 16)

                def body(it):
                    if runs("copy", it):
                        pool.wait_ge(PE.sem, PE.at("x", it - 1))
                        pool.tensor_copy(rows[:, 1, :], g["ctx"][:, it + 1, :]).then_inc(PO.sem, 1)
                    else:
                        PO.skip(pool, "copy", it)
                    if runs("r1", it):
                        pool.wait_ge(VE.sem, VE.at("aggr", it))
                        pool.tensor_tensor(tmp[:, :], mv[:, 1:2], g["eps"][:, 0:1], ALU.add).then_inc(PO.sem, 1)
                        pool.wait_ge(PO.sem, PO.at("r1", it))
                        pool.tensor_tensor(rstd[:, :], tmp[:, :], g["neg_half"][:, 0:1], ALU.pow).then_inc(PO.sem, 1)
                    else:
                        PO.skip(pool, "r1", it)
                        PO.skip(pool, "r2", it)
                    if fetches(it + 3):
                        gather(it)

                gather(-3)
                over_tiles(nc.gpsimd, body)


def experts1(nc, m0, g, out):
    with ExitStack() as ctx:
        m = Mem(nc, ctx)
        xfT = m.sb("d_xfT", [P, P])
        xf = m.sb("d_xf", [P, D])
        stats = m.sb("d_stats", [P, 6])
        mv = m.sb("d_mv", [P, 2])
        tmp = m.sb("d_tmp", [P, 1])
        rstd = m.sb("d_rstd", [P, 1])
        th_l = m.sb("d_th_l", [P, E1])
        sc = m.sb("d_scores", [P, E1])
        choice = m.sb("d_choice", [P, E1])
        top = m.sb("d_top", [P, GROUPS1, 8])
        gs = m.sb("d_group_scores", [P, GROUPS1])
        gt = m.sb("d_gt", [P, GROUPS1, GROUPS1])
        eq = m.sb("d_eq", [P, GROUPS1, GROUPS1])
        rank = m.sb("d_rank", [P, GROUPS1])
        gm = m.sb("d_group_mask", [P, GROUPS1])
        masked = m.sb("d_masked", [P, E1])
        top8 = m.sb("d_top8", [P, 8])
        left = m.sb("d_left", [P, E1])
        picked = m.sb("d_picked", [P, E1])
        wsum = m.sb("d_wsum", [P, 4])
        wts = m.sb("d_wts", [P, E1])
        th = m.sb("d_th", [P, 2, BANK])
        a = m.sb("d_a", [P, 2, BANK])
        h = m.sb("d_h", [P, 2, BANK])
        hT = m.sb("d_hT", [P, 2, BANK])
        g_bank = m.psum("d_g_bank", [P, 2, BANK])
        u_bank = m.psum("d_u_bank", [P, 2, BANK])
        t_bank = m.psum("d_t_bank", [P, 2, BANK])
        in_bank = m.psum("d_in_bank", [P, BANK])
        y_bank = m.psum("d_y_bank", [P, BANK])
        stored = m.sem("stored")

        NQ = 5
        WIDTH = [BANK] * 4 + [P]
        PE = Steps(m.sem("d_pe"), ["gu0", "gu1", "t0", "gu2", "t1", "y0", "gu3", "t2", "y1", "gu4", "x", "t3", "y2",
                                   "t4", "y3", "logits", "y4"])
        SC = Steps(m.sem("d_act"), ["th0", "th1", "t0", "th2", "t1", "th3", "t2", "th4", "x", "t3", "t4", "logits"])
        ROUTE = ["sc", "choice", "go_top", "top", "gs", "gt", "eq", "eqtri", "beat", "rank", "gm", "masked",
                 "go_top8", "top8", "go_left", "left",
                 "picked", "w", "wsum", "wsum_eps", "wrec", "wts"]
        VE = Steps(m.sem("d_dve"), ["a0", "b0", "a1", "b1", "a2", "b2", "stats", "go", "aggr", "norm",
                                    "a3", "b3", "a4", "b4", "y"] + ROUTE)
        PO = Steps(m.sem("d_pool"), ["c0", "c1", "c2", "r1", "r2", "c3"])

        with nc.Block() as block:
            @block.tensor
            def _(pe):
                def body(it, cur, nxt):
                    def gate_up(q):
                        if q == 0:
                            pe.wait_ge(SC.sem, SC.at("x", it - 1))
                        pe.wait_ge(VE.sem, VE.at(f"b{q - 2}" if q >= 2 else f"b{q + (2 if q == 1 else 4)}",
                                it if q >= 2 else it - 1))
                        if q < 4:
                            pe.matmul(g_bank[:, q % 2, :], xfT[:, :],
                                      g["wT"][:, GATE + 4 * q:GATE + 4 * q + 4, :].rearrange("p k c -> p (k c)"),
                                      start=True, stop=True)
                            return pe.matmul(u_bank[:, q % 2, :], xfT[:, :],
                                             g["wT"][:, UP + 4 * q:UP + 4 * q + 4, :].rearrange("p k c -> p (k c)"),
                                             start=True, stop=True)
                        pe.matmul(g_bank[:, 0, 0:P], xfT[:, :], g["wT"][:, SHARED, :], start=True, stop=True)
                        return pe.matmul(u_bank[:, 0, 0:P], xfT[:, :], g["wT"][:, SHARED + 1, :],
                                         start=True, stop=True)

                    def turn(q):
                        pe.wait_ge(PO.sem, PO.at(f"c{q}", it)) if q < 4 else pe.wait_ge(VE.sem, VE.at("b4", it))
                        if q >= 2:
                            pe.wait_ge(SC.sem, SC.at(f"t{q - 2}", it))
                        else:
                            pe.wait_ge(SC.sem, SC.at("t4" if q == 0 else "t3", it - 1))
                        for j in range(WIDTH[q] // P):
                            last = pe.transpose(t_bank[:, q % 2, j * P:j * P + P], h[:, q % 2, j * P:j * P + P],
                                                g["ident"][:, :])
                        return last

                    def down(q):
                        pe.wait_ge(SC.sem, SC.at(f"t{q}", it))
                        if q == 0:
                            pe.wait_ge(VE.sem, VE.at("y", it - 1))
                        for j in range(WIDTH[q] // P):
                            k = DOWN + 4 * q + j if q < 4 else SHARED_DOWN
                            last = pe.matmul(y_bank[:, 0:D], hT[:, q % 2, j * P:j * P + P], g["wT"][:, k, :],
                                             start=(q == 0 and j == 0), stop=(q == 4))
                        return last

                    for n in PE.names:
                        if not (nxt if n in ("x", "logits") else cur):
                            PE.skip(pe, n, it)
                            continue
                        if n == "x":
                            pe.wait_ge(VE.sem, VE.at("norm", it))
                            last = pe.transpose(in_bank[:, 0:P], xf[:, :], g["ident"][:, :])
                        elif n == "logits":
                            pe.wait_ge(SC.sem, SC.at("x", it))
                            last = pe.matmul(in_bank[:, P:P + E1], xfT[:, :], g["wT"][:, ROUTER1, 0:E1],
                                             start=True, stop=True)
                        else:
                            last = {"g": gate_up, "t": turn, "y": down}[n[0]](int(n[-1]))
                        last.then_inc(PE.sem, 1)

                run_tiles(nc.tensor, body)

            @block.scalar
            def _(act):
                def body(it, cur, nxt):
                    for n in SC.names:
                        if not (nxt if n in ("x", "logits") else cur):
                            SC.skip(act, n, it)
                            continue
                        q = int(n[-1]) if n[-1].isdigit() else 0
                        if n[:2] == "th":
                            act.wait_ge(PE.sem, PE.at(f"gu{q}", it))
                            if q >= 2:
                                act.wait_ge(VE.sem, VE.at(f"a{q - 2}", it))
                            else:
                                act.wait_ge(VE.sem, VE.at("a4" if q == 0 else "a3", it - 1))
                            ins = act.activation(th[:, q % 2, 0:WIDTH[q]], g_bank[:, q % 2, 0:WIDTH[q]], ACT.Tanh,
                                                 scale=0.5)
                        elif n == "x":
                            act.wait_ge(PE.sem, PE.at("x", it))
                            ins = act.activation(xfT[:, :], in_bank[:, 0:P], ACT.Copy)
                        elif n == "logits":
                            act.wait_ge(PE.sem, PE.at("logits", it))
                            act.wait_ge(VE.sem, VE.at("sc", it - 1))
                            ins = act.activation(th_l[:, :], in_bank[:, P:P + E1], ACT.Tanh, scale=0.5)
                        else:
                            act.wait_ge(PE.sem, PE.at(n, it))
                            ins = act.activation(hT[:, q % 2, 0:WIDTH[q]], t_bank[:, q % 2, 0:WIDTH[q]], ACT.Copy)
                            
                        ins.then_inc(SC.sem, 1)

                run_tiles(nc.scalar, body)

            @block.vector
            def _(dve):
                def body(it, cur, nxt):
                    def act_out(q):
                        if not cur:
                            VE.skip(dve, f"a{q}", it)
                            VE.skip(dve, f"b{q}", it)
                            return
                        wd = WIDTH[q]
                        ah = a[:, q % 2, 0:wd]
                        dve.wait_ge(SC.sem, SC.at(f"th{q}", it))
                        if q < 2:
                            dve.wait_ge(PO.sem, PO.at("c2" if q == 0 else "c3", it - 1))
                        elif q < 4:
                            dve.wait_ge(PO.sem, PO.at(f"c{q - 2}", it))
                        dve.scalar_tensor_tensor(ah, th[:, q % 2, 0:wd], 1.0, g_bank[:, q % 2, 0:wd], ALU.add,
                                                 ALU.mult).then_inc(VE.sem, 1)
                        dve.wait_ge(VE.sem, VE.at(f"a{q}", it))
                        if q == 4:
                            dve.wait_ge(PE.sem, PE.at("t2", it))
                            dve.wait_ge(PO.sem, PO.at("c2", it))
                        dst = ah if q < 4 else h[:, 0, 0:wd]
                        dve.scalar_tensor_tensor(dst, ah, 0.5, u_bank[:, q % 2, 0:wd], ALU.mult,
                                                 ALU.mult).then_inc(VE.sem, 1)

                    act_out(0)
                    act_out(1)
                    act_out(2)
                    if nxt:
                        dve.bn_stats(stats[:, :], g["x"][:, it + 1, :]).then_inc(VE.sem, 1)
                        dve.wait_ge(VE.sem, VE.at("stats", it))
                        dve.wait_ge(PO.sem, PO.at("r2", it - 1))
                        dve.sem_inc(VE.sem, 1)
                        dve.bn_aggr(mv[:, :], stats[:, :]).then_inc(VE.sem, 1)
                        dve.wait_ge(VE.sem, VE.at("aggr", it))
                        dve.wait_ge(PO.sem, PO.at("r2", it))
                        dve.wait_ge(PE.sem, PE.at("x", it - 1))
                        dve.tensor_scalar(xf[:, :], g["x"][:, it + 1, :], mv[:, 0:1], rstd[:, :], ALU.subtract,
                                          ALU.mult).then_inc(VE.sem, 1)
                    else:
                        for n in ("stats", "go", "aggr", "norm"):
                            VE.skip(dve, n, it)
                    act_out(3)
                    act_out(4)
                    if cur:
                        dve.wait_ge(PE.sem, PE.at("y4", it))
                        xt = g["x"][:, it, :]
                        dve.scalar_tensor_tensor(xt, y_bank[:, 0:D], g["tanh_g"][:, 3:4], xt, ALU.mult,
                                                 ALU.add).then_inc(VE.sem, 1)
                    else:
                        VE.skip(dve, "y", it)
                    if not nxt:
                        for n in ROUTE:
                            VE.skip(dve, n, it)
                        return

                    def chain(name, ins):
                        ins.then_inc(VE.sem, 1)
                        dve.wait_ge(VE.sem, VE.at(name, it))
                    dve.wait_ge(SC.sem, SC.at("logits", it))
                    chain("sc", dve.tensor_scalar(sc[:, :], th_l[:, :], 0.5, 0.5, ALU.mult, ALU.add))
                    def seen(name):
                        dve.sem_inc(VE.sem, 1)
                    chain("choice", dve.tensor_tensor(choice[:, :], sc[:, :], g["gate_bias"][:, :], ALU.add))
                    seen("go_top")
                    for n in range(GROUPS1):
                        last = dve.max(top[:, n, :], choice[:, n * GSIZE1:n * GSIZE1 + GSIZE1])
                    chain("top", last)
                    chain("gs", dve.tensor_tensor(gs[:, :], top[:, :, 0], top[:, :, 1], ALU.add))
                    mine = gs[:, :].unsqueeze(2).broadcast_to([P, GROUPS1, GROUPS1])
                    other = gs[:, :].unsqueeze(1).broadcast_to([P, GROUPS1, GROUPS1])
                    chain("gt", dve.tensor_tensor(gt[:, :, :], other, mine, ALU.is_gt))
                    chain("eq", dve.tensor_tensor(eq[:, :, :], other, mine, ALU.is_equal))
                    chain("eqtri", dve.tensor_tensor(eq[:, :, :], eq[:, :, :], g["tri"][:, :, :], ALU.mult))
                    chain("beat", dve.tensor_tensor(gt[:, :, :], gt[:, :, :], eq[:, :, :], ALU.add))
                    chain("rank", dve.tensor_reduce(rank[:, :], gt[:, :, :], AX_X, ALU.add))
                    chain("gm", dve.tensor_scalar(gm[:, :], rank[:, :], 1.5, None, ALU.is_lt))
                    chain("masked", dve.tensor_tensor(
                        masked[:, :].rearrange("p (g e) -> p g e", g=GROUPS1),
                        choice[:, :].rearrange("p (g e) -> p g e", g=GROUPS1),
                        gm[:, :].unsqueeze(2).broadcast_to([P, GROUPS1, GSIZE1]), ALU.mult))
                    seen("go_top8")
                    chain("top8", dve.max(top8[:, :], masked[:, :]))
                    seen("go_left")
                    chain("left", dve.match_replace(left[:, :], top8[:, :], masked[:, :], MASKED))
                    chain("picked", dve.tensor_tensor(picked[:, :], masked[:, :], left[:, :], ALU.not_equal))
                    chain("w", dve.tensor_tensor(picked[:, :], sc[:, :], picked[:, :], ALU.mult))
                    chain("wsum", dve.tensor_reduce(wsum[:, 0:1], picked[:, :], AX_X, ALU.add))
                    chain("wsum_eps", dve.tensor_scalar(wsum[:, 1:2], wsum[:, 0:1], 1e-20, None, ALU.add))
                    chain("wrec", dve.reciprocal(wsum[:, 2:3], wsum[:, 1:2]))
                    dve.wait_ge(PO.sem, PO.at("c3", it))
                    dve.tensor_scalar(wts[:, :], picked[:, :], wsum[:, 2:3], ROUTED_SCALING, ALU.mult,
                                      ALU.mult).then_inc(VE.sem, 1)

                run_tiles(nc.vector, body)

            @block.gpsimd
            def _(pool):
                def body(it, cur, nxt):
                    def weigh(q):
                        if not cur:
                            PO.skip(pool, f"c{q}", it)
                            return
                        if q == 0:
                            pool.wait_ge(VE.sem, VE.at("wts", it - 1))
                            pool.wait_ge(PE.sem, PE.at("t4", it - 1))
                        else:
                            pool.wait_ge(PE.sem, PE.at("t3", it - 1)) if q == 1 else pool.wait_ge(PE.sem, PE.at(f"t{q - 2}", it))
                        pool.wait_ge(VE.sem, VE.at(f"b{q}", it))
                        pool.tensor_tensor(h[:, q % 2, :].rearrange("p (e i) -> p e i", e=8),
                                           a[:, q % 2, :].rearrange("p (e i) -> p e i", e=8),
                                           wts[:, 8 * q:8 * q + 8].unsqueeze(2).broadcast_to([P, 8, I1]),
                                           ALU.mult).then_inc(PO.sem, 1)
                    weigh(0)
                    weigh(1)
                    weigh(2)
                    if nxt:
                        pool.wait_ge(VE.sem, VE.at("aggr", it))
                        pool.tensor_tensor(tmp[:, :], mv[:, 1:2], g["eps"][:, 0:1], ALU.add).then_inc(PO.sem, 1)
                        pool.wait_ge(PO.sem, PO.at("r1", it))
                        pool.wait_ge(VE.sem, VE.at("norm", it - 1))
                        pool.tensor_tensor(rstd[:, :], tmp[:, :], g["neg_half"][:, 0:1], ALU.pow).then_inc(PO.sem, 1)
                    else:
                        PO.skip(pool, "r1", it)
                        PO.skip(pool, "r2", it)
                    weigh(3)

                run_tiles(nc.gpsimd, body)

            @block.sync
            def _(sp):
                out_v = out.rearrange("(t b) s d -> t (b s) d", b=2)
                with nc.sync.Fori(0, TILES) as it:
                    sp.wait_ge(VE.sem, VE.at("y", it))
                    sp.dma_start(out_v[it], g["x"][:, it, :]).then_inc(stored, 16)
                sp.wait_ge(stored, 16 * TILES)


STAGES = 15


def flamingo(nc, w, out):
    with ExitStack() as ctx:
        m = Mem(nc, ctx)
        g = setup(nc, m, w)
        finish_weights(nc, m, g, w)
        if STAGES & 3:
            attention0(nc, m, g)
        if STAGES & 2:
            experts0(nc, m, g, w)
        if STAGES & 4:
            attention1(nc, m, g)
        if STAGES & 8:
            experts1(nc, m, g, out)
        else:
            write_out(nc, m, g, out)


def write_out(nc, m, g, out):
    stored = m.sem("stored")
    with nc.Block() as block:
        @block.sync
        def _(sp):
            sp.dma_start(out.rearrange("(t b) s d -> (b s) t d", b=2), g["x"][:, :, :]).then_inc(stored, 16)
            sp.wait_ge(stored, 16)


_OUTS = [((B, S, D), 'float32')]


def kernel(**inputs):
    import numpy as _np
    import concourse.bacc as _bacc
    from concourse.bass_utils import run_bass_kernel_spmd as _run

    nc = _bacc.Bacc("TRN2", target_bir_lowering=False, num_devices=1)
    arrays, w = {}, {}
    for name, value in inputs.items():
        a = _np.ascontiguousarray(value)
        arrays[f"in_{name}_dram"] = a
        w[name] = nc.dram_tensor(f"in_{name}_dram", a.shape, mybir.dt.from_np(a.dtype), kind="ExternalInput").ap()
    shape, dtype = _OUTS[0]
    out = nc.dram_tensor("out_0_dram", shape, mybir.dt.from_np(_np.dtype(dtype)), kind="ExternalOutput").ap()
    flamingo(nc, w, out)
    r = _run(nc, [arrays], core_ids=[0])
    return r.results[0]["out_0_dram"]
```

```python
from contextlib import ExitStack

import concourse.bass as bass
from concourse import mybir

ALU = mybir.AluOpType
ACT = mybir.ActivationFunctionType
F32 = mybir.dt.float32
BF16 = mybir.dt.bfloat16
AX_X = mybir.AxisListType.X

P = 128
B, S, D = 64, 64, 128
TILES = B * S // P
H, DH = 16, 64
INNER = H * DH
CH = INNER // P
E0, TOP0 = 64, 4
E1, I1 = 32, 64
GROUPS1, GSIZE1 = 4, 8
ROUTED_SCALING = 2.5
LN_EPS = 1e-5
MASK1 = -1e10
GATE, UP, DOWN, SHARED, SHARED_DOWN, ROUTER1 = 0, 16, 32, 48, 50, 51
BQ, BK, BV = 52, 53, 54
BLOCKS = 55
MASKED = -1e30
REGION = B * S + P
SLOTS0 = 192
BATCH = 4
BATCHES = SLOTS0 // BATCH
BANK = 512
SLOTS = 4


class Steps:

    def __init__(self, sem, names, first=-1):
        self.sem, self.names, self.first = sem, names, first

    def at(self, name, it):
        if isinstance(it, int) and it < self.first:
            return 0
        return (it - self.first) * len(self.names) + self.names.index(name) + 1

    def skip(self, eng, name, it):
        if self.at(name, it) > 1:
            eng.wait_ge(self.sem, self.at(name, it) - 1)
        eng.sem_inc(self.sem, 1)


class Mem:

    def __init__(self, nc, ctx):
        self.nc, self.ctx = nc, ctx

    def sb(self, name, shape, dt=F32):
        return self.ctx.enter_context(self.nc.sbuf_tensor(name, shape, dt))

    def psum(self, name, shape, dt=F32):
        return self.ctx.enter_context(self.nc.psum_tensor(name, shape, dt))

    def sem(self, name):
        return self.ctx.enter_context(self.nc.semaphore(name))


def run_tiles(eng_loop, body, n=TILES, apart=1):
    body(-1, False, True)
    with eng_loop.Fori(0, n - apart) as it:
        body(it, True, True)
    for it in range(n - apart, n):
        body(it, True, it + 1 < n)


def lasting(nc, m):
    g = {}
    g["x"] = m.sb("x_sb", [P, TILES, D])
    g["ctx"] = m.sb("ctx_sb", [P, TILES, D])
    g["ident"] = m.sb("ident", [P, P])
    g["neg_half"] = m.sb("neg_half", [P, 2])
    g["eps"] = m.sb("eps", [P, 2])
    g["tri"] = m.sb("tri", [P, GROUPS1, GROUPS1])
    g["before"] = m.sb("before", [P, P], BF16)
    g["ones"] = m.sb("ones", [P, P], BF16)
    g["zeros"] = m.sb("zeros", [P, D])
    g["expert_id"] = m.sb("expert_id", [P, E0])
    g["slot_id"] = m.sb("slot_id", [P, 2])
    g["starts"] = m.sb("starts", [P, TILES])
    g["base"] = m.sb("base", [P, E0])
    g["chosen"] = m.sb("chosen", [P, TILES, TOP0])
    g["position"] = m.sb("position", [P, TILES, TOP0])
    g["gates"] = m.sb("gates", [P, TILES, TOP0])
    g["first_row"] = m.sb("first_row", [P, E0])
    g["out_rows"] = m.sb("out_rows", [P, TILES, TOP0], mybir.dt.uint32)
    g["xs"] = nc.dram_tensor("expert_tokens", (E0 * REGION, D), F32).ap()
    g["ys"] = nc.dram_tensor("expert_outputs", (SLOTS0 * P, D), F32).ap()
    g["tanh_g"] = m.sb("tanh_g", [P, 4])
    g["cols"] = m.sb("cols", [P, 4])
    g["wq1"] = m.sb("wq1", [P, H, DH])
    g["wk1"] = m.sb("wk1", [P, H, DH])
    g["wv1"] = m.sb("wv1", [P, H, DH])
    g["wo1"] = m.sb("wo1", [P, CH, D])
    g["out_bias1"] = m.sb("out_bias1", [P, D])
    g["mask1"] = m.sb("mask1", [P, S])
    g["gate_bias"] = m.sb("gate_bias", [P, E1])
    g["wT"] = m.sb("wT", [P, BLOCKS, P])
    g["weights0_in"], g["weights1_in"] = m.sem("weights0_in"), m.sem("weights1_in")
    g["raw_in"] = m.sem("raw_weights_in")
    g["keys_in"] = m.sem("b_keys_in")
    return g


def setup(nc, ma, g, w):
    g["mask0"] = ma.sb("mask0", [P, TILES, 2, S], BF16)
    ids = ma.sb("ids", [P, E0 + 2 + TILES], mybir.dt.int32)
    s_ids = ma.sem("ids_made")
    g["wq0"] = ma.sb("wq0", [P, INNER])
    g["wkv0"] = ma.sb("wkv0", [P, 2 * INNER])
    g["wout0"] = ma.sb("wout0", [P, CH, D])
    g["gain_o"] = ma.sb("gain_o", [P, D])
    g["bias_o"] = ma.sb("bias_o", [P, D])
    ident_one = ma.sb("ident_one", [P, P])
    mask_raw = ma.sb("mask_raw", [1, TILES * 2 * S], mybir.dt.uint8)
    g["ln_mv"] = ma.sb("ln_mv", [P, 2, TILES, 2])
    g["ln_rstd"] = ma.sb("ln_rstd", [P, 2, TILES, 1])
    g["router0"] = ma.sb("router0", [P, E0])
    router_raw = ma.sb("router_raw", [E0, P])
    stats = ma.sb("ln_stats", [P, 2, TILES, 6])
    var_eps = ma.sb("ln_var_eps", [P, 2, TILES])
    setup_only = ExitStack()
    router_bank = Mem(nc, setup_only).psum("router_bank", [P, E0])
    mask_in, consts_in, router_in = ma.sem("mask_in"), ma.sem("consts_in"), ma.sem("router_in")
    CHUNKS = 4
    chunk_in = [ma.sem(f"chunk{k}_in") for k in range(CHUNKS)]
    ready, scaled = ma.sem("tanh_ready"), ma.sem("scaled")
    counted, gathered, aggregated = ma.sem("ln_counted"), ma.sem("ln_gathered"), ma.sem("ln_aggregated")
    rstd_step = ma.sem("rstd_step")
    turned = ma.sem("router_turned")
    s_pool = ma.sem("setup_pool")
    s_dve = ma.sem("setup_dve")
    x_v = w["x"].rearrange("(t b) s d -> (b s) t d", b=2)
    ctx_v = w["ctx_1024"].rearrange("(t b) s d -> (b s) t d", b=2)
    chunks = [(k * TILES // CHUNKS, (k + 1) * TILES // CHUNKS) for k in range(CHUNKS)]
    consts = [(g["tanh_g"][:, 0:2], w["g_xattn"].partition_broadcast(P)),
              (g["tanh_g"][:, 2:4], w["g_ffn"].partition_broadcast(P)),
              (g["gain_o"][:, :], w["L0_xattn_ln_o_g"].partition_broadcast(P)),
              (g["bias_o"][:, :], w["L0_xattn_ln_o_b"].partition_broadcast(P))]
    for n, name in enumerate(("ln_x_g", "ln_x_b", "ln_l_g", "ln_l_b")):
        consts.append((g["cols"][:, n:n + 1], w["L0_xattn_" + name].unsqueeze(1)))
    with nc.Block() as block:
        @block.sync
        def _(sp):
            sp.dma_start(mask_raw[:, :],
                         w["mask_BxS2_bk0"].rearrange("b j -> (b j)").unsqueeze(0)).then_inc(mask_in, 16)
            for k, (first, end) in enumerate(chunks):
                t = slice(first, end)
                sp.dma_start(g["ctx"][:, t, :], ctx_v[:, t, :]).then_inc(chunk_in[k], 16)
                sp.dma_start(g["x"][:, t, :], x_v[:, t, :]).then_inc(chunk_in[k], 16)
            sp.dma_start(g["wkv0"][:, :], w["L0_xattn_Wkv"]).then_inc(g["weights0_in"], 16)
            sp.dma_start(g["wq0"][:, :], w["L0_xattn_Wq"]).then_inc(g["weights0_in"], 16)
            sp.dma_start(g["wout0"][:, :, :],
                         w["L0_xattn_Wout"].rearrange("(c p) o -> p c o", p=P)).then_inc(g["weights0_in"], 16)
            wo_v = w["L1_xattn_Wo"].rearrange("(e c p) o -> p e c o", c=CH, p=2)
            late = [(g["wq1"][:, :, :], w["L1_xattn_Wq"].rearrange("h d e -> d h e")),
                    (g["wk1"][:, :, :], w["L1_xattn_Wk"].rearrange("h d e -> d h e")),
                    (g["wv1"][:, :, :], w["L1_xattn_Wv"].rearrange("h d e -> d h e")),
                    (g["out_bias1"][:, :], w["L1_xattn_bo"].partition_broadcast(P)),
                    (g["gate_bias"][:, :], w["L1_ffn_gate_bias"].partition_broadcast(P))]
            for p in range(2):
                late.append((g["mask1"][p:P:2, :], w["mask_SxS2_ff1"]))
                late.append((g["wo1"][DH * p:DH * p + DH, :, :], wo_v[p]))
            for dst, src in late:
                sp.dma_start(dst, src).then_inc(g["weights1_in"], 16)
            g["n_late"] = 16 * len(late)
            raw = g["wT"]
            raws = [(raw[:, GATE:GATE + 16, :], w["L1_ffn_expert_gate"].rearrange("(k e) i d -> (e i) k d", e=2)),
                    (raw[:, UP:UP + 16, :], w["L1_ffn_expert_up"].rearrange("(k e) i d -> (e i) k d", e=2)),
                    (raw[:, DOWN:DOWN + 16, :].rearrange("p k (e i) -> p (k e) i", e=2),
                     w["L1_ffn_expert_down"].rearrange("e h i -> h e i")),
                    (raw[:, SHARED, :], w["L1_ffn_shared_gate"]),
                    (raw[:, SHARED + 1, :], w["L1_ffn_shared_up"]),
                    (raw[:, SHARED_DOWN, :], w["L1_ffn_shared_down"]),
                    (raw[0:E1, ROUTER1, :], w["L1_ffn_gate_w"]),
                    (raw[0:CH, BQ, :], w["L1_xattn_bq"].rearrange("(c p) e -> c (p e)", p=2)),
                    (raw[0:CH, BK, :], w["L1_xattn_bk"].rearrange("(c p) e -> c (p e)", p=2)),
                    (raw[0:CH, BV, :], w["L1_xattn_bv"].rearrange("(c p) e -> c (p e)", p=2))]
            for dst, src in raws:
                sp.dma_start(dst, src).then_inc(g["raw_in"], 16)
            g["n_raw"] = 16 * len(raws)

        @block.gpsimd
        def _(pool):
            pool.memset(g["neg_half"][:, :], -0.5)
            pool.memset(g["eps"][:, :], LN_EPS)
            pool.memset(ident_one[:, :], 1.0).then_inc(s_pool, 1)
            pool.wait_ge(s_pool, 1)
            pool.affine_select(out=g["ident"][:, :], in_=ident_one[:, :], compare_op=ALU.is_equal, fill=0.0,
                               base=0, pattern=[[-1, P]], channel_multiplier=1).then_inc(s_pool, 1)
            pool.affine_select(out=g["before"][:, :], in_=ident_one[:, :], compare_op=ALU.is_gt, fill=0.0,
                               base=0, pattern=[[1, P]], channel_multiplier=-1)
            pool.iota(ids[:, 0:E0], [[1, E0]], 0, 0)
            pool.iota(ids[:, E0:E0 + 2], [[P, 2]], 0, 1)
            pool.iota(ids[:, E0 + 2:], [[P, TILES]], 0, 0).then_inc(s_ids, 1)
            pool.affine_select(out=g["tri"][:, :, :], in_=ident_one[:, 0:16].rearrange("p (a b) -> p a b", a=4),
                               compare_op=ALU.is_gt, fill=0.0, base=0, pattern=[[1, 4], [-1, 4]],
                               channel_multiplier=0)
            done = 0

            def chain(ins):
                nonlocal done
                done += 1
                ins.then_inc(rstd_step, 1)
                pool.wait_ge(rstd_step, done)
            for first, end in chunks:
                t, n = slice(first, end), end - first
                rstd, rstd_x = g["ln_rstd"][:, :, t, 0], g["ln_rstd"][:, 1, t, 0]
                tmp, tmp_x = var_eps[:, :, t], var_eps[:, 0, t]
                eps, nh = g["eps"][:, 0:1], g["neg_half"][:, 0:1]
                pool.wait_ge(aggregated, end)
                chain(pool.tensor_tensor(tmp, g["ln_mv"][:, :, t, 1], eps.unsqueeze(2).broadcast_to([P, 2, n]),
                                         ALU.add))
                chain(pool.tensor_tensor(rstd, tmp, nh.unsqueeze(2).broadcast_to([P, 2, n]), ALU.pow))
                chain(pool.tensor_tensor(tmp_x, g["ln_mv"][:, 1, t, 1], rstd_x, ALU.mult))
                chain(pool.tensor_tensor(tmp_x, tmp_x, rstd_x, ALU.mult))
                chain(pool.tensor_tensor(tmp_x, tmp_x, eps.broadcast_to([P, n]), ALU.add))
                chain(pool.tensor_tensor(tmp_x, tmp_x, nh.broadcast_to([P, n]), ALU.pow))
                chain(pool.tensor_tensor(rstd_x, tmp_x, rstd_x, ALU.mult))

        @block.tensor
        def _(pe):
            pe.wait_ge(s_pool, 2)
            pe.wait_ge(router_in, 16)
            pe.transpose(router_bank[:, :], router_raw[:, :], g["ident"][0:E0, 0:E0]).then_inc(turned, 1)

        @block.scalar
        def _(act):
            act.dma_start(router_raw[:, :], w["L0_ffn_expert_sel"]).then_inc(router_in, 16)
            for dst, src in consts:
                act.dma_start(dst, src).then_inc(consts_in, 16)
            act.wait_ge(turned, 1)
            act.activation(g["router0"][:, :], router_bank[:, :], ACT.Copy).then_inc(scaled, 1)
            act.wait_ge(consts_in, 16 * len(consts))
            act.activation(g["tanh_g"][:, :], g["tanh_g"][:, :], ACT.Tanh).then_inc(ready, 1)

        @block.vector
        def _(dve):
            dve.memset(g["mask0"][:, :, :, :], 0.0).then_inc(s_dve, 1)
            dve.memset(g["ones"][:, :], 1.0)
            dve.memset(g["zeros"][:, :], 0.0)
            dve.memset(g["base"][:, :], 0.0)
            dve.wait_ge(s_ids, 1)
            dve.tensor_copy(g["expert_id"][:, :], ids[:, 0:E0])
            dve.tensor_copy(g["slot_id"][:, :], ids[:, E0:E0 + 2])
            dve.tensor_copy(g["starts"][:, :], ids[:, E0 + 2:])
            dve.wait_ge(mask_in, 16)
            dve.wait_ge(s_dve, 1)
            dve.tensor_scalar(g["mask0"][0:1, :, :, :].rearrange("p t b j -> p (t b j)"), mask_raw[:, :], -MASKED,
                              MASKED, ALU.mult, ALU.add)
            for k, (first, end) in enumerate(chunks):
                dve.wait_ge(chunk_in[k], 32)
                dve.sem_inc(gathered, 1)
                for t in range(first, end):
                    dve.bn_stats(stats[:, 0, t, :], g["ctx"][:, t, :])
                    dve.bn_stats(stats[:, 1, t, :], g["x"][:, t, :]).then_inc(counted, 1)
                dve.wait_ge(counted, end)
                dve.sem_inc(gathered, 1)
                for t in range(first, end):
                    dve.bn_aggr(g["ln_mv"][:, 0, t, :], stats[:, 0, t, :])
                    dve.bn_aggr(g["ln_mv"][:, 1, t, :], stats[:, 1, t, :]).then_inc(aggregated, 1)
            dve.wait_ge(ready, 1)
            dve.tensor_scalar(g["gain_o"][:, :], g["gain_o"][:, :], g["tanh_g"][:, 0:1], None, ALU.mult)
            dve.tensor_scalar(g["bias_o"][:, :], g["bias_o"][:, :], g["tanh_g"][:, 0:1], None,
                              ALU.mult).then_inc(s_dve, 1)

    setup_only.close()


class Route:

    def __init__(self, nc, m, g, bank):
        self.nc, self.g, self.bank = nc, g, bank
        self.xf = m.sb("r_xf", [P, D])
        self.xfT = m.sb("r_xfT", [P, P])
        self.stats = m.sb("r_stats", [P, 6])
        self.mv = m.sb("r_mv", [P, 2])
        self.tmp = m.sb("r_tmp", [P, 1])
        self.rstd = m.sb("r_rstd", [P, 1])
        self.th = m.sb("r_th", [P, E0])
        self.sc = m.sb("r_scores", [P, E0])
        self.top8 = m.sb("r_top8", [P, 8])
        self.index8 = m.sb("r_index8", [P, 8], mybir.dt.uint32)
        self.onehot = m.sb("r_onehot", [P, TOP0, E0])
        self.sent = m.sb("r_sent", [P, E0], BF16)
        self.pos = m.sb("r_pos", [P, E0])
        self.at = m.sb("r_at", [P, TOP0, E0])
        self.rows = m.sb("r_rows", [P, TOP0], mybir.dt.uint32)
        self.scattered = m.sem("scattered")
        self.PE = Steps(m.sem("r_pe"), ["x", "logits", "rank"], 0)
        self.SC = Steps(m.sem("r_act"), ["x", "logits"], 0)
        self.VE = Steps(m.sem("r_dve"), ["stats", "go", "aggr", "norm", "sc", "go_top", "top", "go_index", "index",
                                         "chosen", "onehot", "sent", "pos", "base", "at", "position", "rows"], 0)
        self.PO = Steps(m.sem("r_pool"), ["r1", "r2"], 0)
        self.rows_seen = m.sem("r_rows_seen")

    def on_tensor(self, pe, it, part):
        g, PE = self.g, self.PE
        if part == 0:
            pe.wait_ge(self.VE.sem, self.VE.at("norm", it))
            pe.wait_ge(self.SC.sem, self.SC.at("logits", it - 1))
            pe.transpose(self.bank[:, 0:P], self.xf[:, :], g["ident"][:, :]).then_inc(PE.sem, 1)
        elif part == 1:
            pe.wait_ge(self.SC.sem, self.SC.at("x", it))
            pe.matmul(self.bank[:, P:P + E0], self.xfT[:, :], g["router0"][:, :], start=True,
                      stop=True).then_inc(PE.sem, 1)
        else:
            pe.wait_ge(self.VE.sem, self.VE.at("sent", it))
            pe.wait_ge(self.SC.sem, self.SC.at("logits", it))
            pe.wait_ge(self.VE.sem, self.VE.at("base", it - 1))
            pe.matmul(self.bank[:, P + E0:P + 2 * E0], g["before"][:, :], self.sent[:, :], start=True, stop=True)
            pe.matmul(self.bank[:, P + 2 * E0:P + 3 * E0], g["ones"][:, :], self.sent[:, :], start=True,
                      stop=True).then_inc(PE.sem, 1)

    def on_scalar(self, act, it, part):
        if part == 0:
            act.wait_ge(self.PE.sem, self.PE.at("x", it))
            act.activation(self.xfT[:, :], self.bank[:, 0:P], ACT.Copy).then_inc(self.SC.sem, 1)
            return
        act.wait_ge(self.PE.sem, self.PE.at("logits", it))
        act.wait_ge(self.VE.sem, self.VE.at("sc", it - 1))
        act.activation(self.th[:, :], self.bank[:, P:P + E0], ACT.Tanh, scale=0.5).then_inc(self.SC.sem, 1)

    def on_vector(self, dve, it, part):
        g, VE = self.g, self.VE
        xt = g["x"][:, it, :]

        def chain(name, ins):
            ins.then_inc(VE.sem, 1)
            dve.wait_ge(VE.sem, VE.at(name, it))

        def seen():
            dve.sem_inc(VE.sem, 1)
        if part == 0:
            chain("stats", dve.bn_stats(self.stats[:, :], xt))
            dve.wait_ge(self.PO.sem, self.PO.at("r2", it - 1))
            seen()
            dve.bn_aggr(self.mv[:, :], self.stats[:, :]).then_inc(VE.sem, 1)
        elif part == 1:
            dve.wait_ge(VE.sem, VE.at("aggr", it))
            dve.wait_ge(self.PO.sem, self.PO.at("r2", it))
            dve.wait_ge(self.PE.sem, self.PE.at("x", it - 1))
            if not (isinstance(it, int) and it == 0):
                dve.wait_ge(self.scattered, 16 * TOP0 * it)
            dve.tensor_scalar(self.xf[:, :], xt, self.mv[:, 0:1], self.rstd[:, :], ALU.subtract,
                              ALU.mult).then_inc(VE.sem, 1)
        elif part == 2:
            dve.wait_ge(self.SC.sem, self.SC.at("logits", it))
            chain("sc", dve.tensor_scalar(self.sc[:, :], self.th[:, :], 0.5, 0.5, ALU.mult, ALU.add))
            seen()
            chain("top", dve.max(self.top8[:, :], self.sc[:, :]))
            seen()
            dve.max_index(self.index8[:, :], self.top8[:, :], self.sc[:, :]).then_inc(VE.sem, 1)
            dve.tensor_scalar(g["gates"][:, it, :], self.top8[:, 0:TOP0], g["tanh_g"][:, 2:3], None, ALU.mult)
            dve.wait_ge(VE.sem, VE.at("index", it))
            chain("chosen", dve.tensor_copy(g["chosen"][:, it, :], self.index8[:, 0:TOP0]))
            ids = g["expert_id"][:, :].unsqueeze(1).broadcast_to([P, TOP0, E0])
            chain("onehot", dve.tensor_tensor(
                self.onehot[:, :, :], ids, g["chosen"][:, it, :].unsqueeze(2).broadcast_to([P, TOP0, E0]),
                ALU.is_equal))
            with self.nc.allow_low_precision("zeros and ones"):
                dve.tensor_reduce(self.sent[:, :], self.onehot[:, :, :].rearrange("p j e -> p e j"), AX_X,
                                  ALU.add).then_inc(VE.sem, 1)
        else:
            dve.wait_ge(self.PE.sem, self.PE.at("rank", it))
            chain("pos", dve.tensor_tensor(self.pos[:, :], self.bank[:, P + E0:P + 2 * E0], g["base"][:, :],
                                           ALU.add))
            dve.tensor_tensor(g["base"][:, :], self.bank[:, P + 2 * E0:P + 3 * E0], g["base"][:, :],
                              ALU.add).then_inc(VE.sem, 1)
            chain("at", dve.tensor_tensor(self.at[:, :, :], self.onehot[:, :, :],
                                          self.pos[:, :].unsqueeze(1).broadcast_to([P, TOP0, E0]), ALU.mult))
            chain("position", dve.tensor_reduce(g["position"][:, it, :], self.at[:, :, :], AX_X, ALU.add))
            dve.scalar_tensor_tensor(self.rows[:, :], g["chosen"][:, it, :], float(REGION),
                                     g["position"][:, it, :], ALU.mult, ALU.add).then_inc(VE.sem, 1)

    def on_gpsimd(self, pool, it, part):
        g, PO = self.g, self.PO
        if part == 0:
            pool.wait_ge(self.VE.sem, self.VE.at("aggr", it))
            pool.tensor_tensor(self.tmp[:, :], self.mv[:, 1:2], g["eps"][:, 0:1], ALU.add).then_inc(PO.sem, 1)
            pool.wait_ge(PO.sem, PO.at("r1", it))
            pool.wait_ge(self.VE.sem, self.VE.at("norm", it - 1))
            pool.tensor_tensor(self.rstd[:, :], self.tmp[:, :], g["neg_half"][:, 0:1], ALU.pow).then_inc(PO.sem, 1)
        else:
            pool.wait_ge(self.VE.sem, self.VE.at("rows", it))
            pool.sem_inc(self.rows_seen, 1)
            for j in range(TOP0):
                pool.indirect_dma_start(g["xs"], bass.IndirectOffsetOnAxis(self.rows[:, j:j + 1], 0), self.xf[:, :],
                                        None, bounds_check=E0 * REGION - 1).then_inc(self.scattered, 16)


def attention0(nc, m0, g, w):
    with ExitStack() as ctx:
        m = Mem(nc, ctx)
        kvT = m.sb("a_kvT", [P, 2, 2 * S])
        kT = m.sb("a_kT", [P, CH, 2, 2 * S])
        qT = m.sb("a_qT", [P, CH, 2, 2, S])
        v = m.sb("a_v", [P, 2, INNER])
        probs = m.sb("a_probs", [P, CH, 2, P])
        probsT = m.sb("a_probsT", [P, CH, 2, P])
        oT = m.sb("a_oT", [P, CH, P])
        normed = m.sb("a_normed", [P, 2, D])
        y_raw = m.sb("a_y_raw", [P, D])
        y = m.sb("a_y", [P, D])
        gy = m.sb("a_gy", [P, D])
        stats = m.sb("a_stats", [P, 6])
        mv = m.sb("a_mv", [P, 2])
        tmp = m.sb("a_tmp", [P, 1])
        rstd = m.sb("a_rstd", [P, 1])
        mx = m.sb("a_mx", [P, H])
        sums = m.sb("a_sums", [P, H])
        rsum = m.sb("a_rsum", [P, H])
        cleared = m.sem("a_qT_cleared")
        scores = m.psum("a_scores", [P, 4, BANK])
        ring = m.psum("a_ring", [P, 3, BANK])
        route = Route(nc, m, g, m.psum("r_bank", [P, BANK]))

        PE = Steps(m.sem("a_pe"), ["s0", "s1", "s2", "s3", "pv0", "pv1", "v0", "y", "v1", "v2", "v3", "x",
                                   "pt0", "pt1", "k0", "k1", "k2", "k3", "q0", "q1", "pt2", "pt3"])
        SC = Steps(m.sem("a_act"), ["exp0", "exp1", "exp2", "pv0", "pv1", "exp3", "v0", "y", "v1", "v2", "v3", "x",
                                    "pt0", "pt1", "k0", "k1", "k2", "k3", "q0", "q1", "pt2", "pt3"])
        VE = Steps(m.sem("a_dve"), ["max0", "max1", "sub0", "max2", "sub1", "max3", "sub2", "sum0", "sub3",
                                    "norm", "sum1", "recip0", "scale0", "scale1", "sum2", "sum3", "recip1", "scale2", "scale3",
                                    "ystats", "go", "yaggr", "ynorm"])
        PO = Steps(m.sem("a_pool"), ["y1", "y2", "g1", "g2", "x1"])
        RING = PE.names[4:]
        RSLOTS = 3
        assert len(RING) % RSLOTS == 0

        def slot(n):
            return ring[:, RING.index(n) % RSLOTS, :]

        def runs(n, it):
            if not isinstance(it, int):
                return True
            tile = it + 1 if n[0] in "xkq" or n == "norm" else it - 1 if n[0] == "y" or n[:2] == "pv" else it
            return 0 <= tile < TILES

        def routes(tile):
            return not isinstance(tile, int) or 0 <= tile < TILES

        def over_tiles(eng, body):
            for it in range(-1, 4):
                body(it)
            with eng.Fori(4, TILES - 1) as it:
                body(it)
            for it in range(TILES - 1, TILES + 3):
                body(it)

        with nc.Block() as block:
            @block.sync
            def _(sp):
                sp.dma_start(g["keys"][:, :, :], w["L0_ffn_keys"].rearrange("k d e -> d k e")).then_inc(g["keys_in"], 16)

            @block.tensor
            def _(pe):
                def body(it):
                    def score(n):
                        q = int(n[1])
                        if q % 2 == 0:
                            pe.wait_ge(SC.sem, SC.at(f"q{q // 2}", it - 1))
                        pe.wait_ge(VE.sem, VE.at(f"sub{q}", it - 1))
                        for k in range(4):
                            c, b = 2 * q + k // 2, k % 2
                            pe.matmul(scores[:, q, k * P:k * P + P], qT[:, c, b, :, :].rearrange("p h s -> p (h s)"),
                                      kT[:, c, b, :], start=(k == 0), stop=False, skip_group_check=True)
                        return pe.matmul(scores[:, q, :].rearrange("p (c b j) -> p c b j", c=2, b=2)[:, :, :, 0:S],
                                         g["ones"][:, :],
                                         g["mask0"][:, it, :, :].unsqueeze(1).broadcast_to([P, 2, 2, S]),
                                         start=False, stop=True, skip_group_check=True)

                    def pv(n):
                        if n == "pv0":
                            pe.wait_ge(SC.sem, SC.at("pt3", it - 1))
                        for k in range(4):
                            c = 4 * int(n[2]) + k
                            for b in range(2):
                                for h2 in range(2):
                                    last = pe.matmul(slot(n)[S * h2:S * h2 + S, k * P + S * b:k * P + S * b + S],
                                                     v[:, b, c * P + S * h2:c * P + S * h2 + S],
                                                     probsT[:, c, b, S * h2:S * h2 + S], start=True, stop=True)
                        return last

                    def proj_v(n):
                        b, half = int(n[1]) // 2, int(n[1]) % 2
                        at = INNER + half * BANK
                        return pe.matmul(slot(n), kvT[:, b, :], g["wkv0"][:, at:at + BANK], start=True, stop=True)

                    def out(n):
                        pe.wait_ge(SC.sem, SC.at("pv1", it))
                        for c in range(CH):
                            last = pe.matmul(slot(n)[:, 0:D], oT[:, c, :], g["wout0"][:, c, :],
                                             start=(c == 0), stop=(c == CH - 1))
                        return last

                    def t_in(n):
                        pe.wait_ge(VE.sem, VE.at("norm", it))
                        for j in range(2):
                            last = pe.transpose(slot(n)[:, j * P:j * P + P], normed[:, j, :], g["ident"][:, :])
                        return last

                    def t_probs(n):
                        q = int(n[2])
                        pe.wait_ge(VE.sem, VE.at(f"scale{q}", it))
                        for k in range(4):
                            last = pe.transpose(slot(n)[:, k * P:k * P + P], probs[:, 2 * q + k // 2, k % 2, :],
                                                g["ident"][:, :])
                        return last

                    def proj_k(n):
                        if n == "k0":
                            pe.wait_ge(SC.sem, SC.at("x", it))
                        for j in range(2):
                            c = 2 * int(n[1]) + j
                            last = pe.matmul(slot(n)[:, j * 256:j * 256 + 256], g["wkv0"][:, c * P:c * P + P],
                                             kvT[:, :, :], start=True, stop=True)
                        return last

                    def proj_q(n):
                        for j in range(4):
                            c = 4 * int(n[1]) + j
                            last = pe.matmul(slot(n)[:, j * P:j * P + P], g["wq0"][:, c * P:c * P + P],
                                             kvT[:, :, S:2 * S], start=True, stop=True)
                        return last

                    emit = {"s": score, "v": proj_v, "y": out, "x": t_in, "k": proj_k, "q": proj_q}
                    for n in PE.names:
                        if n in ("s1", "s3", "v3") and routes(it - 3):
                            route.on_tensor(pe, it - 3, ("s1", "s3", "v3").index(n))
                        if n in RING:
                            i = RING.index(n) - RSLOTS
                            pe.wait_ge(SC.sem, SC.at(RING[i], it if i >= 0 else it - 1))
                        if not runs(n, it):
                            PE.skip(pe, n, it)
                            continue
                        step = {"pv": pv, "pt": t_probs}[n[:2]] if n[0] == "p" else emit[n[0]]
                        step(n).then_inc(PE.sem, 1)

                pe.wait_ge(cleared, 1)
                pe.wait_ge(g["weights0_in"], 48)
                over_tiles(nc.tensor, body)

            @block.scalar
            def _(act):
                def body(it):
                    for n in SC.names:
                        if n in ("exp0", "exp1") and routes(it - 3):
                            route.on_scalar(act, it - 3, int(n[3]))
                        if not runs(n, it):
                            SC.skip(act, n, it)
                            continue
                        if n[:3] == "exp":
                            q = int(n[3])
                            act.wait_ge(VE.sem, VE.at(f"sub{q}", it))
                            p = probs[:, 2 * q:2 * q + 2, :, :].rearrange("p c b j -> p (c b j)")
                            act.activation(p, p, ACT.Exp).then_inc(SC.sem, 1)
                            continue
                        act.wait_ge(PE.sem, PE.at(n, it))
                        if n == "x":
                            for j in range(2):
                                ins = act.activation(
                                    kvT[:, :, S * j:S * j + S],
                                    slot(n)[:, j * P:j * P + P].rearrange("p (b s) -> p b s", b=2),
                                    ACT.Identity, bias=g["cols"][:, 2 * j + 1:2 * j + 2],
                                    scale=g["cols"][:, 2 * j:2 * j + 1])
                        elif n[0] == "k":
                            c = 2 * int(n[1])
                            ins = act.activation(kT[:, c:c + 2, :, :].rearrange("p c b j -> p (c b j)"), slot(n),
                                                 ACT.Copy)
                        elif n[0] == "q":
                            c = 4 * int(n[1])
                            for h2 in range(2):
                                r = slice(S * h2, S * h2 + S)
                                ins = act.activation(qT[r, c:c + 4, :, h2, :],
                                                     slot(n)[r, :].rearrange("p (c b s) -> p c b s", c=4, b=2),
                                                     ACT.Copy, scale=DH ** -0.5)
                        elif n[0] == "v":
                            b, half = int(n[1]) // 2, int(n[1]) % 2
                            ins = act.activation(v[:, b, half * BANK:half * BANK + BANK], slot(n), ACT.Copy)
                        elif n == "y":
                            act.wait_ge(VE.sem, VE.at("ynorm", it - 1))
                            ins = act.activation(y_raw[:, :], slot(n)[:, 0:D], ACT.Copy)
                        elif n[:2] == "pt":
                            c = 2 * int(n[2])
                            ins = act.activation(probsT[:, c:c + 2, :, :].rearrange("p c b j -> p (c b j)"),
                                                 slot(n), ACT.Copy)
                        else:
                            c = 4 * int(n[2])
                            ins = act.activation(oT[:, c:c + 4, :].rearrange("p c j -> p (c j)"), slot(n),
                                                 ACT.Copy)
                        ins.then_inc(SC.sem, 1)

                over_tiles(nc.scalar, body)

            @block.vector
            def _(dve):
                def body(it):
                    for n in VE.names:
                        if n in ("sum1", "sum2") and routes(it - 3):
                            route.on_vector(dve, it - 3, 2 + ("sum1", "sum2").index(n))
                        if n == "ynorm" and routes(it - 2):
                            dve.wait_ge(PO.sem, PO.at("x1", it - 1))
                            route.on_vector(dve, it - 2, 0)
                        if not runs(n, it) or (n == "go" and not runs("y", it)):
                            VE.skip(dve, n, it)
                        elif n == "norm":
                            dve.wait_ge(PE.sem, PE.at("x", it - 1))
                            for j, src in enumerate(("ctx", "x")):
                                ins = dve.tensor_scalar(normed[:, j, :], g[src][:, it + 1, :],
                                                        g["ln_mv"][:, j, it + 1, 0:1], g["ln_rstd"][:, j, it + 1, :],
                                                        ALU.subtract, ALU.mult)
                            ins.then_inc(VE.sem, 1)
                        elif n[:3] in ("max", "sub", "sum", "sca"):
                            q = int(n[-1])
                            s4 = scores[:, q, :].rearrange("p (h j) -> p h j", h=4)
                            p4 = probs[:, 2 * q:2 * q + 2, :, :].rearrange("p c b j -> p (c b) j")
                            per = [P, 4, P]
                            if n[:3] == "max":
                                dve.wait_ge(PE.sem, PE.at(f"s{q}", it))
                                dve.tensor_reduce(mx[:, 4 * q:4 * q + 4], s4, AX_X, ALU.max).then_inc(VE.sem, 1)
                            elif n[:3] == "sub":
                                dve.wait_ge(VE.sem, VE.at(f"max{q}", it))
                                dve.wait_ge(PE.sem, PE.at(f"pt{q}", it - 1))
                                dve.tensor_tensor(p4, s4, mx[:, 4 * q:4 * q + 4].unsqueeze(2).broadcast_to(per),
                                                  ALU.subtract).then_inc(VE.sem, 1)
                            elif n[:3] == "sum":
                                dve.wait_ge(SC.sem, SC.at(f"exp{q}", it))
                                dve.tensor_reduce(sums[:, 4 * q:4 * q + 4], p4, AX_X, ALU.add).then_inc(VE.sem, 1)
                            else:
                                dve.wait_ge(VE.sem, VE.at(f"recip{q // 2}", it))
                                dve.tensor_tensor(p4, p4, rsum[:, 4 * q:4 * q + 4].unsqueeze(2).broadcast_to(per),
                                                  ALU.mult).then_inc(VE.sem, 1)
                        elif n[:5] == "recip":
                            half = int(n[5])
                            dve.wait_ge(VE.sem, VE.at(f"sum{2 * half + 1}", it))
                            dve.reciprocal(rsum[:, 8 * half:8 * half + 8],
                                           sums[:, 8 * half:8 * half + 8]).then_inc(VE.sem, 1)
                        elif n == "ystats":
                            dve.wait_ge(SC.sem, SC.at("y", it))
                            dve.bn_stats(stats[:, :], y_raw[:, :]).then_inc(VE.sem, 1)
                        elif n == "go":
                            dve.wait_ge(VE.sem, VE.at("ystats", it))
                            dve.sem_inc(VE.sem, 1)
                        elif n == "yaggr":
                            dve.bn_aggr(mv[:, :], stats[:, :]).then_inc(VE.sem, 1)
                        else:
                            dve.wait_ge(VE.sem, VE.at("yaggr", it))
                            dve.wait_ge(PO.sem, PO.at("y2", it))
                            dve.wait_ge(PO.sem, PO.at("g1", it - 1))
                            dve.tensor_scalar(y[:, :], y_raw[:, :], mv[:, 0:1], rstd[:, :], ALU.subtract,
                                              ALU.mult).then_inc(VE.sem, 1)
                    if routes(it - 2):
                        route.on_vector(dve, it - 2, 1)

                dve.memset(qT[:, :, :, :, :], 0.0).then_inc(cleared, 1)
                over_tiles(nc.vector, body)

            @block.gpsimd
            def _(pool):
                def body(it):
                    if routes(it - 3):
                        route.on_gpsimd(pool, it - 3, 1)
                    if runs("y", it):
                        pool.wait_ge(VE.sem, VE.at("yaggr", it))
                        pool.wait_ge(VE.sem, VE.at("ynorm", it - 1))
                        pool.tensor_tensor(tmp[:, :], mv[:, 1:2], g["eps"][:, 0:1], ALU.add).then_inc(PO.sem, 1)
                        pool.wait_ge(PO.sem, PO.at("y1", it))
                        pool.tensor_tensor(rstd[:, :], tmp[:, :], g["neg_half"][:, 0:1], ALU.pow).then_inc(PO.sem, 1)
                    else:
                        PO.skip(pool, "y1", it)
                        PO.skip(pool, "y2", it)
                    if routes(it - 2):
                        route.on_gpsimd(pool, it - 2, 0)
                    if runs("y", it):
                        t = it - 1
                        pool.wait_ge(VE.sem, VE.at("ynorm", it))
                        pool.tensor_tensor(gy[:, :], y[:, :], g["gain_o"][:, :], ALU.mult).then_inc(PO.sem, 1)
                        pool.wait_ge(PO.sem, PO.at("g1", it))
                        pool.tensor_tensor(gy[:, :], gy[:, :], g["bias_o"][:, :], ALU.add).then_inc(PO.sem, 1)
                        pool.wait_ge(PO.sem, PO.at("g2", it))
                        pool.tensor_tensor(g["x"][:, t, :], g["x"][:, t, :], gy[:, :],
                                           ALU.add).then_inc(PO.sem, 1)
                    else:
                        for n in PO.names[2:]:
                            PO.skip(pool, n, it)

                over_tiles(nc.gpsimd, body)
                pool.wait_ge(route.scattered, 16 * TOP0 * TILES)


class FinishWeights:

    def __init__(self, m, g):
        self.g = g
        self.banks = m.psum("w_banks", [P, 4, BANK])
        self.bias_bank = m.psum("w_bias_bank", [P, BANK])
        self.turned = m.sem("weights_turned")
        self.kept = m.sem("weights_kept")
        self.biased = m.sem("out_bias_summed")
        self.mask_step = m.sem("mask1_step")
        self.rows = [P] * ROUTER1 + [E1, CH, CH, CH]
        self.sets = [range(k, min(k + 4, BLOCKS)) for k in range(0, BLOCKS, 4)]

    def on_tensor(self, pe):
        g = self.g
        pe.wait_ge(g["raw_in"], g["n_raw"])
        for n, blocks in enumerate(self.sets):
            if n >= 4:
                pe.wait_ge(self.kept, n - 3)
            for j, k in enumerate(blocks):
                r = self.rows[k]
                last = pe.transpose(self.banks[:, n % 4, j * P:j * P + r], g["wT"][0:r, k, :], g["ident"][0:r, 0:r])
            last.then_inc(self.turned, 1)
        pe.wait_ge(g["weights1_in"], g["n_late"])
        pe.wait_ge(self.kept, len(self.sets))
        for k in range(CH):
            last = pe.matmul(self.bias_bank[:, 0:D], g["wT"][:, BV, k:k + 1].broadcast_to([P, P]),
                             g["wo1"][:, k, :], start=(k == 0), stop=(k == CH - 1))
        last.then_inc(self.biased, 1)

    def on_scalar(self, act):
        g = self.g
        for n, blocks in enumerate(self.sets):
            act.wait_ge(self.turned, n + 1)
            if blocks[-1] < ROUTER1:
                last = act.activation(g["wT"][:, blocks[0]:blocks[-1] + 1, :].rearrange("p k c -> p (k c)"),
                                      self.banks[:, n % 4, 0:len(blocks) * P], ACT.Copy)
            else:
                for j, k in enumerate(blocks):
                    last = act.activation(g["wT"][:, k, 0:self.rows[k]],
                                          self.banks[:, n % 4, j * P:j * P + self.rows[k]],
                                          ACT.Copy, scale=DH ** -0.5 if k == BQ else 1.0)
            last.then_inc(self.kept, 1)

    def on_vector(self, dve):
        g = self.g
        dve.wait_ge(g["weights1_in"], g["n_late"])
        dve.tensor_scalar(g["mask1"][:, :], g["mask1"][:, :], -1.0, 1.0, ALU.mult, ALU.add).then_inc(self.mask_step, 1)
        dve.wait_ge(self.mask_step, 1)
        dve.tensor_scalar(g["mask1"][:, :], g["mask1"][:, :], MASK1, None, ALU.mult)
        dve.wait_ge(self.biased, 1)
        dve.tensor_tensor(g["out_bias1"][:, :], self.bias_bank[:, 0:D], g["out_bias1"][:, :],
                          ALU.add).then_inc(self.mask_step, 1)
        dve.wait_ge(self.mask_step, 2)
        dve.tensor_scalar(g["out_bias1"][:, :], g["out_bias1"][:, :], g["tanh_g"][:, 1:2], None,
                          ALU.mult).then_inc(self.mask_step, 1)


def experts0(nc, m0, g, w):
    with ExitStack() as ctx:
        m = Mem(nc, ctx)
        keys = g["keys"]
        values = m.sb("b_values", [P, E0, D])
        table = m.sb("b_table", [1, 512], mybir.dt.int32)
        counts = m.sb("b_counts", [1, E0], mybir.dt.int32)
        weights_in = m.sem("b_values_in")
        VALUES_PIECE = 8
        TAILS = (6, 11)
        tails_sp, tails_act, tails_pool = m.sem("b_tails_sp"), m.sem("b_tails_act"), m.sem("b_tails_pool")
        with ExitStack() as ctx2:
            n = Mem(nc, ctx2)
            over = n.sb("b_over", [P, E0, TILES], BF16)
            tiles = n.sb("b_tiles", [P, E0])
            upto = n.sb("b_upto", [P, E0])
            none = n.sb("b_none", [P, E0])
            passed = n.sb("b_passed", [P, 2, E0])
            before = n.sb("b_before", [P, 2, E0])
            slot = n.sb("b_slot", [P, 4, 2])
            plan_bank = n.psum("b_plan_bank", [P, BANK])
            finish = FinishWeights(n, g)
            V = n.sem("b_plan")
            counted, planned, tabled = n.sem("b_counted"), n.sem("b_planned"), n.sem("b_tabled")
            with nc.Block() as block:
                @block.sync
                def _(sp):
                    sp.wait_ge(counted, 1)
                    with nc.sync.Fori(0, TAILS[0]) as e:
                        rows = nc.values_load_multi_w_load_instructions(
                            counts[0:1, bass.ds(e * 4, 4)], engines=[mybir.EngineType.SP], min_val=0,
                            max_val=E0 * REGION - P)[1]
                        for row in rows:
                            sp.dma_start(g["xs"][bass.ds(row, P), :], g["zeros"][:, :]).then_inc(tails_sp, 16)

                @block.scalar
                def _(act):
                    finish.on_scalar(act)
                    act.wait_ge(counted, 1)
                    with nc.scalar.Fori(TAILS[0], TAILS[1]) as e:
                        rows = nc.values_load_multi_w_load_instructions(
                            counts[0:1, bass.ds(e * 4, 4)], engines=[mybir.EngineType.Activation], min_val=0,
                            max_val=E0 * REGION - P)[1]
                        for row in rows:
                            act.dma_start(g["xs"][bass.ds(row, P), :], g["zeros"][:, :]).then_inc(tails_act, 16)

                @block.gpsimd
                def _(pool):
                    pool.wait_ge(counted, 1)
                    with nc.gpsimd.Fori(TAILS[1], E0 // 4) as e:
                        rows = nc.values_load_multi_w_load_instructions(
                            counts[0:1, bass.ds(e * 4, 4)], engines=[mybir.EngineType.Pool], min_val=0,
                            max_val=E0 * REGION - P)[1]
                        for row in rows:
                            pool.dma_start(g["xs"][bass.ds(row, P), :], g["zeros"][:, :]).then_inc(tails_pool, 16)
                    for k in range(0, E0, VALUES_PIECE):
                        piece = slice(k, k + VALUES_PIECE)
                        pool.dma_start(values[:, piece, :], w["L0_ffn_values"].rearrange("k e v -> e k v")[:, piece, :]
                                       ).then_inc(weights_in, 16)

                @block.tensor
                def _(pe):
                    finish.on_tensor(pe)
                    pe.wait_ge(planned, 1)
                    for v in range(2):
                        for h in range(2):
                            last = pe.matmul(plan_bank[0:1, 256 * v + P * h:256 * v + P * h + P],
                                             slot[:, 3 * v, h:h + 1], g["ident"][:, :], start=True, stop=True)
                    last.then_inc(tabled, 1)

                @block.vector
                def _(dve):
                    step = [0]

                    def chain(ins):
                        ins.then_inc(V, 1)
                        step[0] += 1
                        dve.wait_ge(V, step[0])
                    base = g["base"][:, :]
                    dve.scalar_tensor_tensor(counts[:, :], g["expert_id"][0:1, :], float(REGION), g["base"][0:1, :],
                                             ALU.mult, ALU.add).then_inc(counted, 1)
                    chain(dve.tensor_tensor(over[:, :, :], base.unsqueeze(2).broadcast_to([P, E0, TILES]),
                                            g["starts"][:, :].unsqueeze(1).broadcast_to([P, E0, TILES]), ALU.is_gt))
                    chain(dve.tensor_reduce(tiles[:, :], over[:, :, :], AX_X, ALU.add))
                    chain(dve.memset(none[:, :], 0.0))
                    chain(dve.tensor_tensor_scan(upto[:, :], tiles[:, :], none[:, :], 0.0, ALU.add, ALU.add))
                    chain(dve.tensor_tensor(none[:, :], upto[:, :], tiles[:, :], ALU.subtract))
                    chain(dve.tensor_scalar(g["first_row"][:, :], none[:, :], float(P), None, ALU.mult))
                    both = [P, 2, E0]
                    sid = g["slot_id"][:, :]
                    chain(dve.tensor_tensor(passed[:, :, :], upto[:, :].unsqueeze(1).broadcast_to(both),
                                            sid.unsqueeze(2).broadcast_to(both), ALU.is_le))
                    chain(dve.tensor_reduce(slot[:, 0, :], passed[:, :, :], AX_X, ALU.add))
                    chain(dve.tensor_tensor(before[:, :, :], passed[:, :, :],
                                            tiles[:, :].unsqueeze(1).broadcast_to(both), ALU.mult))
                    chain(dve.tensor_reduce(slot[:, 1, :], before[:, :, :], AX_X, ALU.add))
                    chain(dve.tensor_scalar(slot[:, 2, :], slot[:, 0, :], E0 - 0.5, None, ALU.is_lt))
                    chain(dve.tensor_tensor(slot[:, 1, :], sid, slot[:, 1, :], ALU.subtract))
                    chain(dve.tensor_tensor(slot[:, 0, :], slot[:, 0, :], slot[:, 2, :], ALU.mult))
                    chain(dve.tensor_tensor(slot[:, 1, :], slot[:, 1, :], slot[:, 2, :], ALU.mult))
                    chain(dve.tensor_scalar(slot[:, 1, :], slot[:, 1, :], float(P), None, ALU.mult))
                    dve.scalar_tensor_tensor(slot[:, 3, :], slot[:, 0, :], float(REGION), slot[:, 1, :], ALU.mult,
                                             ALU.add).then_inc(planned, 1)
                    dve.wait_ge(tabled, 1)
                    dve.tensor_copy(table[:, :], plan_bank[0:1, :]).then_inc(V, 1)
                    finish.on_vector(dve)

        xr = m.sb("b_rows", [P, 4, BATCH, D])
        xT = m.sb("b_xT", [P, BATCH, P])
        h = m.sb("b_h", [P, BATCH, P])
        hT = m.sb("b_hT", [P, BATCH, P])
        y = m.sb("b_y", [P, 4, BATCH, D])
        x_bank = m.psum("b_x_bank", [P, BANK])
        h_bank = m.psum("b_h_bank", [P, BANK])
        t_bank = m.psum("b_t_bank", [P, BANK])
        y_bank = m.psum("b_y_bank", [P, BANK])
        loaded = [m.sem(f"b_loaded{u}") for u in range(4)]
        stored = [m.sem(f"b_stored{u}") for u in range(4)]
        LAG = {"h": 1, "x": 0, "y": 2, "ht": 1}
        PE = Steps(m.sem("b_pe"), ["h", "x", "y", "ht"], 0)
        SC = Steps(m.sem("b_act"), ["x", "ht"], 0)
        VE = Steps(m.sem("b_dve"), ["h", "y"], 0)
        L = Steps(m.sem("b_rows_located"), ["onehot", "times", "first", "row"], 0)
        onehot = m.sb("b_onehot", [P, TOP0, E0])
        first = m.sb("b_first", [P, TOP0])
        END = BATCHES + 2

        def active(name, n):
            return True if not isinstance(n, int) else LAG[name] <= n < BATCHES + LAG[name]

        def over_time(eng, body):
            for n in range(8):
                body(n, n % 4, n - n % 4)
            with eng.Fori(8, BATCHES, 4) as n4:
                for u in range(4):
                    body(n4 + u, u, n4)
            for n in range(BATCHES, END):
                body(n, n % 4, n - n % 4)

        with nc.Block() as block:
            @block.sync
            def _(sp):
                sp.wait_ge(tails_sp, 64 * TAILS[0])
                sp.wait_ge(tails_act, 64 * (TAILS[1] - TAILS[0]))
                sp.wait_ge(tails_pool, 16 * E0 - 64 * TAILS[1])

                def load(n, u):
                    if not isinstance(n, int) or n >= 4:
                        sp.wait_ge(PE.sem, PE.at("x", n - 4))
                    first_rows = nc.values_load_multi_w_load_instructions(
                        table[0:1, bass.ds(n * BATCH + 256, BATCH)], engines=[mybir.EngineType.SP], min_val=0,
                        max_val=E0 * REGION - P)[1]
                    for j in range(BATCH):
                        sp.dma_start(xr[:, u, j, :], g["xs"][bass.ds(first_rows[j], P), :]).then_inc(loaded[u], 16)

                for n in range(4):
                    load(n, n)
                with nc.sync.Fori(4, BATCHES, 4) as n4:
                    for u in range(4):
                        load(n4 + u, u)

            @block.gpsimd
            def _(pool):
                ys_v = g["ys"].rearrange("(b j p) d -> b p j d", j=BATCH, p=P)
                with nc.gpsimd.Fori(0, BATCHES // 4) as k:
                    for u in range(4):
                        pool.wait_ge(VE.sem, VE.at("y", k * 4 + (u + 2)))
                        pool.dma_start(ys_v[k * 4 + u], y[:, u, :, :]).then_inc(stored[u], 16)
                for u in range(4):
                    pool.wait_ge(stored[u], 16 * (BATCHES // 4))

            @block.tensor
            def _(pe):
                es = {}

                def experts(b, count):
                    got = nc.values_load_multi_w_load_instructions(
                        table[0:1, bass.ds(b * BATCH, count * BATCH)], engines=[mybir.EngineType.PE], min_val=0,
                        max_val=E0 - 1)[1]
                    return [got[k * BATCH:k * BATCH + BATCH] for k in range(count)]

                def body(n, u, n4, first=False, last_here=False):
                    if first:
                        es["y"], es["h"] = experts(n - 2, 2)
                    ahead = not last_here and (not isinstance(n, int) or n < BATCHES)
                    for name in PE.names:
                        if not active(name, n):
                            PE.skip(pe, name, n)
                            continue
                        if name == "h":
                            pe.wait_ge(SC.sem, SC.at("x", n - 1))
                            for j in range(BATCH):
                                last = pe.matmul(h_bank[:, j * P:j * P + P], xT[:, j, :], keys[:, es["h"][j], :],
                                                 start=True, stop=True)
                        elif name == "x":
                            pe.wait_ge(loaded[u], n4 * 16 + 64)
                            for j in range(BATCH):
                                last = pe.transpose(x_bank[:, j * P:j * P + P], xr[:, u, j, :], g["ident"][:, :])
                        elif name == "y":
                            pe.wait_ge(SC.sem, SC.at("ht", n - 1))
                            pe.wait_ge(VE.sem, VE.at("y", n - 1))
                            for j in range(BATCH):
                                last = pe.matmul(y_bank[:, j * P:j * P + P], hT[:, j, :], values[:, es["y"][j], :],
                                                 start=True, stop=True)
                        else:
                            if ahead:
                                es["next"] = experts(n, 1)[0]
                            pe.wait_ge(VE.sem, VE.at("h", n))
                            for j in range(BATCH):
                                last = pe.transpose(t_bank[:, j * P:j * P + P], h[:, j, :], g["ident"][:, :])
                        last.then_inc(PE.sem, 1)
                    if isinstance(n, int) and n == 0:
                        es["next"] = experts(0, 1)[0]
                    es["y"], es["h"] = es.get("h"), es.get("next")

                pe.wait_ge(g["keys_in"], 16)
                pe.wait_ge(weights_in, 16 * E0 // VALUES_PIECE)
                for n in range(8):
                    body(n, n % 4, n - n % 4, last_here=n == 7)
                with nc.tensor.Fori(8, BATCHES, 8) as n8:
                    for k in range(8):
                        body(n8 + k, k % 4, n8 + (k - k % 4), first=k == 0, last_here=k == 7)
                for n in range(BATCHES, END):
                    body(n, n % 4, n - n % 4, first=n == BATCHES)

            @block.scalar
            def _(act):
                def body(n, u, n4):
                    for name, bank, dst in (("x", x_bank, xT), ("ht", t_bank, hT)):
                        if not active(name, n):
                            SC.skip(act, name, n)
                            continue
                        act.wait_ge(PE.sem, PE.at(name, n))
                        act.activation(dst[:, :, :].rearrange("p j c -> p (j c)"), bank[:, :],
                                       ACT.Copy).then_inc(SC.sem, 1)
                over_time(nc.scalar, body)

            @block.vector
            def _(dve):
                def locate(tile):
                    shape = [P, TOP0, E0]
                    dve.wait_ge(L.sem, L.at("row", tile - 1))
                    dve.tensor_tensor(onehot[:, :, :], g["expert_id"][:, :].unsqueeze(1).broadcast_to(shape),
                                      g["chosen"][:, tile, :].unsqueeze(2).broadcast_to(shape),
                                      ALU.is_equal).then_inc(L.sem, 1)
                    dve.wait_ge(L.sem, L.at("onehot", tile))
                    dve.tensor_tensor(onehot[:, :, :], onehot[:, :, :],
                                      g["first_row"][:, :].unsqueeze(1).broadcast_to(shape),
                                      ALU.mult).then_inc(L.sem, 1)
                    dve.wait_ge(L.sem, L.at("times", tile))
                    dve.tensor_reduce(first[:, :], onehot[:, :, :], AX_X, ALU.add).then_inc(L.sem, 1)
                    dve.wait_ge(L.sem, L.at("first", tile))
                    dve.tensor_tensor(g["out_rows"][:, tile, :], first[:, :], g["position"][:, tile, :],
                                      ALU.add).then_inc(L.sem, 1)

                def body(n, u, n4):
                    if active("h", n):
                        dve.wait_ge(PE.sem, PE.at("h", n))
                        dve.tensor_scalar(h[:, :, :].rearrange("p j c -> p (j c)"), h_bank[:, :], 0.0, None,
                                          ALU.max).then_inc(VE.sem, 1)
                    else:
                        VE.skip(dve, "h", n)
                    if active("y", n):
                        dve.wait_ge(PE.sem, PE.at("y", n))
                        if not isinstance(n, int) or n >= 6:
                            dve.wait_ge(stored[(u + 2) % 4], n4 * 4 if u >= 2 else (n4 - 4) * 4)
                        dve.tensor_copy(y[:, (u + 2) % 4, :, :].rearrange("p j c -> p (j c)"),
                                        y_bank[:, :]).then_inc(VE.sem, 1)
                    else:
                        VE.skip(dve, "y", n)

                for n in range(8):
                    body(n, n % 4, n - n % 4)
                    locate(n)
                with nc.vector.Fori(2, TILES // 4) as k:
                    for u in range(4):
                        body(k * 4 + u, u, k * 4)
                        locate(k * 4 + u)
                with nc.vector.Fori(TILES, BATCHES, 4) as n4:
                    for u in range(4):
                        body(n4 + u, u, n4)
                for n in range(BATCHES, END):
                    body(n, n % 4, n - n % 4)


def attention1(nc, m0, g):
    with ExitStack() as ctx:
        m = Mem(nc, ctx)
        inT = m.sb("c_inT", [P, 2, P])
        kT = m.sb("c_kT", [P, CH, P])
        qT = m.sb("c_qT", [P, CH, P, 2])
        v = m.sb("c_v", [P, INNER])
        probs = m.sb("c_probs", [P, CH, 2, S])
        probsT = m.sb("c_probsT", [P, CH, S, 2])
        oT = m.sb("c_oT", [P, CH, P])
        rows = m.sb("c_rows", [P, 2, D])
        y_raw = m.sb("c_y_raw", [P, D])
        stats = m.sb("c_stats", [P, 6])
        mv = m.sb("c_mv", [P, 2])
        tmp = m.sb("c_tmp", [P, 1])
        rstd = m.sb("c_rstd", [P, 1])
        mx = m.sb("c_mx", [P, H])
        sums = m.sb("c_sums", [P, H])
        rsum = m.sb("c_rsum", [P, H])
        fetched = m.sb("c_fetched", [P, TOP0, D])
        weighed = m.sb("c_weighed", [P, TOP0, D])
        RSLOTS = 6
        scores = m.psum("c_scores", [P, 2, BANK])
        ring = m.psum("c_ring", [P, RSLOTS, BANK])
        cleared = m.sem("c_qT_cleared")

        PE = Steps(m.sem("c_pe"), ["s0", "s1", "pv0", "pv1", "v0", "v1", "x", "y", "q0", "k0", "q1", "k1",
                                   "pt0", "pt1"], -2)
        SC = Steps(m.sem("c_act"), ["copy", "pv0", "pv1", "v0", "exp0", "exp1", "v1", "x", "y", "k0", "k1",
                                    "pt0", "pt1"], -2)
        VE = Steps(m.sem("c_dve"), ["add0", "add1", "norm", "max0", "max1", "sub0", "sub1", "mixed", "stats", "sum0",
                                    "go", "aggr", "sum1", "recip", "scale0", "scale1", "q0", "q1", "y1"], -2)
        PO = Steps(m.sem("c_pool"), ["weigh", "mix0", "mix1", "mix2", "mix3", "r1", "r2", "y2"], -2)
        gathered = m.sem("c_gathered")
        rows_u = m.sb("c_out_rows", [P, TOP0], mybir.dt.uint32)
        rows_copied, rows_seen = m.sem("c_rows_copied"), m.sem("c_rows_seen")
        pe_free, pool_free = m.sem("c_pe_free"), m.sem("c_pool_free")
        RING = PE.names[2:]
        assert len(RING) % RSLOTS == 0

        def slot(n):
            return ring[:, RING.index(n) % RSLOTS, :]

        def runs(n, it):
            if not isinstance(it, int):
                return True
            if n[:3] == "mix" or n in ("weigh", "stats", "go", "aggr", "r1", "r2"):
                tile = it + 2
            elif n[0] in "xkq" or n in ("norm", "copy"):
                tile = it + 1
            else:
                tile = it - 1 if n[0] == "y" or n[:2] == "pv" else it
            return 0 <= tile < TILES

        def fetches(tile):
            return not isinstance(tile, int) or 0 <= tile < TILES

        def over_tiles(eng, body):
            for it in range(-2, 1):
                body(it)
            with eng.Fori(1, TILES - 3) as it:
                body(it)
            for it in range(TILES - 3, TILES + 1):
                body(it)

        with nc.Block() as block:
            @block.tensor
            def _(pe):
                def body(it):
                    def score(n):
                        h2 = int(n[1])
                        pe.wait_ge(SC.sem, SC.at(f"k{h2}", it - 1))
                        pe.wait_ge(VE.sem, VE.at(f"q{h2}", it - 1))
                        pe.sem_inc(pe_free, 1)
                        for k in range(4):
                            for b in range(2):
                                c = 4 * h2 + k
                                last = pe.matmul(scores[:, h2, k * P + S * b:k * P + S * b + S],
                                                 qT[:, c, S * b:S * b + S, :].rearrange("p s h -> p (s h)"),
                                                 kT[:, c, S * b:S * b + S], start=True, stop=True)
                        return last

                    def pv(n):
                        b = int(n[2])
                        if b == 0:
                            pe.wait_ge(SC.sem, SC.at("pt1", it - 1))
                        pe.sem_inc(pe_free, 1)
                        r = slice(S * b, S * b + S)
                        for c in range(CH):
                            for h2 in range(2):
                                last = pe.matmul(slot(n)[S * h2:S * h2 + S, c * S:c * S + S],
                                                 v[r, c * P + S * h2:c * P + S * h2 + S],
                                                 probsT[r, c, :, h2], start=True, stop=True)
                        return last

                    def proj_v(n):
                        at = BANK * int(n[1])
                        return pe.matmul(slot(n), inT[:, 1, :],
                                         g["wv1"][:, :, :].rearrange("p h e -> p (h e)")[:, at:at + BANK],
                                         start=True, stop=True)

                    def out(n):
                        pe.wait_ge(SC.sem, SC.at("pv1", it))
                        for k in range(CH):
                            last = pe.matmul(slot(n)[:, 0:D], oT[:, k, :], g["wo1"][:, k, :],
                                             start=(k == 0), stop=(k == CH - 1))
                        return last

                    def t_in(n):
                        pe.wait_ge(VE.sem, VE.at("norm", it))
                        pe.wait_ge(SC.sem, SC.at("copy", it))
                        for j in range(2):
                            last = pe.transpose(slot(n)[:, j * P:j * P + P], rows[:, j, :], g["ident"][:, :])
                        return last

                    def proj(n):
                        if n == "q0":
                            pe.wait_ge(SC.sem, SC.at("x", it))
                        wt, src = (g["wk1"], 1) if n[0] == "k" else (g["wq1"], 0)
                        for j in range(4):
                            c = 4 * int(n[1]) + j
                            last = pe.matmul(slot(n)[:, j * P:j * P + P],
                                             wt[:, 2 * c:2 * c + 2, :].rearrange("p h e -> p (h e)"),
                                             inT[:, src, :], start=True, stop=True)
                        return last

                    def t_probs(n):
                        h2 = int(n[2])
                        pe.wait_ge(VE.sem, VE.at(f"scale{h2}", it))
                        for j in range(4):
                            last = pe.transpose(slot(n)[:, j * P:j * P + P],
                                                probs[:, 4 * h2 + j, :, :].rearrange("p b j -> p (b j)"),
                                                g["ident"][:, :])
                        return last

                    emit = {"s": score, "v": proj_v, "y": out, "x": t_in, "k": proj, "q": proj}
                    for n in PE.names:
                        if n in RING:
                            i = RING.index(n) - RSLOTS
                            src = VE if RING[i][0] == "q" else SC
                            pe.wait_ge(src.sem, src.at(RING[i], it if i >= 0 else it - 1))
                        if not runs(n, it):
                            PE.skip(pe, n, it)
                            continue
                        step = {"pv": pv, "pt": t_probs}[n[:2]] if n[0] == "p" else emit[n[0]]
                        step(n).then_inc(PE.sem, 1)

                pe.wait_ge(cleared, 1)
                over_tiles(nc.tensor, body)

            @block.scalar
            def _(act):
                def body(it):
                    for n in SC.names:
                        if not runs(n, it):
                            SC.skip(act, n, it)
                            continue
                        if n[:3] == "exp":
                            h2 = int(n[3])
                            act.wait_ge(VE.sem, VE.at(f"sub{h2}", it))
                            p = probs[:, 4 * h2:4 * h2 + 4, :, :].rearrange("p c b j -> p (c b j)")
                            act.activation(p, p, ACT.Exp).then_inc(SC.sem, 1)
                            continue
                        if n == "copy":
                            act.wait_ge(PE.sem, PE.at("x", it - 1))
                            act.activation(rows[:, 1, :], g["ctx"][:, it + 1, :], ACT.Copy).then_inc(SC.sem, 1)
                            continue
                        act.wait_ge(PE.sem, PE.at(n, it))
                        if n == "x":
                            ins = act.activation(inT[:, :, :].rearrange("p a b -> p (a b)"), slot(n)[:, 0:2 * P],
                                                 ACT.Copy)
                        elif n == "y":
                            act.wait_ge(VE.sem, VE.at("y1", it - 1))
                            ins = act.activation(y_raw[:, :], slot(n)[:, 0:D], ACT.Copy)
                        elif n[0] == "v":
                            at = BANK * int(n[1])
                            ins = act.activation(v[:, at:at + BANK], slot(n), ACT.Copy)
                        elif n[0] == "k":
                            for j in range(4):
                                c = 4 * int(n[1]) + j
                                ins = act.activation(kT[:, c, :], slot(n)[:, j * P:j * P + P], ACT.Identity,
                                                     bias=g["wT"][:, BK, c:c + 1])
                        elif n[:2] == "pv":
                            b = int(n[2])
                            ins = act.activation(oT[:, :, S * b:S * b + S],
                                                 slot(n).rearrange("p (c s) -> p c s", c=CH), ACT.Copy)
                        else:
                            c = 4 * int(n[2])
                            ins = act.activation(probsT[:, c:c + 4, :, :].rearrange("p c s h -> p (c s h)"), slot(n),
                                                 ACT.Copy)
                        ins.then_inc(SC.sem, 1)

                over_tiles(nc.scalar, body)

            @block.vector
            def _(dve):
                def body(it):
                    per = [P, 8, S]
                    for n in VE.names:
                        if not runs(n, it):
                            VE.skip(dve, n, it)
                        elif n == "mixed":
                            dve.wait_ge(VE.sem, VE.at("sub1", it))
                            dve.wait_ge(PO.sem, PO.at("mix3", it))
                            dve.sem_inc(VE.sem, 1)
                        elif n == "stats":
                            dve.bn_stats(stats[:, :], g["x"][:, it + 2, :]).then_inc(VE.sem, 1)
                        elif n == "go":
                            dve.wait_ge(VE.sem, VE.at("sum0", it))
                            dve.wait_ge(PO.sem, PO.at("r2", it - 1))
                            dve.sem_inc(VE.sem, 1)
                        elif n == "aggr":
                            dve.bn_aggr(mv[:, :], stats[:, :]).then_inc(VE.sem, 1)
                        elif n == "norm":
                            dve.wait_ge(PO.sem, PO.at("r2", it - 1))
                            dve.wait_ge(PE.sem, PE.at("x", it - 1))
                            dve.tensor_scalar(rows[:, 0, :], g["x"][:, it + 1, :], mv[:, 0:1], rstd[:, :],
                                              ALU.subtract, ALU.mult).then_inc(VE.sem, 1)
                        elif n == "recip":
                            dve.wait_ge(VE.sem, VE.at("sum1", it))
                            dve.reciprocal(rsum[:, :], sums[:, :]).then_inc(VE.sem, 1)
                        elif n[0] == "q":
                            c = 4 * int(n[1])
                            dve.wait_ge(PE.sem, PE.at(n, it))
                            for h2 in range(2):
                                r = slice(S * h2, S * h2 + S)
                                ins = dve.scalar_tensor_tensor(
                                    qT[r, c:c + 4, :, h2], slot(n)[r, :].rearrange("p (c s) -> p c s", c=4), DH ** -0.5,
                                    g["wT"][r, BQ, c:c + 4].unsqueeze(2).broadcast_to([S, 4, P]),
                                    ALU.mult, ALU.add)
                            ins.then_inc(VE.sem, 1)
                        elif n == "y1":
                            dve.wait_ge(SC.sem, SC.at("y", it))
                            xt = g["x"][:, it - 1, :]
                            dve.scalar_tensor_tensor(xt, y_raw[:, :], g["tanh_g"][:, 1:2], xt, ALU.mult,
                                                     ALU.add).then_inc(VE.sem, 1)
                        else:
                            h2 = int(n[-1])
                            p8 = probs[:, 4 * h2:4 * h2 + 4, :, :].rearrange("p c b j -> p (c b) j")
                            m8 = slice(8 * h2, 8 * h2 + 8)
                            if n[:3] == "add":
                                dve.wait_ge(PE.sem, PE.at(f"s{h2}", it))
                                dve.wait_ge(PE.sem, PE.at(f"pt{h2}", it - 1))
                                dve.tensor_tensor(p8, scores[:, h2, :].rearrange("p (c j) -> p c j", j=S),
                                                  g["mask1"][:, :].unsqueeze(1).broadcast_to(per),
                                                  ALU.add).then_inc(VE.sem, 1)
                            elif n[:3] == "max":
                                dve.wait_ge(VE.sem, VE.at(f"add{h2}", it))
                                dve.tensor_reduce(mx[:, m8], p8, AX_X, ALU.max).then_inc(VE.sem, 1)
                            elif n[:3] == "sub":
                                dve.wait_ge(VE.sem, VE.at(f"max{h2}", it))
                                dve.tensor_tensor(p8, p8, mx[:, m8].unsqueeze(2).broadcast_to(per),
                                                  ALU.subtract).then_inc(VE.sem, 1)
                            elif n[:3] == "sum":
                                dve.wait_ge(SC.sem, SC.at(f"exp{h2}", it))
                                dve.tensor_reduce(sums[:, m8], p8, AX_X, ALU.add).then_inc(VE.sem, 1)
                            else:
                                dve.wait_ge(VE.sem, VE.at("recip", it))
                                dve.tensor_tensor(p8, p8, rsum[:, m8].unsqueeze(2).broadcast_to(per),
                                                  ALU.mult).then_inc(VE.sem, 1)

                dve.memset(qT[:, :, :, :], 0.0).then_inc(cleared, 1)
                over_tiles(nc.vector, body)

            @block.gpsimd
            def _(pool):
                def gather(it):
                    if not (isinstance(it, int) and it < -2):
                        pool.wait_ge(PO.sem, PO.at("weigh", it))
                    pool.tensor_copy(rows_u[:, :], g["out_rows"][:, it + 3, :]).then_inc(rows_copied, 1)
                    pool.wait_ge(rows_copied, it + 4)
                    pool.sem_inc(rows_seen, 1)
                    for j in range(TOP0):
                        pool.indirect_dma_start(fetched[:, j, :], None, g["ys"],
                                                bass.IndirectOffsetOnAxis(rows_u[:, j:j + 1], 0),
                                                bounds_check=SLOTS0 * P - 1).then_inc(gathered, 16)

                def body(it):
                    for n in PO.names:
                        if n == "r1" and fetches(it + 3):
                            gather(it)
                        if not runs(n, it):
                            PO.skip(pool, n, it)
                            continue
                        if n == "weigh":
                            if not (isinstance(it, int) and it <= -2):
                                pool.wait_ge(PO.sem, PO.at("mix3", it - 1))
                            pool.wait_ge(gathered, (it + 3) * 16 * TOP0)
                            pool.sem_inc(pool_free, 1)
                            ins = pool.tensor_tensor(
                                weighed[:, :, :], fetched[:, :, :],
                                g["gates"][:, it + 2, :].unsqueeze(2).broadcast_to([P, TOP0, D]), ALU.mult)
                        elif n[:3] == "mix":
                            xt = g["x"][:, it + 2, :]
                            pool.wait_ge(PO.sem, PO.at(PO.names[PO.names.index(n) - 1], it))
                            pool.sem_inc(pool_free, 1)
                            ins = pool.tensor_tensor(xt, xt, weighed[:, int(n[3]), :], ALU.add)
                        elif n == "y2":
                            xt = g["x"][:, it - 1, :]
                            pool.wait_ge(VE.sem, VE.at("y1", it))
                            pool.sem_inc(pool_free, 1)
                            ins = pool.tensor_tensor(xt, xt, g["out_bias1"][:, :], ALU.add)
                        elif n == "r1":
                            pool.wait_ge(VE.sem, VE.at("aggr", it))
                            ins = pool.tensor_tensor(tmp[:, :], mv[:, 1:2], g["eps"][:, 0:1], ALU.add)
                        else:
                            pool.wait_ge(PO.sem, PO.at("r1", it))
                            ins = pool.tensor_tensor(rstd[:, :], tmp[:, :], g["neg_half"][:, 0:1], ALU.pow)
                        ins.then_inc(PO.sem, 1)

                gather(-3)
                over_tiles(nc.gpsimd, body)


def experts1(nc, m0, g, out):
    with ExitStack() as ctx:
        m = Mem(nc, ctx)
        xfT = m.sb("d_xfT", [P, P])
        xfT_next = m.sb("d_xfT_next", [P, P])
        xf = m.sb("d_xf", [P, D])
        stats = m.sb("d_stats", [P, 6])
        mv = m.sb("d_mv", [P, 2])
        tmp = m.sb("d_tmp", [P, 1])
        rstd = m.sb("d_rstd", [P, 1])
        th_l = m.sb("d_th_l", [P, E1])
        sc = m.sb("d_scores", [P, E1])
        choice = m.sb("d_choice", [P, E1])
        top = m.sb("d_top", [P, GROUPS1, 8])
        gs = m.sb("d_group_scores", [P, GROUPS1])
        gt = m.sb("d_gt", [P, GROUPS1, GROUPS1])
        eq = m.sb("d_eq", [P, GROUPS1, GROUPS1])
        rank = m.sb("d_rank", [P, GROUPS1])
        gm = m.sb("d_group_mask", [P, GROUPS1])
        masked = m.sb("d_masked", [P, E1])
        top8 = m.sb("d_top8", [P, 8])
        left = m.sb("d_left", [P, E1])
        picked = m.sb("d_picked", [P, E1])
        wsum = m.sb("d_wsum", [P, 4])
        wts = m.sb("d_wts", [P, E1])
        th = m.sb("d_th", [P, 2, BANK])
        a = m.sb("d_a", [P, 2, BANK])
        h = m.sb("d_h", [P, 2, BANK])
        hT = m.sb("d_hT", [P, 2, BANK])
        g_bank = m.psum("d_g_bank", [P, 2, BANK])
        u_bank = m.psum("d_u_bank", [P, 2, BANK])
        t_bank = m.psum("d_t_bank", [P, 2, BANK])
        in_bank = m.psum("d_in_bank", [P, BANK])
        y_bank = m.psum("d_y_bank", [P, BANK])
        stored = m.sem("stored")

        NQ = 5
        WIDTH = [BANK] * 4 + [P]
        PE = Steps(m.sem("d_pe"), ["gu0", "t3", "y2", "gu1", "t4", "y3", "y4", "gu2", "t0", "x", "gu3", "logits",
                                   "t1", "gu4", "y0", "t2", "y1"])
        SC = Steps(m.sem("d_act"), ["th0", "t3", "th1", "t4", "th2", "t0", "x", "th3", "logits", "t1", "th4", "xcopy",
                                    "t2"])
        ROUTE = ["sc", "choice", "go_top", "top", "gs", "gt", "eq", "eqtri", "beat", "rank", "gm", "masked"]
        ROUTE_END = ["go_top8", "top8", "go_left", "left", "picked", "w", "wsum", "wsum_eps", "wrec", "wts"]
        VE = Steps(m.sem("d_dve"), ["a0", "go_top8", "top8", "b0", "go_left", "left", "stats", "picked", "go", "w",
                                    "aggr", "wsum", "wsum_eps", "wrec", "wts", "a1", "b1", "norm", "y", "a2", "b2",
                                    "a3", "sc", "b3", "a4", "b4", "choice"] + ROUTE[2:])
        PO = Steps(m.sem("d_pool"), ["r1", "r2", "c0", "c1", "c2", "c3"])
        LATE = ("t3", "y2", "t4", "y3", "y4", "y")
        EARLY = ["x", "logits", "xcopy", "stats", "go", "aggr", "norm", "r1", "r2"] + ROUTE

        def runs(n, it):
            if not isinstance(it, int):
                return True
            return 0 <= it + (1 if n in EARLY else -1 if n in LATE else 0) < TILES

        def over_tiles(eng, body):
            body(-1)
            body(0)
            with eng.Fori(1, TILES - 1) as it:
                body(it)
            body(TILES - 1)
            body(TILES)

        with nc.Block() as block:
            @block.tensor
            def _(pe):
                def body(it):
                    def gate_up(q):
                        if q == 0:
                            pe.wait_ge(SC.sem, SC.at("xcopy", it - 1))
                        pe.wait_ge(VE.sem, VE.at(f"b{q - 2}", it) if q >= 2 else VE.at(f"b{4 - q}", it - 1))
                        if q < 4:
                            pe.matmul(g_bank[:, q % 2, :], xfT[:, :],
                                      g["wT"][:, GATE + 4 * q:GATE + 4 * q + 4, :].rearrange("p k c -> p (k c)"),
                                      start=True, stop=True)
                            return pe.matmul(u_bank[:, q % 2, :], xfT[:, :],
                                             g["wT"][:, UP + 4 * q:UP + 4 * q + 4, :].rearrange("p k c -> p (k c)"),
                                             start=True, stop=True)
                        pe.matmul(g_bank[:, 0, 0:P], xfT[:, :], g["wT"][:, SHARED, :], start=True, stop=True)
                        return pe.matmul(u_bank[:, 0, 0:P], xfT[:, :], g["wT"][:, SHARED + 1, :],
                                         start=True, stop=True)

                    def turn(q):
                        if q == 4:
                            pe.wait_ge(VE.sem, VE.at("b4", it - 1))
                        elif q == 3:
                            pe.wait_ge(PO.sem, PO.at("c3", it - 1))
                        else:
                            pe.wait_ge(PO.sem, PO.at(f"c{q}", it))
                        last_in_bank, when = (("t4", it), ("t3", it), ("t0", it), ("t1", it - 1), ("t2", it - 1))[q]
                        pe.wait_ge(SC.sem, SC.at(last_in_bank, when))
                        for j in range(WIDTH[q] // P):
                            last = pe.transpose(t_bank[:, q % 2, j * P:j * P + P], h[:, q % 2, j * P:j * P + P],
                                                g["ident"][:, :])
                        return last

                    def down(q):
                        pe.wait_ge(SC.sem, SC.at(f"t{q}", it - 1 if q == 2 else it))
                        if q == 0:
                            pe.wait_ge(VE.sem, VE.at("y", it))
                        for j in range(WIDTH[q] // P):
                            k = DOWN + 4 * q + j if q < 4 else SHARED_DOWN
                            last = pe.matmul(y_bank[:, 0:D], hT[:, q % 2, j * P:j * P + P], g["wT"][:, k, :],
                                             start=(q == 0 and j == 0), stop=(q == 4))
                        return last

                    for n in PE.names:
                        if not runs(n, it):
                            PE.skip(pe, n, it)
                            continue
                        if n == "x":
                            pe.wait_ge(VE.sem, VE.at("norm", it))
                            last = pe.transpose(in_bank[:, 0:P], xf[:, :], g["ident"][:, :])
                        elif n == "logits":
                            pe.wait_ge(SC.sem, SC.at("x", it))
                            last = pe.matmul(in_bank[:, P:P + E1], xfT_next[:, :], g["wT"][:, ROUTER1, 0:E1],
                                             start=True, stop=True)
                        else:
                            last = {"g": gate_up, "t": turn, "y": down}[n[0]](int(n[-1]))
                        last.then_inc(PE.sem, 1)

                over_tiles(nc.tensor, body)

            @block.scalar
            def _(act):
                def body(it):
                    for n in SC.names:
                        if not runs(n, it):
                            SC.skip(act, n, it)
                            continue
                        q = int(n[-1]) if n[-1].isdigit() else 0
                        if n[:2] == "th":
                            act.wait_ge(PE.sem, PE.at(f"gu{q}", it))
                            act.wait_ge(VE.sem, VE.at(f"a{q - 2}", it) if q >= 2 else VE.at(f"a{4 - q}", it - 1))
                            ins = act.activation(th[:, q % 2, 0:WIDTH[q]], g_bank[:, q % 2, 0:WIDTH[q]], ACT.Tanh,
                                                 scale=0.5)
                        elif n == "x":
                            act.wait_ge(PE.sem, PE.at("x", it))
                            ins = act.activation(xfT_next[:, :], in_bank[:, 0:P], ACT.Copy)
                        elif n == "xcopy":
                            act.wait_ge(SC.sem, SC.at("x", it))
                            act.wait_ge(PE.sem, PE.at("gu4", it))
                            ins = act.activation(xfT[:, :], xfT_next[:, :], ACT.Copy)
                        elif n == "logits":
                            act.wait_ge(PE.sem, PE.at("logits", it))
                            act.wait_ge(VE.sem, VE.at("sc", it - 1))
                            ins = act.activation(th_l[:, :], in_bank[:, P:P + E1], ACT.Tanh, scale=0.5)
                        else:
                            act.wait_ge(PE.sem, PE.at(n, it))
                            ins = act.activation(hT[:, q % 2, 0:WIDTH[q]], t_bank[:, q % 2, 0:WIDTH[q]], ACT.Copy)
                        ins.then_inc(SC.sem, 1)

                over_tiles(nc.scalar, body)

            @block.vector
            def _(dve):
                def body(it):
                    def gate(q):
                        wd = WIDTH[q]
                        dve.wait_ge(SC.sem, SC.at(f"th{q}", it))
                        if q < 2:
                            dve.wait_ge(PO.sem, PO.at(f"c{q + 2}", it - 1))
                        else:
                            dve.wait_ge(PO.sem, PO.at(f"c{q - 2}", it))
                        return dve.scalar_tensor_tensor(a[:, q % 2, 0:wd], th[:, q % 2, 0:wd], 1.0,
                                                        g_bank[:, q % 2, 0:wd], ALU.add, ALU.mult)

                    def times_up(q):
                        wd = WIDTH[q]
                        dve.wait_ge(VE.sem, VE.at(f"a{q}", it))
                        if q == 4:
                            dve.wait_ge(PE.sem, PE.at("t2", it))
                        dst = a if q < 4 else h
                        return dve.scalar_tensor_tensor(dst[:, q % 2, 0:wd], a[:, q % 2, 0:wd], 0.5,
                                                        u_bank[:, q % 2, 0:wd], ALU.mult, ALU.mult)

                    def step(n):
                        if n[0] == "a" and n[1].isdigit():
                            return gate(int(n[1]))
                        if n[0] == "b" and n[1].isdigit():
                            return times_up(int(n[1]))
                        if n == "stats":
                            return dve.bn_stats(stats[:, :], g["x"][:, it + 1, :])
                        if n == "go":
                            dve.wait_ge(VE.sem, VE.at("picked", it))
                            dve.wait_ge(PO.sem, PO.at("r2", it - 1))
                            return dve.sem_inc(VE.sem, 1)
                        if n == "aggr":
                            return dve.bn_aggr(mv[:, :], stats[:, :])
                        if n == "norm":
                            dve.wait_ge(PO.sem, PO.at("r2", it))
                            dve.wait_ge(PE.sem, PE.at("x", it - 1))
                            return dve.tensor_scalar(xf[:, :], g["x"][:, it + 1, :], mv[:, 0:1], rstd[:, :],
                                                     ALU.subtract, ALU.mult)
                        if n == "y":
                            dve.wait_ge(PE.sem, PE.at("y4", it))
                            xt = g["x"][:, it - 1, :]
                            return dve.scalar_tensor_tensor(xt, y_bank[:, 0:D], g["tanh_g"][:, 3:4], xt, ALU.mult,
                                                            ALU.add)
                        if n == "sc":
                            dve.wait_ge(SC.sem, SC.at("logits", it))
                            return dve.tensor_scalar(sc[:, :], th_l[:, :], 0.5, 0.5, ALU.mult, ALU.add)
                        order = ROUTE + ROUTE_END
                        before = VE.names[VE.names.index(n) - 1] if n[:2] == "go" else order[order.index(n) - 1]
                        if before[:2] != "go":
                            dve.wait_ge(VE.sem, VE.at(before, it))
                        if n[:2] == "go":
                            return dve.sem_inc(VE.sem, 1)
                        if n == "choice":
                            return dve.tensor_tensor(choice[:, :], sc[:, :], g["gate_bias"][:, :], ALU.add)
                        if n == "top":
                            for k in range(GROUPS1):
                                last = dve.max(top[:, k, :], choice[:, k * GSIZE1:k * GSIZE1 + GSIZE1])
                            return last
                        if n == "gs":
                            return dve.tensor_tensor(gs[:, :], top[:, :, 0], top[:, :, 1], ALU.add)
                        mine = gs[:, :].unsqueeze(2).broadcast_to([P, GROUPS1, GROUPS1])
                        other = gs[:, :].unsqueeze(1).broadcast_to([P, GROUPS1, GROUPS1])
                        if n == "gt":
                            return dve.tensor_tensor(gt[:, :, :], other, mine, ALU.is_gt)
                        if n == "eq":
                            return dve.tensor_tensor(eq[:, :, :], other, mine, ALU.is_equal)
                        if n == "eqtri":
                            return dve.tensor_tensor(eq[:, :, :], eq[:, :, :], g["tri"][:, :, :], ALU.mult)
                        if n == "beat":
                            return dve.tensor_tensor(gt[:, :, :], gt[:, :, :], eq[:, :, :], ALU.add)
                        if n == "rank":
                            return dve.tensor_reduce(rank[:, :], gt[:, :, :], AX_X, ALU.add)
                        if n == "gm":
                            return dve.tensor_scalar(gm[:, :], rank[:, :], 1.5, None, ALU.is_lt)
                        if n == "masked":
                            return dve.tensor_tensor(
                                masked[:, :].rearrange("p (g e) -> p g e", g=GROUPS1),
                                choice[:, :].rearrange("p (g e) -> p g e", g=GROUPS1),
                                gm[:, :].unsqueeze(2).broadcast_to([P, GROUPS1, GSIZE1]), ALU.mult)
                        if n == "top8":
                            return dve.max(top8[:, :], masked[:, :])
                        if n == "left":
                            return dve.match_replace(left[:, :], top8[:, :], masked[:, :], MASKED)
                        if n == "picked":
                            return dve.tensor_tensor(picked[:, :], masked[:, :], left[:, :], ALU.not_equal)
                        if n == "w":
                            return dve.tensor_tensor(picked[:, :], sc[:, :], picked[:, :], ALU.mult)
                        if n == "wsum":
                            return dve.tensor_reduce(wsum[:, 0:1], picked[:, :], AX_X, ALU.add)
                        if n == "wsum_eps":
                            return dve.tensor_scalar(wsum[:, 1:2], wsum[:, 0:1], 1e-20, None, ALU.add)
                        if n == "wrec":
                            return dve.reciprocal(wsum[:, 2:3], wsum[:, 1:2])
                        dve.wait_ge(PO.sem, PO.at("c3", it - 1))
                        return dve.tensor_scalar(wts[:, :], picked[:, :], wsum[:, 2:3], ROUTED_SCALING, ALU.mult,
                                                 ALU.mult)

                    for n in VE.names:
                        if not runs(n, it):
                            VE.skip(dve, n, it)
                        elif n[:2] == "go":
                            step(n)
                        else:
                            step(n).then_inc(VE.sem, 1)

                over_tiles(nc.vector, body)

            @block.gpsimd
            def _(pool):
                def body(it):
                    def weigh(q):
                        if not runs(f"c{q}", it):
                            PO.skip(pool, f"c{q}", it)
                            return
                        if q == 0:
                            pool.wait_ge(VE.sem, VE.at("wts", it))
                        pool.wait_ge(PE.sem, PE.at(("t4", "t3", "t0", "t1")[q], it))
                        if q > 0:
                            pool.wait_ge(VE.sem, VE.at(f"b{q}", it))
                        pool.tensor_tensor(h[:, q % 2, :].rearrange("p (e i) -> p e i", e=8),
                                           a[:, q % 2, :].rearrange("p (e i) -> p e i", e=8),
                                           wts[:, 8 * q:8 * q + 8].unsqueeze(2).broadcast_to([P, 8, I1]),
                                           ALU.mult).then_inc(PO.sem, 1)
                    if runs("r1", it):
                        pool.wait_ge(VE.sem, VE.at("aggr", it))
                        pool.tensor_tensor(tmp[:, :], mv[:, 1:2], g["eps"][:, 0:1], ALU.add).then_inc(PO.sem, 1)
                        pool.wait_ge(PO.sem, PO.at("r1", it))
                        pool.tensor_tensor(rstd[:, :], tmp[:, :], g["neg_half"][:, 0:1], ALU.pow).then_inc(PO.sem, 1)
                    else:
                        PO.skip(pool, "r1", it)
                        PO.skip(pool, "r2", it)
                    for q in range(4):
                        weigh(q)

                over_tiles(nc.gpsimd, body)

            @block.sync
            def _(sp):
                out_v = out.rearrange("(t b) s d -> t (b s) d", b=2)
                with nc.sync.Fori(0, TILES) as it:
                    sp.wait_ge(VE.sem, VE.at("y", it + 1))
                    sp.dma_start(out_v[it], g["x"][:, it, :]).then_inc(stored, 16)
                sp.wait_ge(stored, 16 * TILES)


STAGES = 15


def flamingo(nc, w, out):
    with ExitStack() as ctx:
        m = Mem(nc, ctx)
        g = lasting(nc, m)
        with ExitStack() as ctx0:
            g["keys"] = Mem(nc, ctx0).sb("b_keys", [P, E0, P])
            with ExitStack() as ctx_a:
                setup(nc, Mem(nc, ctx_a), g, w)
                attention0(nc, m, g, w)
            if STAGES & 14:
                experts0(nc, m, g, w)
        if STAGES & 4:
            attention1(nc, m, g)
        if STAGES & 8:
            experts1(nc, m, g, out)
        else:
            write_out(nc, m, g, out)


def write_out(nc, m, g, out):
    stored = m.sem("stored")
    with nc.Block() as block:
        @block.sync
        def _(sp):
            sp.dma_start(out.rearrange("(t b) s d -> (b s) t d", b=2), g["x"][:, :, :]).then_inc(stored, 16)
            sp.wait_ge(stored, 16)


_OUTS = [((B, S, D), 'float32')]


def kernel(**inputs):
    import numpy as _np
    import concourse.bacc as _bacc
    from concourse.bass_utils import run_bass_kernel_spmd as _run

    nc = _bacc.Bacc("TRN2", target_bir_lowering=False, num_devices=1)
    arrays, w = {}, {}
    for name, value in inputs.items():
        a = _np.ascontiguousarray(value)
        arrays[f"in_{name}_dram"] = a
        w[name] = nc.dram_tensor(f"in_{name}_dram", a.shape, mybir.dt.from_np(a.dtype), kind="ExternalInput").ap()
    shape, dtype = _OUTS[0]
    out = nc.dram_tensor("out_0_dram", shape, mybir.dt.from_np(_np.dtype(dtype)), kind="ExternalOutput").ap()
    flamingo(nc, w, out)
    r = _run(nc, [arrays], core_ids=[0])
    return r.results[0]["out_0_dram"]
```
